# Optimizing a Trainium2 kernel written in Bass

```python
import numpy as np
import jax
import jax.numpy as jnp

def _softmax(x, axis=-1):
    return jax.nn.softmax(x, axis=axis)

def _gelu(x):
    return jax.nn.gelu(x, approximate=True)

def _silu(x):
    return jax.nn.silu(x)

def _sigmoid(x):
    return jax.nn.sigmoid(x)

def _layernorm(x, axis=-1, eps=1e-05):
    m = jnp.mean(x, axis=axis, keepdims=True)
    v = jnp.var(x, axis=axis, keepdims=True)
    return (x - m) / jnp.sqrt(v + eps)

def _scatter_add(tgt, idx, src, axis=0):
    return tgt.at[idx].add(src)

def _segment_sum(src, seg, n):
    return jax.ops.segment_sum(src, seg, n)
kernel_name = 'mk_seq_preln_d1_jaxref_r8_90a8a0'

def setup_inputs(seed: int=0):
    np.random.seed(seed)
    _w = jnp.asarray

    def _L0_attn_setup():
        import jax, jax.numpy as jnp
        import numpy as np
        from jax import lax
        H, KVH, D, CHUNK = (32, 8, 128, 128)
        ROPE_THETA = 10000.0
        RMS_EPS = 1e-05

        def _rope_tables(L):
            inv_freq = 1.0 / ROPE_THETA ** (jnp.arange(0, D, 2, dtype=jnp.float32) / D)
            ang = jnp.arange(L, dtype=jnp.float32)[:, None] * inv_freq
            cos = jnp.concatenate([jnp.cos(ang), jnp.cos(ang)], axis=-1)[:, None, :]
            sin = jnp.concatenate([jnp.sin(ang), jnp.sin(ang)], axis=-1)[:, None, :]
            return (cos, sin)

        def _apply_rope(x, cos, sin):
            half = D // 2
            rot = jnp.concatenate([-x[..., half:], x[..., :half]], axis=-1)
            return x * cos + rot * sin
        key = jax.random.key(seed)
        ks = jax.random.split(key, 10)
        B, L, HID = (1, 512, 512)
        s = lambda fan: 1.0 / np.sqrt(fan)
        return {'hidden_states': jax.random.normal(ks[0], (B, L, HID), jnp.float32), 'Wq': jax.random.normal(ks[1], (H * D, HID), jnp.float32) * s(HID), 'Wk': jax.random.normal(ks[2], (KVH * D, HID), jnp.float32) * s(HID), 'Wv': jax.random.normal(ks[3], (KVH * D, HID), jnp.float32) * s(HID), 'Wo': jax.random.normal(ks[4], (HID, H * D), jnp.float32) * s(H * D), 'Wg': jax.random.normal(ks[5], (H * D, HID), jnp.float32) * (s(HID) * 2 ** (-2.5)), 'Win': jax.random.normal(ks[6], (H, HID), jnp.float32) * s(HID), 'dt_bias': jnp.zeros((H,), jnp.float32), 'A_log_bias': jnp.log(jax.random.uniform(ks[7], (H,), jnp.float32, 1.0, 16.0)), 'gnorm_w': jnp.ones((D,), jnp.float32)}
    _L0_attn_in = _L0_attn_setup()

    def _L0_ffn_setup():
        import jax, jax.numpy as jnp
        import numpy as np
        import math
        E, DK, R = (8, 32, 16)
        SCALING = 16.0 / 16.0
        key = jax.random.key(seed)
        ks = jax.random.split(key, 7)
        Bt, S, Din, Dout = (4, 256, 512, 512)
        x = jax.random.normal(ks[0], (Bt, S, Din), jnp.float32)
        W = jax.random.normal(ks[1], (Dout, Din), jnp.float32) * 0.02
        b = jnp.zeros((Dout,), jnp.float32)
        Wq = jax.random.normal(ks[2], (E * DK, Din), jnp.float32) * 0.02
        Wk = jax.random.normal(ks[3], (E * DK, Din), jnp.float32) * 0.02
        A = jax.random.normal(ks[4], (E, R, Din), jnp.float32) * 0.02
        Bm = jax.random.normal(ks[5], (E, Dout, R), jnp.float32) * 0.02
        return {'x': x, 'W': W, 'b': b, 'Wq': Wq, 'Wk': Wk, 'A': A, 'Bm': Bm}
    _L0_ffn_in = _L0_ffn_setup()
    _d = {'L0_attn_hidden_states': _L0_attn_in['hidden_states'], 'L0_attn_Wq': _L0_attn_in['Wq'], 'L0_attn_Wk': _L0_attn_in['Wk'], 'L0_attn_Wv': _L0_attn_in['Wv'], 'L0_attn_Wo': _L0_attn_in['Wo'], 'L0_attn_Wg': _L0_attn_in['Wg'], 'L0_attn_Win': _L0_attn_in['Win'], 'L0_attn_dt_bias': _L0_attn_in['dt_bias'], 'L0_attn_A_log_bias': _L0_attn_in['A_log_bias'], 'L0_attn_gnorm_w': _L0_attn_in['gnorm_w'], 'L0_ffn_W': _L0_ffn_in['W'], 'L0_ffn_b': _L0_ffn_in['b'], 'L0_ffn_Wq': _L0_ffn_in['Wq'], 'L0_ffn_Wk': _L0_ffn_in['Wk'], 'L0_ffn_A': _L0_ffn_in['A'], 'L0_ffn_Bm': _L0_ffn_in['Bm']}
    _x0 = _d['L0_attn_hidden_states']
    _d['L0_attn_hidden_states'] = jax.random.normal(jax.random.fold_in(jax.random.key(seed), 1), (4, 512, 512), dtype=_x0.dtype)
    del _x0
    return _d

def reference(L0_attn_hidden_states, L0_attn_Wq, L0_attn_Wk, L0_attn_Wv, L0_attn_Wo, L0_attn_Wg, L0_attn_Win, L0_attn_dt_bias, L0_attn_A_log_bias, L0_attn_gnorm_w, L0_ffn_W, L0_ffn_b, L0_ffn_Wq, L0_ffn_Wk, L0_ffn_A, L0_ffn_Bm):

    def _L0_attn_ref(hidden_states, Wq, Wk, Wv, Wo, Wg, Win, dt_bias, A_log_bias, gnorm_w):
        import jax, jax.numpy as jnp
        import numpy as np
        from jax import lax
        H, KVH, D, CHUNK = (32, 8, 128, 128)
        ROPE_THETA = 10000.0
        RMS_EPS = 1e-05

        def _rope_tables(L):
            inv_freq = 1.0 / ROPE_THETA ** (jnp.arange(0, D, 2, dtype=jnp.float32) / D)
            ang = jnp.arange(L, dtype=jnp.float32)[:, None] * inv_freq
            cos = jnp.concatenate([jnp.cos(ang), jnp.cos(ang)], axis=-1)[:, None, :]
            sin = jnp.concatenate([jnp.sin(ang), jnp.sin(ang)], axis=-1)[:, None, :]
            return (cos, sin)

        def _apply_rope(x, cos, sin):
            half = D // 2
            rot = jnp.concatenate([-x[..., half:], x[..., :half]], axis=-1)
            return x * cos + rot * sin
        B, L, HID = hidden_states.shape
        NC = L // CHUNK
        q = (hidden_states @ Wq.T).reshape(B, L, H, D)
        k = (hidden_states @ Wk.T).reshape(B, L, KVH, D)
        v = (hidden_states @ Wv.T).reshape(B, L, KVH, D)
        cos, sin = _rope_tables(L)
        q = _apply_rope(q, cos, sin)
        k = _apply_rope(k, cos, sin)
        k = jnp.repeat(k, H // KVH, axis=2)
        v = jnp.repeat(v, H // KVH, axis=2)
        dt = jax.nn.softplus(hidden_states @ Win.T + dt_bias)
        A = -jnp.exp(A_log_bias)
        g = dt * A

        def chunked(t):
            return t.transpose(0, 2, 1, 3).reshape(B, H, NC, CHUNK, D)
        qc, kc = (chunked(q), chunked(k))
        xc = chunked(v * dt[..., None])
        gc = g.transpose(0, 2, 1).reshape(B, H, NC, CHUNK)
        G = jnp.cumsum(gc, axis=-1)
        scores = jnp.einsum('bhnid,bhnjd->bhnij', qc, kc)
        idx = jnp.arange(CHUNK)
        causal = idx[:, None] >= idx[None, :]
        decay = jnp.where(causal, jnp.exp(G[..., :, None] - G[..., None, :]), 0.0)
        y_intra = jnp.einsum('bhnij,bhnjd->bhnid', scores * decay, xc)
        Glast = G[..., -1:]
        k_dec = kc * jnp.exp(Glast - G)[..., None]
        cstates = jnp.einsum('bhnjd,bhnje->bhnde', k_dec, xc)
        chunk_decay = jnp.exp(G[..., -1])

        def step(state, inp):
            dec, cs = inp
            return (state * dec + cs, state)
        init = jnp.zeros((B, H, D, D), hidden_states.dtype)
        _, prev = lax.scan(step, init, (chunk_decay.transpose(2, 0, 1)[..., None, None], cstates.transpose(2, 0, 1, 3, 4)))
        prev = prev.transpose(1, 2, 0, 3, 4)
        y_inter = jnp.einsum('bhnid,bhnde->bhnie', qc * jnp.exp(G)[..., None], prev)
        y = (y_intra + y_inter).reshape(B, H, L, D).transpose(0, 2, 1, 3)
        rms = jnp.sqrt(jnp.mean(jnp.square(y), axis=-1, keepdims=True) + RMS_EPS)
        y = y / rms * gnorm_w
        gate = (hidden_states @ Wg.T).reshape(B, L, H, D)
        y = y * (gate * jax.nn.sigmoid(gate))
        return y.reshape(B, L, H * D) @ Wo.T

    def _L0_ffn_ref(x, W, b, Wq, Wk, A, Bm):
        import jax, jax.numpy as jnp
        import numpy as np
        import math
        E, DK, R = (8, 32, 16)
        SCALING = 16.0 / 16.0
        Bt, S, Din = x.shape
        result = jnp.einsum('bsi,oi->bso', x, W) + b
        q = jnp.einsum('bsi,ni->bsn', x, Wq).reshape(Bt, S, E, DK)
        k = jnp.einsum('bsi,ni->bsn', x, Wk).reshape(Bt, S, E, DK)
        scores = jnp.einsum('bsed,bsed->bse', q, k) / math.sqrt(DK)
        w = jax.nn.softmax(scores, axis=-1)
        h = jnp.einsum('bsi,eri->bser', x, A)
        combined = jnp.einsum('bse,bser,eor->bso', w, h, Bm) * SCALING
        return result + combined
    x = L0_attn_hidden_states
    x = x + _L0_attn_ref(_layernorm(x, axis=-1), L0_attn_Wq, L0_attn_Wk, L0_attn_Wv, L0_attn_Wo, L0_attn_Wg, L0_attn_Win, L0_attn_dt_bias, L0_attn_A_log_bias, L0_attn_gnorm_w)
    x = x + _L0_ffn_ref(_layernorm(x, axis=-1), L0_ffn_W, L0_ffn_b, L0_ffn_Wq, L0_ffn_Wk, L0_ffn_A, L0_ffn_Bm)
    return x

_drawn_inputs = setup_inputs


def setup_inputs(seed=0):
    import zlib

    import numpy as np

    out = dict(_drawn_inputs(seed))
    spreads = {'L0_attn_dt_bias': (0.0, 0.8), 'L0_attn_gnorm_w': (1.0, 0.6), 'L0_ffn_b': (0.0, 0.1)}
    factors = {'L0_ffn_Wq': 8.0, 'L0_ffn_Wk': 8.0, 'L0_ffn_A': 4.894, 'L0_ffn_Bm': 4.896}
    for name, (base, spread) in spreads.items():
        noise = np.random.default_rng([zlib.crc32(name.encode()), seed]).standard_normal(out[name].shape)
        drawn = base * np.exp(spread * noise) if base else spread * noise
        out[name] = jnp.asarray(drawn.astype(out[name].dtype))
    for name, factor in factors.items():
        out[name] = (out[name] * factor).astype(out[name].dtype)
    return out
```

```python
from contextlib import ExitStack

import numpy as np

import concourse.bass as bass
from concourse import mybir

ALU = mybir.AluOpType
ACT = mybir.ActivationFunctionType
AX = mybir.AxisListType
F32 = mybir.dt.float32
F32R = mybir.dt.float32r

P = 128
B, L, HID = 4, 512, 512
H, KVH, D = 32, 8, 128
C = 128
HG = H // KVH
NC = L // C
KT = HID // P
NT = B * NC
GW = HG * D
EPS = 1e-5
E, DK, R = 8, 32, 16
UNITS = 10
FIRST_UNITS = 6
ROPED = 1 + HG
TAB = 4
T_DT, T_NEGG, T_EXPG, T_W = range(TAB)


def wait_ge(engine, sem, count):
    if not isinstance(count, int) or count > 0:
        engine.wait_ge(sem, count)


def norm_stage(nc, io, keep):
    xh, xl, tab, ident, g_dram = (keep[k] for k in ("xh", "xl", "tab", "ident", "g_dram"))
    with ExitStack() as ctx:
        def sb(name, shape, dt=F32):
            return ctx.enter_context(nc.sbuf_tensor(name, shape, dt))

        def pb(name, shape):
            return ctx.enter_context(nc.psum_tensor(name, shape, F32))

        def sem(name):
            return ctx.enter_context(nc.semaphore(name))

        xin = sb("n_xin", [P, NT, HID])
        stats = sb("n_stats", [P, NT, 6])
        mv = sb("n_mv", [P, NT, 2])
        var = sb("n_var", [P, NT])
        rstd = sb("n_rstd", [P, NT])
        mhalf = sb("n_mhalf", [P, NT])
        xn = sb("n_xn", [P, 2, HID])
        xt = sb("n_xt", [P, 2, KT, P])
        win = sb("n_win", [P, KT, H])
        hcol = sb("n_hcol", [H, 3])
        ones = sb("n_ones", [H, C])
        pre = sb("n_pre", [H, L])
        ab = sb("n_ab", [H, L])
        ex = sb("n_ex", [H, L])
        u1 = sb("n_u1", [H, L])
        ln = sb("n_ln", [H, L])
        df = sb("n_df", [H, L])
        rc = sb("n_rc", [H, L])
        gg = sb("n_gg", [H, L])
        G = sb("n_G", [H, 2, L])
        wexp = sb("n_wexp", [H, L])
        rows = sb("n_rows", [P, L])
        pt = [pb(f"n_pt{i}", [P, KT, P]) for i in range(2)]
        pdt = [pb(f"n_pdt{i}", [P, L]) for i in range(2)]
        ptab = pb("n_ptab", [P, NC, P])

        x_in = [sem(f"n_x_in{b}") for b in range(B)]
        small_in = sem("n_small_in")
        const_set = sem("n_const_set")
        stats_set = sem("n_stats_set")
        mv_set = sem("n_mv_set")
        var_set = sem("n_var_set")
        rstd_set = sem("n_rstd_set")
        xn_set = sem("n_xn_set")
        xt_done = sem("n_xt_done")
        raw_set = sem("n_raw_set")
        lo_set = sem("n_lo_set")
        dt_done = sem("n_dt_done")
        act_step = sem("n_act_step")
        raw_step = sem("n_raw_step")
        dve_step = sem("n_dve_step")
        rows_set = sem("n_rows_set")
        tabs_done = sem("n_tabs_done")
        tabs_saved = sem("n_tabs_saved")
        g_out = [sem(f"n_g_out{b}") for b in range(B)]
        block = ctx.enter_context(nc.Block())

        @block.sync
        def _(sp):
            for b in range(B):
                sp.dma_start(xin[:, b * NC:(b + 1) * NC, :],
                             io["x"][b * L:(b + 1) * L, :].rearrange("(c p) n -> p c n", p=P)).then_inc(x_in[b], 16)
            sp.dma_start(win[:, :, :], io["win_t"].rearrange("(k p) h -> p k h", p=P)).then_inc(small_in, 16)
            sp.dma_start(hcol[:, 0:1], io["dt_bias"].rearrange("(h a) -> h a", a=1)).then_inc(small_in, 16)
            sp.dma_start(hcol[:, 1:2], io["A_log_bias"].rearrange("(h a) -> h a", a=1)).then_inc(small_in, 16)
            for b in range(B):
                sp.wait_ge(dve_step, 9 * b + 8)
                for g in range(KVH):
                    sp.dma_start(g_dram[g, b].rearrange("c h t -> h c t"),
                                 G[g * HG:(g + 1) * HG, b % 2, :].rearrange("h (c t) -> h c t", t=C)).then_inc(g_out[b], 16)
            for b in range(B):
                sp.wait_ge(g_out[b], 16 * KVH)

        @block.gpsimd
        def _(pool):
            pool.memset(ident[:, :], 0.0).then_inc(const_set, 1)
            pool.memset(mhalf[:, :], -0.5).then_inc(const_set, 1)
            pool.memset(ones[:, :], 1.0).then_inc(const_set, 1)
            pool.wait_ge(const_set, 3)
            pool.affine_select(out=ident[:, :], in_=ident[:, :], compare_op=ALU.not_equal, fill=1.0,
                               base=0, pattern=[[-1, P]], channel_multiplier=1).then_inc(const_set, 1)
            for b in range(B):
                c0, c1 = b * NC, (b + 1) * NC
                pool.wait_ge(mv_set, c1)
                pool.tensor_scalar(var[:, c0:c1], mv[:, c0:c1, 1], EPS, None, ALU.add).then_inc(var_set, 1)
                pool.wait_ge(var_set, b + 1)
                pool.tensor_tensor(rstd[:, c0:c1], var[:, c0:c1], mhalf[:, c0:c1], ALU.pow).then_inc(rstd_set, 1)

        @block.vector
        def _(dve):
            def statistics(b):
                dve.wait_ge(x_in[b], 16)
                for i in range(b * NC, (b + 1) * NC):
                    dve.bn_stats(stats[:, i, :], xin[:, i, :]).then_inc(stats_set, 1)
                for i in range(b * NC, (b + 1) * NC):
                    dve.wait_ge(stats_set, i + 1)
                    dve.bn_aggr(mv[:, i, :], stats[:, i, :]).then_inc(mv_set, 1)

            def normalise(i):
                if i % NC == 0:
                    dve.wait_ge(rstd_set, i // NC + 1)
                if i >= 2:
                    dve.wait_ge(xt_done, i - 1)
                dve.tensor_scalar(xn[:, i % 2, :], xin[:, i, :], mv[:, i, 0:1], rstd[:, i:i + 1],
                                  ALU.subtract, ALU.mult).then_inc(xn_set, 1)

            def low_part(i):
                dve.wait_ge(raw_set, i + 2)
                dve.tensor_tensor(xl[:, :, i * P:(i + 1) * P], pt[i % 2][:, :, :],
                                  xh[:, :, i * P:(i + 1) * P].bitcast(F32), ALU.subtract).then_inc(lo_set, 1)

            def tables(b):
                s, G_b = 9 * b, G[:, b % 2, :]
                dve.wait_ge(act_step, 4 * b + 2)
                dve.tensor_scalar(u1[:, :], ex[:, :], 1.0, None, ALU.add).then_inc(dve_step, 1)
                dve.wait_ge(dve_step, s + 1)
                dve.scalar_tensor_tensor(df[:, :], u1[:, :], -1.0, ex[:, :], ALU.add, ALU.subtract).then_inc(dve_step, 1)
                dve.reciprocal(rc[:, :], u1[:, :]).then_inc(dve_step, 1)
                dve.wait_ge(dve_step, s + 3)
                dve.tensor_tensor(rc[:, :], df[:, :], rc[:, :], ALU.mult).then_inc(dve_step, 1)
                dve.wait_ge(dve_step, s + 4)
                dve.wait_ge(act_step, 4 * b + 3)
                dve.tensor_tensor(ln[:, :], ln[:, :], rc[:, :], ALU.subtract).then_inc(dve_step, 1)
                dve.wait_ge(dve_step, s + 5)
                if b:
                    dve.wait_ge(tabs_done, b)
                dve.scalar_tensor_tensor(rows[0:H, :], pre[:, :], 0.0, ln[:, :], ALU.max, ALU.add).then_inc(dve_step, 1)
                dve.wait_ge(dve_step, s + 6)
                dve.tensor_scalar(gg[:, :], rows[0:H, :], hcol[:, 2:3], -1.0, ALU.mult, ALU.mult).then_inc(dve_step, 1)
                dve.wait_ge(dve_step, s + 7)
                if b >= 2:
                    dve.wait_ge(g_out[b - 2], 16 * KVH)
                for c in range(NC):
                    scan = dve.tensor_tensor_scan(G_b[:, c * C:(c + 1) * C], ones[:, :], gg[:, c * C:(c + 1) * C],
                                                  0.0, ALU.mult, ALU.add)
                scan.then_inc(dve_step, 1)
                dve.wait_ge(dve_step, s + 8)
                dve.tensor_scalar(rows[H:2 * H, :], G_b, -1.0, None, ALU.mult).then_inc(dve_step, 1)
                dve.wait_ge(act_step, 4 * b + 4)
                dve.tensor_tensor(rows[3 * H:4 * H, :], rows[0:H, :], wexp[:, :], ALU.mult).then_inc(rows_set, 1)

            dve.wait_ge(const_set, 3)
            dve.wait_ge(raw_set, 1)
            statistics(0)
            for b in range(B):
                if b + 1 < B:
                    statistics(b + 1)
                for i in range(b * NC, (b + 1) * NC):
                    normalise(i)
                    if i:
                        low_part(i - 1)
                    if b and i == b * NC:
                        tables(b - 1)
            low_part(NT - 1)
            tables(B - 1)

        @block.scalar
        def _(act):
            act.wait_ge(small_in, 48)
            act.activation(hcol[:, 2:3], hcol[:, 1:2], ACT.Exp).then_inc(raw_set, 1)

            def halves(i):
                act.wait_ge(xt_done, i + 1)
                act.activation(xh[:, :, i * P:(i + 1) * P], pt[i % 2][:, :, :], ACT.Copy)
                if i >= 2:
                    act.wait_ge(dt_done, i - 1)
                act.activation(xt[:, i % 2, :, :], pt[i % 2][:, :, :], ACT.Copy).then_inc(raw_set, 1)

            def tables(b):
                act.wait_ge(dt_done, NC * (b + 1))
                if b:
                    act.wait_ge(dve_step, 9 * b)
                    act.wait_ge(rows_set, b)
                act.activation(pre[:, :], pdt[b % 2][0:H, :], ACT.Identity, bias=hcol[:, 0:1]).then_inc(act_step, 1)
                act.activation(ab[:, :], pdt[b % 2][0:H, :], ACT.Abs, bias=hcol[:, 0:1]).then_inc(raw_step, 1)
                act.wait_ge(raw_step, 2 * b + 1)
                act.wait_ge(act_step, 4 * b + 1)
                act.activation(ex[:, :], ab[:, :], ACT.Exp, scale=-1.0).then_inc(act_step, 1)
                act.wait_ge(dve_step, 9 * b + 1)
                act.activation(ln[:, :], u1[:, :], ACT.Ln).then_inc(act_step, 1)
                act.wait_ge(dve_step, 9 * b + 8)
                for c in range(NC):
                    at = slice(c * C, (c + 1) * C)
                    last = G[:, b % 2, (c + 1) * C - 1:(c + 1) * C]
                    w = act.activation(wexp[:, at], G[:, b % 2, at], ACT.Exp, scale=-1.0, bias=last)
                w.then_inc(act_step, 1)
                act.activation(rows[2 * H:3 * H, :], G[:, b % 2, :], ACT.Exp).then_inc(raw_step, 1)

            def save_tables(b):
                act.wait_ge(tabs_done, b + 1)
                act.activation(tab[:, b * NC:(b + 1) * NC, :], ptab[:, :, :], ACT.Copy).then_inc(tabs_saved, 1)

            for b in range(B):
                for i in range(b * NC, (b + 1) * NC):
                    halves(i)
                    if i >= 1 and i % NC == 0:
                        tables(i // NC - 1)
                if b:
                    save_tables(b - 1)
            tables(B - 1)
            save_tables(B - 1)

        @block.tensor
        def _(pe):
            pe.wait_ge(const_set, 4)
            pe.wait_ge(small_in, 48)

            def turn(i):
                pe.wait_ge(xn_set, i + 1)
                if i >= 2:
                    pe.wait_ge(lo_set, i - 1)
                    pe.wait_ge(raw_set, i)
                for k in range(KT):
                    t = pe.transpose(pt[i % 2][:, k, :], xn[:, i % 2, k * P:(k + 1) * P], ident[:, :])
                t.then_inc(xt_done, 1)

            def dt_rows(i):
                b, c = i // NC, i % NC
                pe.wait_ge(raw_set, i + 2)
                if b >= 2:
                    pe.wait_ge(act_step, 4 * (b - 2) + 2)
                    pe.wait_ge(raw_step, 2 * (b - 2) + 1)
                for k in range(KT):
                    m = pe.matmul(pdt[b % 2][0:H, c * P:(c + 1) * P], win[:, k, :], xt[:, i % 2, k, :],
                                  start=(k == 0), stop=(k == KT - 1))
                m.then_inc(dt_done, 1)

            def turn_tables(b):
                pe.wait_ge(rows_set, b + 1)
                pe.wait_ge(raw_step, 2 * b + 2)
                pe.wait_ge(dve_step, 9 * b + 9)
                if b:
                    pe.wait_ge(tabs_saved, b)
                for c in range(NC):
                    t = pe.transpose(ptab[:, c, :], rows[:, c * C:(c + 1) * C], ident[:, :])
                t.then_inc(tabs_done, 1)

            for i in range(NT):
                turn(i)
                if i:
                    dt_rows(i - 1)
                if i >= 2 * NC - 1 and i % NC == NC - 1:
                    turn_tables(i // NC - 1)
            dt_rows(NT - 1)
            turn_tables(B - 1)


def attention_stage(nc, io, keep):
    xh, xl, tab, ident, g_dram, z_dram = (keep[k] for k in ("xh", "xl", "tab", "ident", "g_dram", "z_dram"))
    with ExitStack() as ctx:
        def sb(name, shape, dt=F32):
            return ctx.enter_context(nc.sbuf_tensor(name, shape, dt))

        def pb(name):
            return ctx.enter_context(nc.psum_tensor(name, [P, HG, P], F32))

        def sem(name):
            return ctx.enter_context(nc.semaphore(name))

        w_raw = [sb(f"w_raw{i}", [P, 2 * GW]) for i in range(3)]
        wkv = [sb(f"wkv_{n}", [P, KT, 2 * D], F32R) for n in ("hi", "lo")]
        wq = [sb(f"wq_{n}", [P, KT, GW], F32R) for n in ("hi", "lo")]
        wg = [sb(f"wg_{n}", [P, KT, GW], F32R) for n in ("hi", "lo")]
        cos = sb("cos", [P, L])
        sin = sb("sin", [P, L])
        rope_a = sb("rope_a", [P, 2, L])
        rope_b = sb("rope_b", [P, 2, L])
        q = sb("q", [P, 2, HG, L])
        k = sb("k", [P, 2, L])
        v_t = sb("v_t", [P, L])
        k_tok = sb("k_tok", [P, NC, D])
        v_tok = sb("v_tok", [P, NC, D])
        stab = sb("stab", [P, 2, NC, TAB, HG])
        xc = sb("xc", [P, 2, HG, D])
        xw = sb("xw", [P, 2, HG, D])
        g_row = sb("g_row", [P, 2, HG, C])
        decay = sb("decay", [P, 2, HG, C])
        chunk_decay = sb("chunk_decay", [P, NC, HG])
        probs = sb("probs", [P, HG, C])
        state = sb("state", [P, 2, HG, D])
        tanh = sb("tanh", [P, GW])
        gate = sb("gate", [P, 2, GW])
        y_int = sb("y_int", [P, HG, D])
        y = sb("y", [P, HG, D])
        square = sb("square", [P, HG, D])
        ssum = sb("ssum", [P, NC, HG])
        svar = sb("svar", [P, NC, HG])
        srstd = sb("srstd", [P, NC, HG])
        mhalf = sb("mhalf", [P, HG])
        eps4 = sb("eps4", [P, HG])
        before = sb("before", [P, C])
        z = sb("z", [P, HG, D])
        z_t = sb("z_t", [P, 2, HG, C])

        p_proj = [pb(f"p_proj{i}") for i in range(2)]
        p_score, p_inter, p_intra, p_cst, p_zt, p_tok = (pb(n) for n in (
            "p_score", "p_inter", "p_intra", "p_cst", "p_zt", "p_tok"))

        w_in = [sem(f"w_in{i}") for i in range(3)]
        tab_in = sem("tab_in")
        g_in = [sem(f"g_in{i}") for i in range(2)]
        z_out = [sem(f"z_out{i}") for i in range(2)]
        unit_done, unit_free = sem("unit_done"), sem("unit_free")
        score_done, intra_done, inter_done = sem("score_done"), sem("intra_done"), sem("inter_done")
        cst_done, zt_done, tok_done = sem("cst_done"), sem("zt_done"), sem("tok_done")
        probs_set, state_set, y_set, z_set = sem("probs_set"), sem("state_set"), sem("y_set"), sem("z_set")
        gate_set, rope_terms, v_set = sem("gate_set"), sem("rope_terms"), sem("v_set")
        kv_split, q_split, g_split = sem("kv_split"), sem("q_split"), sem("g_split")
        kv_hi, q_hi, g_hi = sem("kv_hi"), sem("q_hi"), sem("g_hi")
        decay_set, tanh_set, yint_set = sem("decay_set"), sem("tanh_set"), sem("yint_set")
        squares_set, zt_saved, tok_saved = sem("squares_set"), sem("zt_saved"), sem("tok_saved")
        masked_set, roped, xc_set, xw_set = sem("masked_set"), sem("roped"), sem("xc_set"), sem("xw_set")
        mask_set = sem("mask_set")
        svar_set, srstd_set, stab_set, const_set = sem("svar_set"), sem("srstd_set"), sem("stab_set"), sem("const_set")
        block = ctx.enter_context(nc.Block())

        GATE_UNIT, K_UNIT, V_UNIT, Q_UNIT = (0, 3, 5, 7), 1, 2, (4, 6, 8, 9)

        def unit(n, at):
            if isinstance(n, int) and n == B * KVH - 1:
                at = GATE_UNIT.index(at)
            return UNITS * n + (FIRST_UNITS + at)

        def bank(n, b, at):
            if isinstance(n, int):
                return p_proj[unit(n, at) % 2]
            return p_proj[(FIRST_UNITS + UNITS * b + at) % 2]

        def steps(engine, first, step):
            def group(g):
                for b in range(B):
                    step(g, b, B * g + b)

            first()
            group(0)
            with engine.Fori(1, KVH - 1) as g:
                group(g)
            group(KVH - 1)

        def ahead(n):
            return not (isinstance(n, int) and n == B * KVH - 1)

        def more(n, c, by):
            return not (isinstance(n, int) and NC * n + c + by >= NC * B * KVH)

        def group_ahead(g):
            return not (isinstance(g, int) and g == KVH - 1)

        def part(i):
            return w_raw[i][:, :].rearrange("p (k n) -> p k n", k=KT if i == 0 else KT // 2)

        def dst(w, i):
            return w[:, :, :] if i == 0 else w[:, (i - 1) * 2:i * 2, :]

        @block.sync
        def _(sp):
            def load_kv(g):
                sp.dma_start(part(0), io["wkv_t"][bass.ds(g, 1)].rearrange("a (k p) n -> p (a k) n", p=P)).then_inc(w_in[0], 16)

            def load_half(w, g, i):
                sp.dma_start(part(i), io[w][bass.ds(g, 1), (i - 1) * 2 * P:i * 2 * P].rearrange(
                    "a (k p) n -> p (a k) n", p=P)).then_inc(w_in[i], 16)

            def load_g(g, b, c):
                src = g_dram[bass.ds(g, 1), b, c].rearrange("a h t -> a (h t)").to_broadcast([P, HG * C])
                sp.dma_start(g_row[:, c % 2].rearrange("p h t -> p (h t)"), src).then_inc(g_in[c % 2], 16)

            def first():
                load_kv(0)
                load_half("wq_t", 0, 1)
                load_half("wq_t", 0, 2)
                sp.dma_start(cos[:, :], io["cos_t"]).then_inc(tab_in, 16)
                sp.dma_start(sin[:, :], io["sin_t"]).then_inc(tab_in, 16)
                load_g(0, 0, 0)
                load_g(0, 0, 1)
                sp.wait_ge(q_split, 1)
                load_half("wg_t", 0, 1)
                load_half("wg_t", 0, 2)

            def step(g, b, n):
                for c in range(NC):
                    m = NC * n + c
                    if more(n, c, 2):
                        sp.wait_ge(decay_set, m + 1)
                        nb, ncc = b + (c + 2) // NC, (c + 2) % NC
                        load_g(g + nb // B, nb % B, ncc)
                    if c > 0:
                        store_z(g, b, n, c - 1)
                    if group_ahead(g):
                        if b == 0 and c == 1:
                            sp.wait_ge(kv_split, g + 1)
                            load_kv(g + 1)
                        if b == 0 and c == 2:
                            sp.wait_ge(g_split, g + 1)
                            load_half("wq_t", g + 1, 1)
                            load_half("wq_t", g + 1, 2)
                        if b == B - 1 and c == 2:
                            sp.wait_ge(q_split, g + 2)
                            load_half("wg_t", g + 1, 1)
                            load_half("wg_t", g + 1, 2)
                store_z(g, b, n, NC - 1)

            def store_z(g, b, n, c):
                sp.wait_ge(zt_saved, NC * n + c + 1)
                sp.dma_start(z_dram[b * NC + c, :, bass.ds(g * HG, HG), :], z_t[:, c % 2]).then_inc(z_out[c % 2], 16)

            steps(sp, first, step)
            for s in range(2):
                sp.wait_ge(z_out[s], 16 * B * KVH * NC // 2)

        @block.tensor
        def _(pe):
            def wide(out, pairs):
                for i, (lhs, rhs) in enumerate(pairs):
                    for j, (a, e) in enumerate(((0, 0), (1, 0), (0, 1))):
                        mm = pe.matmul(out, lhs[a], rhs[e], start=(i == 0 and j == 0),
                                       stop=(i == len(pairs) - 1 and j == 2))
                return mm

            def project(w, w0, b, u, into):
                t = slice(b * L, (b + 1) * L)
                wide(into[:, :, :].rearrange("p h t -> p (h t)"),
                     [((w[0][:, kt, w0:w0 + D], w[1][:, kt, w0:w0 + D]), (xh[:, kt, t], xl[:, kt, t]))
                      for kt in range(KT)]).then_inc(unit_done, 1)

            def gates(g, b, n, c):
                u = unit(n, GATE_UNIT[c])
                wait_ge(pe, unit_free, u - 1)
                if b == 0 and c == 0:
                    pe.wait_ge(g_split, g + 1)
                t = slice(b * L + c * C, b * L + (c + 1) * C)
                wide(bank(n, b, GATE_UNIT[c])[:, :, :].rearrange("p h t -> p (h t)"),
                     [((xh[:, kt, t], xl[:, kt, t]), (wg[0][:, kt, :], wg[1][:, kt, :]))
                      for kt in range(KT)]).then_inc(unit_done, 1)

            def next_unit(g, b, n, at):
                if not ahead(n):
                    return
                u = unit(n, at)
                wait_ge(pe, unit_free, u - 1)
                if b == B - 1 and at == K_UNIT:
                    pe.wait_ge(kv_split, g + 2)
                if b == B - 1 and at == Q_UNIT[0]:
                    pe.wait_ge(q_split, g + 2)
                w, w0 = (wkv, 0) if at == K_UNIT else (wkv, D) if at == V_UNIT else (wq, Q_UNIT.index(at) * D)
                project(w, w0, (b + 1) % B, u, bank(n, b, at))

            def v_turn(n):
                pe.wait_ge(v_set, n + 1)
                wait_ge(pe, tok_saved, 2 * n)
                for c in range(NC):
                    t = pe.transpose(p_tok[:, c, :], v_t[:, c * C:(c + 1) * C], ident[:, :])
                t.then_inc(tok_done, 1)

            def k_turn(n, b):
                pe.wait_ge(roped, ROPED * n + 1)
                pe.wait_ge(tok_saved, 2 * n + 1)
                for c in range(NC - 1):
                    t = pe.transpose(p_tok[:, c, :], k[:, b % 2, c * C:(c + 1) * C], ident[:, :])
                t.then_inc(tok_done, 1)

            def scores(n, b, c):
                if c == 0:
                    pe.wait_ge(roped, ROPED * (n + 1))
                wait_ge(pe, probs_set, NC * n + c)
                pe.matmul(p_score[:, :, :], k[:, b % 2, c * C:(c + 1) * C], q[:, b % 2, :, c * C:(c + 1) * C],
                          start=True, stop=True).then_inc(score_done, 1)

            def chunk_state(n, c):
                pe.wait_ge(xw_set, 3 * n + c + 1)
                if c == 0:
                    pe.wait_ge(tok_saved, 2 * n + 2)
                wait_ge(pe, state_set, 3 * n + c)
                pe.matmul(p_cst[:, :, :], k_tok[:, c, :], xw[:, c % 2, :, :], start=True, stop=True).then_inc(cst_done, 1)

            def inter(n, b, c):
                wait_ge(pe, state_set, 3 * n + c)
                wait_ge(pe, yint_set, 3 * n + c - 1)
                for h in range(HG):
                    mm = pe.matmul(p_inter[:, h, :], q[:, b % 2, h, c * C:(c + 1) * C], state[:, c % 2, h, :],
                                   start=True, stop=True)
                mm.then_inc(inter_done, 1)

            def intra(n, c):
                m = NC * n + c
                pe.wait_ge(probs_set, m + 1)
                pe.wait_ge(xc_set, m + 1)
                wait_ge(pe, y_set, m)
                for h in range(HG):
                    mm = pe.matmul(p_intra[:, h, :], probs[:, h, :], xc[:, c % 2, h, :], start=True, stop=True)
                mm.then_inc(intra_done, 1)

            def z_turn(n, c):
                m = NC * n + c
                pe.wait_ge(z_set, m + 1)
                wait_ge(pe, zt_saved, m)
                for h in range(HG):
                    t = pe.transpose(p_zt[:, h, :], z[:, h, :], ident[:, :])
                t.then_inc(zt_done, 1)

            def first():
                pe.wait_ge(kv_split, 1)
                project(wkv, 0, 0, 0, p_proj[0])
                project(wkv, D, 0, 1, p_proj[1])
                pe.wait_ge(q_split, 1)
                for h in range(HG):
                    pe.wait_ge(unit_free, h + 1)
                    project(wq, h * D, 0, 2 + h, p_proj[h % 2])
                v_turn(0)
                k_turn(0, 0)

            def step(g, b, n):
                gates(g, b, n, 0)
                next_unit(g, b, n, K_UNIT)
                scores(n, b, 0)
                chunk_state(n, 0)
                next_unit(g, b, n, V_UNIT)
                intra(n, 0)
                for c in (1, 2):
                    scores(n, b, c)
                    gates(g, b, n, c)
                    chunk_state(n, c)
                    inter(n, b, c)
                    next_unit(g, b, n, Q_UNIT[c - 1])
                    intra(n, c)
                    z_turn(n, c - 1)
                scores(n, b, 3)
                if ahead(n):
                    v_turn(n + 1)
                gates(g, b, n, 3)
                if ahead(n):
                    k_turn(n + 1, b + 1)
                inter(n, b, 3)
                intra(n, 3)
                z_turn(n, 2)
                next_unit(g, b, n, Q_UNIT[2])
                next_unit(g, b, n, Q_UNIT[3])
                z_turn(n, 3)

            steps(pe, first, step)

        @block.vector
        def _(dve):
            def split(w, pieces, hi_sem, done, g, last_use):
                for j, i in enumerate(pieces):
                    dve.wait_ge(hi_sem, len(pieces) * g + j + 1)
                    lo = dve.tensor_tensor(dst(w[1], i), part(i), dst(w[0], i).bitcast(F32), ALU.subtract)
                lo.then_inc(done, 1)

            def rotate(bank_, r, n, b):
                s, half = (b + r) % 2, D // 2
                x = bank_[:, :, :].rearrange("p h t -> p (h t)")
                wait_ge(dve, roped, ROPED * n + r - 1)
                dve.tensor_tensor(rope_a[:, s, :], x, cos[:, :], ALU.mult)
                dve.tensor_tensor(rope_b[0:half, s, :], x[half:D, :], sin[0:half, :], ALU.mult)
                dve.tensor_tensor(rope_b[half:D, s, :], x[0:half, :], sin[half:D, :], ALU.mult).then_inc(rope_terms, 1)

            def rotate_next(g, b, n, at, r):
                if not ahead(n):
                    return
                u = unit(n, at)
                dve.wait_ge(unit_done, u + 1)
                rotate(bank(n, b, at), r, n + 1, b + 1)
                dve.wait_ge(rope_terms, ROPED * (n + 1) + r + 1)
                dve.sem_inc(unit_free, 1)

            def first():
                dve.memset(mhalf[:, :], -0.5).then_inc(const_set, 1)
                dve.memset(eps4[:, :], 4.0 * EPS).then_inc(const_set, 1)
                split(wkv, (0,), kv_hi, kv_split, 0, None)
                split(wq, (1, 2), q_hi, q_split, 0, None)
                dve.wait_ge(tab_in, 32)
                for j in range(FIRST_UNITS):
                    dve.wait_ge(unit_done, j + 1)
                    if j == 1:
                        dve.tensor_copy(v_t[:, :], p_proj[1][:, :, :].rearrange("p h t -> p (h t)")).then_inc(v_set, 1)
                        dve.wait_ge(v_set, 1)
                    else:
                        r = 0 if j == 0 else j - 1
                        rotate(p_proj[j % 2], r, 0, 0)
                        dve.wait_ge(rope_terms, r + 1)
                    dve.sem_inc(unit_free, 1)
                split(wg, (1, 2), g_hi, g_split, 0, None)

            def make_gate(g, b, n, c):
                m, u = NC * n + c, unit(n, GATE_UNIT[c])
                dve.wait_ge(tanh_set, m + 1)
                dve.scalar_tensor_tensor(gate[:, c % 2, :], tanh[:, :], 1.0,
                                         bank(n, b, GATE_UNIT[c])[:, :, :].rearrange("p h t -> p (h t)"),
                                         ALU.add, ALU.mult).then_inc(unit_free, 1)

            def make_probs(n, c):
                m = NC * n + c
                dve.wait_ge(score_done, m + 1)
                dve.wait_ge(decay_set, m + 1)
                dve.tensor_tensor(probs[:, :, :], p_score[:, :, :], decay[:, c % 2, :, :], ALU.mult).then_inc(probs_set, 1)

            def make_state(n, c):
                dve.wait_ge(cst_done, 3 * n + c + 1)
                if c == 0:
                    s = dve.tensor_copy(state[:, 1, :, :], p_cst[:, :, :])
                else:
                    for h in range(HG):
                        s = dve.scalar_tensor_tensor(state[:, (c + 1) % 2, h, :], state[:, c % 2, h, :],
                                                     chunk_decay[:, c, h:h + 1], p_cst[:, h, :], ALU.mult, ALU.add)
                s.then_inc(state_set, 1)

            def make_y(n, c):
                m = NC * n + c
                dve.wait_ge(intra_done, m + 1)
                if c == 0:
                    dve.tensor_copy(y[:, :, :], p_intra[:, :, :]).then_inc(y_set, 1)
                else:
                    wait_ge(dve, yint_set, 3 * n + c)
                    dve.tensor_tensor(y[:, :, :], p_intra[:, :, :], y_int[:, :, :], ALU.add).then_inc(y_set, 1)

            def make_z(n, c):
                m = NC * n + c
                dve.wait_ge(srstd_set, m + 1)
                wait_ge(dve, zt_done, m)
                for h in range(HG):
                    zz = dve.scalar_tensor_tensor(z[:, h, :], y[:, h, :], srstd[:, c, h:h + 1],
                                                  gate[:, c % 2, h * D:(h + 1) * D], ALU.mult, ALU.mult)
                zz.then_inc(z_set, 1)

            def step(g, b, n):
                if group_ahead(g) and b == B - 1:
                    split(wq, (1, 2), q_hi, q_split, g + 1, None)
                make_gate(g, b, n, 0)
                rotate_next(g, b, n, K_UNIT, 0)
                make_probs(n, 0)
                make_state(n, 0)
                if ahead(n):
                    dve.wait_ge(unit_done, unit(n, V_UNIT) + 1)
                    dve.tensor_copy(v_t[:, :], bank(n, b, V_UNIT)[:, :, :].rearrange("p h t -> p (h t)")).then_inc(v_set, 1)
                    dve.wait_ge(v_set, n + 2)
                    dve.sem_inc(unit_free, 1)
                make_y(n, 0)
                make_z(n, 0)
                for c in (1, 2):
                    make_probs(n, c)
                    make_gate(g, b, n, c)
                    make_state(n, c)
                    make_y(n, c)
                    rotate_next(g, b, n, Q_UNIT[c - 1], c)
                    if c == 1 and group_ahead(g) and b == B - 2:
                        split(wkv, (0,), kv_hi, kv_split, g + 1, None)
                    make_z(n, c)
                make_probs(n, 3)
                make_gate(g, b, n, 3)
                make_y(n, 3)
                rotate_next(g, b, n, Q_UNIT[2], 3)
                make_z(n, 3)
                if group_ahead(g) and b == B - 1:
                    split(wg, (1, 2), g_hi, g_split, g + 1, None)
                rotate_next(g, b, n, Q_UNIT[3], 4)

            steps(dve, first, step)

        @block.scalar
        def _(act):
            def split(w, pieces, done, g, loads):
                for i in pieces:
                    act.wait_ge(w_in[i], 16 * loads)
                    act.activation(dst(w[0], i), part(i), ACT.Copy).then_inc(done, 1)

            def make_decay(n, b, c):
                act.wait_ge(masked_set, NC * n + c + 1)
                if c == 0:
                    act.wait_ge(stab_set, n + 1)
                wait_ge(act, probs_set, NC * n + c - 1)
                act.activation(chunk_decay[:, c, :], g_row[:, c % 2, :, C - 1], ACT.Exp)
                for h in range(HG):
                    e = act.activation(decay[:, c % 2, h, :], g_row[:, c % 2, h, :], ACT.Exp,
                                       bias=stab[:, b % 2, c, T_NEGG, h:h + 1])
                e.then_inc(decay_set, 1)

            def make_tanh(g, b, n, c):
                act.wait_ge(unit_done, unit(n, GATE_UNIT[c]) + 1)
                act.activation(tanh[:, :], bank(n, b, GATE_UNIT[c])[:, :, :].rearrange("p h t -> p (h t)"),
                               ACT.Tanh, scale=0.5).then_inc(tanh_set, 1)

            def scale_inter(n, b, c):
                act.wait_ge(inter_done, 3 * n + c)
                wait_ge(act, y_set, NC * n + c)
                for h in range(HG):
                    s = act.activation(y_int[:, h, :], p_inter[:, h, :], ACT.Copy, scale=stab[:, b % 2, c, T_EXPG, h:h + 1])
                s.then_inc(yint_set, 1)

            def squares(n, c):
                act.wait_ge(y_set, NC * n + c + 1)
                for h in range(HG):
                    s = act.activation(square[:, h, :], y[:, h, :], ACT.Square, scale=2.0 / float(np.sqrt(D)),
                                       accum_out=ssum[:, c, h:h + 1])
                s.then_inc(squares_set, 1)

            def save_z(n, c):
                m = NC * n + c
                act.wait_ge(zt_done, m + 1)
                wait_ge(act, z_out[c % 2], 16 * (2 * n + c // 2))
                act.activation(z_t[:, c % 2, :, :], p_zt[:, :, :], ACT.Copy).then_inc(zt_saved, 1)

            def save_v(n):
                act.wait_ge(tok_done, 2 * n + 1)
                wait_ge(act, xc_set, NC * n)
                wait_ge(act, xw_set, 3 * n)
                act.activation(v_tok[:, :, :], p_tok[:, :, :], ACT.Copy).then_inc(tok_saved, 1)

            def save_k(n):
                act.wait_ge(tok_done, 2 * n + 2)
                act.activation(k_tok[:, 0:NC - 1, :], p_tok[:, 0:NC - 1, :], ACT.Copy).then_inc(tok_saved, 1)

            def first():
                split(wkv, (0,), kv_hi, 0, 1)
                split(wq, (1, 2), q_hi, 0, 1)
                make_decay(0, 0, 0)
                split(wg, (1, 2), g_hi, 0, 2)
                save_v(0)
                save_k(0)

            def step(g, b, n):
                if group_ahead(g) and b == B - 1:
                    act.wait_ge(unit_done, UNITS * n + FIRST_UNITS)
                    split(wq, (1, 2), q_hi, g + 1, 2 * g + 3)
                make_tanh(g, b, n, 0)
                make_decay(n, b, 1)
                squares(n, 0)
                for c in (1, 2):
                    make_decay(n, b, c + 1)
                    make_tanh(g, b, n, c)
                    scale_inter(n, b, c)
                    if c == 1 and group_ahead(g) and b == B - 2:
                        act.wait_ge(unit_done, unit(n, V_UNIT) + 1)
                        split(wkv, (0,), kv_hi, g + 1, g + 2)
                    squares(n, c)
                    save_z(n, c - 1)
                if ahead(n):
                    save_v(n + 1)
                make_tanh(g, b, n, 3)
                if ahead(n):
                    save_k(n + 1)
                scale_inter(n, b, 3)
                squares(n, 3)
                save_z(n, 2)
                if group_ahead(g) and b == B - 1:
                    split(wg, (1, 2), g_hi, g + 1, 2 * g + 4)
                if ahead(n):
                    make_decay(n + 1, b + 1, 0)
                save_z(n, 3)

            steps(act, first, step)

        @block.gpsimd
        def _(pool):
            def step_tables(g, b, n):
                src = tab[:, b * NC:(b + 1) * NC, :].rearrange("p c (k h) -> p c k h", k=TAB)
                pool.tensor_copy(stab[:, b % 2], src[:, :, :, bass.ds(g * HG, HG)]).then_inc(stab_set, 1)

            def mask(n, c):
                pool.wait_ge(g_in[c % 2], 16 * (2 * n + c // 2 + 1))
                pool.tensor_tensor(g_row[:, c % 2], g_row[:, c % 2], before[:, :].unsqueeze(1).to_broadcast([P, HG, C]),
                                   ALU.add).then_inc(masked_set, 1)

            def add_rope(n, b, r):
                s = (b + r) % 2
                pool.wait_ge(rope_terms, ROPED * n + r + 1)
                out = k[:, b % 2, :] if r == 0 else q[:, b % 2, r - 1, :]
                pool.tensor_tensor(out, rope_a[:, s, :], rope_b[:, s, :], ALU.add).then_inc(roped, 1)

            def scaled_v(out, b, c, which):
                v = v_tok[:, c, :].unsqueeze(1).to_broadcast([P, HG, D])
                w = stab[:, b % 2, c, which, :].unsqueeze(2).to_broadcast([P, HG, D])
                return pool.tensor_tensor(out[:, c % 2], v, w, ALU.mult)

            def make_xc(n, b, c):
                if c == 0:
                    pool.wait_ge(tok_saved, 2 * n + 1)
                    pool.wait_ge(stab_set, n + 1)
                wait_ge(pool, intra_done, NC * n + c - 1)
                scaled_v(xc, b, c, T_DT).then_inc(xc_set, 1)

            def make_xw(n, b, c):
                wait_ge(pool, cst_done, 3 * n + (c - 1 if c else 0))
                scaled_v(xw, b, c, T_W).then_inc(xw_set, 1)

            def rms(n, c):
                m = NC * n + c
                pool.wait_ge(squares_set, m + 1)
                pool.tensor_tensor(svar[:, c, :], ssum[:, c, :], eps4[:, :], ALU.add).then_inc(svar_set, 1)
                pool.wait_ge(svar_set, m + 1)
                pool.tensor_tensor(srstd[:, c, :], svar[:, c, :], mhalf[:, :], ALU.pow).then_inc(srstd_set, 1)

            def first():
                pool.memset(before[:, :], 0.0).then_inc(mask_set, 1)
                pool.wait_ge(mask_set, 1)
                pool.affine_select(out=before[:, :], in_=before[:, :], compare_op=ALU.is_ge, fill=-1e30,
                                   base=0, pattern=[[1, C]], channel_multiplier=-1).then_inc(mask_set, 1)
                pool.wait_ge(const_set, 2)
                step_tables(0, 0, 0)
                pool.wait_ge(mask_set, 2)
                mask(0, 0)
                for r in range(ROPED):
                    add_rope(0, 0, r)
                make_xc(0, 0, 0)
                make_xw(0, 0, 0)

            def step(g, b, n):
                mask(n, 1)
                make_xc(n, b, 1)
                make_xw(n, b, 1)
                if ahead(n):
                    wait_ge(pool, yint_set, 3 * n)
                    step_tables(g if b < B - 1 else g + 1, (b + 1) % B, n + 1)
                    add_rope(n + 1, b + 1, 0)
                rms(n, 0)
                mask(n, 2)
                make_xc(n, b, 2)
                make_xw(n, b, 2)
                rms(n, 1)
                if ahead(n):
                    add_rope(n + 1, b + 1, 1)
                mask(n, 3)
                make_xc(n, b, 3)
                rms(n, 2)
                if ahead(n):
                    add_rope(n + 1, b + 1, 2)
                    mask(n + 1, 0)
                    make_xc(n + 1, b + 1, 0)
                    make_xw(n + 1, b + 1, 0)
                rms(n, 3)
                if ahead(n):
                    add_rope(n + 1, b + 1, 3)
                    add_rope(n + 1, b + 1, 4)

            steps(pool, first, step)


def output_stage(nc, io, keep):
    ident, z_dram = keep["ident"], keep["z_dram"]
    HP = 8
    NP = H // HP
    WH = 2
    NW = H // WH
    SLOTS = 4
    SCALE = 1.0 / float(np.sqrt(np.float32(DK)))
    with ExitStack() as ctx:
        def sb(name, shape, dt=F32):
            return ctx.enter_context(nc.sbuf_tensor(name, shape, dt))

        def pb(name, shape=(P, HID)):
            return ctx.enter_context(nc.psum_tensor(name, list(shape), F32))

        def sem(name):
            return ctx.enter_context(nc.semaphore(name))

        raw = [sb(f"raw{i}", [P, HP * P]) for i in range(SLOTS)]
        z_hi = [sb(f"z_hi{i}", [P, HP, P], F32R) for i in range(2)]
        z_lo = [sb(f"z_lo{i}", [P, HP, P], F32R) for i in range(2)]
        wo = [sb(f"wo_{n}", [P, H, HID], F32R) for n in ("hi", "lo")]
        gn = sb("gn", [P, 1])
        ws = sb("ws", [P, KT, HID])
        wqk = sb("wqk", [P, KT, 2 * E * DK])
        wa = sb("wa", [P, KT, E * R])
        bm = sb("bm", [P, HID])
        bias = sb("bias", [P, HID])
        x_res = sb("x_res", [P, 2, HID])
        x1 = sb("x1", [P, HID])
        x1b = sb("x1b", [P, HID])
        xn = sb("xn", [P, HID])
        xt = sb("xt", [P, KT, P])
        stats, mv, var, rstd, mhalf = sb("stats", [P, 6]), sb("mv", [P, 2]), sb("var", [P, 1]), sb("rstd", [P, 1]), sb("mh", [P, 1])
        eps = sb("eps", [P, 1])
        keys = sb("keys", [P, E, DK])
        qk = sb("qk", [P, E, DK])
        sc, ew = sb("sc", [P, E]), sb("ew", [P, E])
        mx, nmx, den, rden = (sb(n, [P, 1]) for n in ("mx", "nmx", "den", "rden"))
        hw, hwn = sb("hw", [P, E, R]), sb("hwn", [P, E * R])
        hwt = sb("hwt", [P, P])
        res = sb("res", [P, 2, HID])

        p_out = [pb(f"p_out{i}") for i in range(2)]
        p_xt, p_qk, p_h, p_hwt, p_f = pb("p_xt", (P, KT, P)), pb("p_qk"), pb("p_h", (P, E * R)), pb("p_hwt", (P, P)), pb("p_f")

        raw_in = [sem(f"raw_in{i}") for i in range(SLOTS)]
        small_in, gn_in = sem("small_in"), sem("gn_in")
        x_in = [sem(f"x_in{i}") for i in range(2)]
        out_sent = [sem(f"out_sent{i}") for i in range(2)]
        hi_set, lo_set, out_done, heads_done = sem("hi_set"), sem("lo_set"), sem("out_done"), sem("heads_done")
        x1_set, x1b_set, stats_set, mv_set, var_set, rstd_set, xn_set = (sem(s) for s in (
            "x1_set", "x1b_set", "stats_set", "mv_set", "var_set", "rstd_set", "xn_set"))
        xt_done, xt_saved, qk_done, keys_saved, prod_set, sc_set, mx_set, nmx_set, ew_set = (sem(s) for s in (
            "xt_done", "xt_saved", "qk_done", "keys_saved", "prod_set", "sc_set", "mx_set", "nmx_set", "ew_set"))
        rden_set, hw_set, hwn_set, hwt_done, hwt_saved, f_done, res_set, c_set = (sem(s) for s in (
            "rden_set", "hw_set", "hwn_set", "hwt_done", "hwt_saved", "f_done", "res_set", "c_set"))
        block = ctx.enter_context(nc.Block())

        def tiles(engine, first, step):
            first()
            step(0, 0, True)
            step(1, 1, True)
            with engine.Fori(1, NT // 2 - 1) as pair:
                step(2 * pair, 0, True)
                step(2 * pair + 1, 1, True)
            step(NT - 2, 0, True)
            step(NT - 1, 1, False)

        @block.sync
        def _(sp):
            def load_z(i, j):
                sp.dma_start(raw[j % SLOTS][:, :], z_dram[bass.ds(i, 1), :, j * HP:(j + 1) * HP, :].rearrange(
                    "a p h t -> p (a h t)")).then_inc(raw_in[j % SLOTS], 16)

            def load_x(i, s):
                sp.dma_start(x_res[:, s, :], io["x"][bass.ds(i * P, P), :]).then_inc(x_in[s], 16)

            def first():
                sp.dma_start(gn[:, :], io["gnorm_w"].rearrange("(p a) -> p a", a=1)).then_inc(gn_in, 16)
                for w in range(NW):
                    if w >= SLOTS:
                        sp.wait_ge(lo_set, w - SLOTS + 1)
                    sp.dma_start(raw[w % SLOTS][:, :].rearrange("p (h n) -> p h n", h=WH),
                                 io["wo_t"][w * WH * P:(w + 1) * WH * P, :].rearrange("(h p) n -> p h n", p=P)).then_inc(raw_in[w % SLOTS], 16)
                    if w == SLOTS - 1:
                        load_x(0, 0)
                        sp.dma_start(bias[:, :], io["b"].rearrange("(a n) -> a n", a=1).to_broadcast([P, HID])).then_inc(small_in, 16)
                        sp.dma_start(wqk[:, :, :], io["wqk_t"].rearrange("(k p) n -> p k n", p=P)).then_inc(small_in, 16)
                        sp.dma_start(wa[:, :, :], io["a_t"].rearrange("(k p) n -> p k n", p=P)).then_inc(small_in, 16)
                        sp.dma_start(ws[:, :, :], io["w_t"].rearrange("(k p) n -> p k n", p=P)).then_inc(small_in, 16)
                        sp.dma_start(bm[:, :], io["bm_t"]).then_inc(small_in, 16)
                for j in range(NP):
                    sp.wait_ge(lo_set, NW - SLOTS + j + 1)
                    load_z(0, j)

            def step(i, s, has_next):
                if has_next:
                    wait_ge(sp, x1_set, i)
                    load_x(i + 1, 1 - s)
                    for j in range(NP):
                        sp.wait_ge(lo_set, NW + NP * i + j + 1)
                        load_z(i + 1, j)
                if not isinstance(i, int) or i > 0:
                    store(i - 1, 1 - s)

            def store(i, s):
                sp.wait_ge(res_set, i + 1)
                sp.dma_start(io["out"][bass.ds(i * P, P), :], res[:, s, :]).then_inc(out_sent[s], 16)

            tiles(sp, first, step)
            store(NT - 1, 1)
            for s in range(2):
                sp.wait_ge(out_sent[s], 16 * NT // 2)

        @block.tensor
        def _(pe):
            def wo_piece(i, s, j):
                pe.wait_ge(lo_set, NW + NP * i + j + 1)
                if j == 0:
                    wait_ge(pe, x1_set, i - 1)
                for h in range(HP):
                    hh = j * HP + h
                    for t, (a, e) in enumerate(((z_hi, 0), (z_lo, 0), (z_hi, 1))):
                        mm = pe.matmul(p_out[s][:, :], a[j % 2][:, h, :], wo[e][:, hh, :],
                                       start=(hh == 0 and t == 0), stop=(hh == H - 1 and t == 2))
                mm.then_inc(heads_done, 1)

            def turn_x(i):
                pe.wait_ge(xn_set, i + 1)
                wait_ge(pe, xt_saved, i)
                for kt in range(KT):
                    t = pe.transpose(p_xt[:, kt, :], xn[:, kt * P:(kt + 1) * P], ident[:, :])
                t.then_inc(xt_done, 1)

            def experts(i):
                pe.wait_ge(xt_saved, i + 1)
                wait_ge(pe, prod_set, i)
                for kt in range(KT):
                    mm = pe.matmul(p_qk[:, :], xt[:, kt, :], wqk[:, kt, :], start=(kt == 0), stop=(kt == KT - 1))
                mm.then_inc(qk_done, 1)
                wait_ge(pe, hw_set, i)
                for kt in range(KT):
                    mm = pe.matmul(p_h[:, :], xt[:, kt, :], wa[:, kt, :], start=(kt == 0), stop=(kt == KT - 1))
                mm.then_inc(qk_done, 1)

            def dense(i):
                wait_ge(pe, res_set, i)
                for kt in range(KT):
                    pe.matmul(p_f[:, :], xt[:, kt, :], ws[:, kt, :], start=(kt == 0), stop=False)

            def turn_hw(i):
                pe.wait_ge(hwn_set, i + 1)
                wait_ge(pe, hwt_saved, i)
                pe.transpose(p_hwt[:, :], hwn[:, :], ident[:, :]).then_inc(hwt_done, 1)

            def combine(i):
                pe.wait_ge(hwt_saved, i + 1)
                pe.matmul(p_f[:, :], hwt[:, :], bm[:, :], start=False, stop=True).then_inc(f_done, 1)

            def first():
                for j in range(NP):
                    wo_piece(0, 0, j)
                pe.wait_ge(small_in, 80)

            def step(i, s, has_next):
                if has_next:
                    wo_piece(i + 1, 1 - s, 0)
                turn_x(i)
                if has_next:
                    wo_piece(i + 1, 1 - s, 1)
                experts(i)
                dense(i)
                if has_next:
                    wo_piece(i + 1, 1 - s, 2)
                turn_hw(i)
                if has_next:
                    wo_piece(i + 1, 1 - s, 3)
                combine(i)

            tiles(pe, first, step)

        @block.vector
        def _(dve):
            def wo_low(w):
                at = slice(w * WH, (w + 1) * WH)
                dve.wait_ge(hi_set, w + 1)
                dve.scalar_tensor_tensor(wo[1][:, at, :], raw[w % SLOTS][:, :].rearrange("p (h n) -> p h n", h=WH), gn[:, 0:1],
                                         wo[0][:, at, :].bitcast(F32), ALU.mult, ALU.subtract).then_inc(lo_set, 1)

            def z_low(i, j):
                dve.wait_ge(hi_set, NW + NP * i + j + 1)
                dve.tensor_tensor(z_lo[j % 2][:, :, :], raw[j % SLOTS][:, :].rearrange("p (h t) -> p h t", h=HP),
                                  z_hi[j % 2][:, :, :].bitcast(F32), ALU.subtract).then_inc(lo_set, 1)

            def first():
                dve.memset(mhalf[:, :], -0.5).then_inc(c_set, 1)
                dve.memset(eps[:, :], EPS).then_inc(c_set, 1)
                dve.wait_ge(gn_in, 16)
                for w in range(NW):
                    wo_low(w)
                for j in range(NP):
                    z_low(0, j)

            def step(i, s, has_next):
                if has_next:
                    z_low(i + 1, 0)
                dve.wait_ge(heads_done, NP * (i + 1))
                dve.wait_ge(x_in[s], 8 * (i - s) + 16)
                wait_ge(dve, x1b_set, i)
                dve.tensor_tensor(x1[:, :], p_out[s][:, :], x_res[:, s, :], ALU.add).then_inc(x1_set, 1)
                dve.wait_ge(x1_set, i + 1)
                dve.bn_stats(stats[:, :], x1[:, :]).then_inc(stats_set, 1)
                dve.wait_ge(c_set, 2)
                dve.wait_ge(stats_set, i + 1)
                dve.bn_aggr(mv[:, :], stats[:, :]).then_inc(mv_set, 1)
                dve.wait_ge(rstd_set, i + 1)
                wait_ge(dve, xt_done, i)
                dve.tensor_scalar(xn[:, :], x1[:, :], mv[:, 0:1], rstd[:, 0:1], ALU.subtract, ALU.mult).then_inc(xn_set, 1)
                if has_next:
                    z_low(i + 1, 1)
                    z_low(i + 1, 2)
                dve.wait_ge(keys_saved, i + 1)
                dve.tensor_tensor(qk[:, :, :], p_qk[:, 0:E * DK].rearrange("p (e d) -> p e d", e=E), keys[:, :, :],
                                  ALU.mult).then_inc(prod_set, 1)
                dve.wait_ge(prod_set, i + 1)
                dve.tensor_reduce(sc[:, :], qk[:, :, :], AX.X, ALU.add).then_inc(sc_set, 1)
                dve.wait_ge(sc_set, i + 1)
                dve.reduce_max(mx[:, :], sc[:, :], AX.X).then_inc(mx_set, 1)
                dve.wait_ge(mx_set, i + 1)
                dve.tensor_scalar(nmx[:, :], mx[:, :], -SCALE, None, ALU.mult).then_inc(nmx_set, 1)
                dve.wait_ge(ew_set, i + 1)
                dve.reciprocal(rden[:, :], den[:, :]).then_inc(rden_set, 1)
                dve.wait_ge(qk_done, 2 * i + 2)
                dve.tensor_tensor(hw[:, :, :], p_h[:, :].rearrange("p (e r) -> p e r", e=E),
                                  ew[:, :].unsqueeze(2).to_broadcast([P, E, R]), ALU.mult).then_inc(hw_set, 1)
                dve.wait_ge(hw_set, i + 1)
                dve.wait_ge(rden_set, i + 1)
                wait_ge(dve, hwt_done, i)
                dve.tensor_scalar(hwn[:, :], hw[:, :, :].rearrange("p e r -> p (e r)"), rden[:, 0:1], None,
                                  ALU.mult).then_inc(hwn_set, 1)
                if has_next:
                    z_low(i + 1, 3)
                dve.wait_ge(f_done, i + 1)
                dve.wait_ge(x1b_set, i + 1)
                wait_ge(dve, out_sent[s], 8 * (i - s))
                dve.tensor_tensor(res[:, s, :], p_f[:, :], x1b[:, :], ALU.add).then_inc(res_set, 1)

            tiles(dve, first, step)

        @block.scalar
        def _(act):
            def wo_high(w):
                at = slice(w * WH, (w + 1) * WH)
                act.wait_ge(raw_in[w % SLOTS], 16 * (w // SLOTS + 1))
                act.activation(wo[0][:, at, :], raw[w % SLOTS][:, :].rearrange("p (h n) -> p h n", h=WH), ACT.Copy,
                               scale=gn[:, 0:1]).then_inc(hi_set, 1)

            def z_high(i, j):
                act.wait_ge(raw_in[j % SLOTS], 16 * (NW // SLOTS) + 16 * (i + 1))
                wait_ge(act, heads_done, NP * i + j - 1)
                act.activation(z_hi[j % 2][:, :, :], raw[j % SLOTS][:, :].rearrange("p (h t) -> p h t", h=HP),
                               ACT.Copy).then_inc(hi_set, 1)

            def first():
                act.wait_ge(gn_in, 16)
                for w in range(NW):
                    wo_high(w)
                for j in range(NP):
                    z_high(0, j)

            def step(i, s, has_next):
                if has_next:
                    z_high(i + 1, 0)
                    z_high(i + 1, 1)
                act.wait_ge(xt_done, i + 1)
                wait_ge(act, f_done, i)
                act.activation(xt[:, :, :], p_xt[:, :, :], ACT.Copy).then_inc(xt_saved, 1)
                if has_next:
                    z_high(i + 1, 2)
                act.wait_ge(qk_done, 2 * i + 1)
                wait_ge(act, prod_set, i)
                act.activation(keys[:, :, :], p_qk[:, E * DK:].rearrange("p (e d) -> p e d", e=E), ACT.Copy).then_inc(keys_saved, 1)
                act.wait_ge(nmx_set, i + 1)
                wait_ge(act, hw_set, i)
                wait_ge(act, rden_set, i)
                act.activation(ew[:, :], sc[:, :], ACT.Exp, scale=SCALE, bias=nmx[:, 0:1], accum_out=den[:, 0:1]).then_inc(ew_set, 1)
                if has_next:
                    z_high(i + 1, 3)
                act.wait_ge(hwt_done, i + 1)
                act.activation(hwt[:, :], p_hwt[:, :], ACT.Copy).then_inc(hwt_saved, 1)

            tiles(act, first, step)

        @block.gpsimd
        def _(pool):
            def first():
                pool.wait_ge(c_set, 2)
                pool.wait_ge(small_in, 80)

            def step(i, s, has_next):
                pool.wait_ge(mv_set, i + 1)
                pool.tensor_tensor(var[:, :], mv[:, 1:2], eps[:, :], ALU.add).then_inc(var_set, 1)
                pool.wait_ge(var_set, i + 1)
                pool.tensor_tensor(rstd[:, :], var[:, :], mhalf[:, :], ALU.pow).then_inc(rstd_set, 1)
                wait_ge(pool, res_set, i)
                pool.wait_ge(xn_set, i + 1)
                pool.tensor_tensor(x1b[:, :], x1[:, :], bias[:, :], ALU.add).then_inc(x1b_set, 1)

            tiles(pool, first, step)


def build(nc, io):
    with ExitStack() as ctx:
        keep = {"g_dram": nc.dram_tensor("g_scratch", [KVH, B, NC, HG, C], F32).ap(),
                "z_dram": nc.dram_tensor("z_scratch", [NT, P, H, C], F32).ap(),
                "ident": ctx.enter_context(nc.sbuf_tensor("ident", [P, P], F32))}
        with ExitStack() as inner:
            keep["xh"] = inner.enter_context(nc.sbuf_tensor("xh", [P, KT, B * L], F32R))
            keep["xl"] = inner.enter_context(nc.sbuf_tensor("xl", [P, KT, B * L], F32R))
            keep["tab"] = inner.enter_context(nc.sbuf_tensor("tab", [P, NT, TAB * H], F32))
            norm_stage(nc, io, keep)
            attention_stage(nc, io, keep)
        output_stage(nc, io, keep)


def rope_tables():
    inv = (1.0 / np.float32(10000.0) ** (np.arange(0, D, 2, dtype=np.float32) / np.float32(D))).astype(np.float32)
    ang = np.arange(L, dtype=np.float32)[:, None] * inv
    cos, sin = np.cos(ang).T, np.sin(ang).T
    return (np.ascontiguousarray(np.concatenate([cos, cos]), np.float32),
            np.ascontiguousarray(np.concatenate([-sin, sin]), np.float32))


def kernel(**inputs):
    import numpy as _np
    import concourse.bacc as _bacc
    from concourse import mybir as _mybir
    from concourse.bass_utils import run_bass_kernel_spmd as _run

    a = {k: _np.asarray(v) for k, v in inputs.items()}
    cos, sin = rope_tables()
    t = _np.ascontiguousarray
    by_group = lambda w, n: t(w.reshape(KVH, n, HID).transpose(0, 2, 1))
    arrays = {
        "x": t(a["L0_attn_hidden_states"].reshape(B * L, HID)),
        "win_t": t(a["L0_attn_Win"].T),
        "dt_bias": t(a["L0_attn_dt_bias"]),
        "A_log_bias": t(a["L0_attn_A_log_bias"]),
        "gnorm_w": t(a["L0_attn_gnorm_w"]),
        "wq_t": by_group(a["L0_attn_Wq"], GW),
        "wg_t": by_group(a["L0_attn_Wg"], GW),
        "wkv_t": t(_np.concatenate([by_group(a["L0_attn_Wk"], D), by_group(a["L0_attn_Wv"], D)], axis=2)),
        "wo_t": t(a["L0_attn_Wo"].T),
        "w_t": t(a["L0_ffn_W"].T),
        "b": t(a["L0_ffn_b"]),
        "wqk_t": t(_np.concatenate([a["L0_ffn_Wq"].T, a["L0_ffn_Wk"].T], axis=1)),
        "a_t": t(a["L0_ffn_A"].reshape(E * R, HID).T),
        "bm_t": t(a["L0_ffn_Bm"].transpose(0, 2, 1).reshape(E * R, HID)),
        "cos_t": cos,
        "sin_t": sin,
    }
    nc = _bacc.Bacc("TRN2", target_bir_lowering=False, num_devices=1)
    io = {k: nc.dram_tensor(f"in_{k}", v.shape, _mybir.dt.from_np(v.dtype), kind="ExternalInput").ap()
          for k, v in arrays.items()}
    io["out"] = nc.dram_tensor("out_dram", (B * L, HID), _mybir.dt.float32, kind="ExternalOutput").ap()
    build(nc, io)
    r = _run(nc, [{f"in_{k}": v for k, v in arrays.items()}], core_ids=[0])
    return r.results[0]["out_dram"].reshape(B, L, HID)
```

```python
from contextlib import ExitStack

import numpy as np

import concourse.bass as bass
from concourse import mybir

ALU = mybir.AluOpType
ACT = mybir.ActivationFunctionType
AX = mybir.AxisListType
F32 = mybir.dt.float32
F32R = mybir.dt.float32r

P = 128
B, L, HID = 4, 512, 512
H, KVH, D = 32, 8, 128
C = 128
HG = H // KVH
NC = L // C
KT = HID // P
NT = B * NC
GW = HG * D
EPS = 1e-5
E, DK, R = 8, 32, 16
UNITS = 10
FIRST_UNITS = 6
ROPED = 1 + HG
TAB = 4
T_DT, T_NEGG, T_EXPG, T_W = range(TAB)


def wait_ge(engine, sem, count):
    if not isinstance(count, int) or count > 0:
        engine.wait_ge(sem, count)


def part(w_raw, i):
    return w_raw[i][:, :].rearrange("p (k n) -> p k n", k=KT if i == 0 else KT // 2)


def dst(w, i):
    return w[:, :, :] if i == 0 else w[:, (i - 1) * 2:i * 2, :]


def kv_piece(io, g):
    return io["wkv_t"][bass.ds(g, 1)].rearrange("a (k p) n -> p (a k) n", p=P)


def half_piece(w, g, i):
    return w[bass.ds(g, 1), (i - 1) * 2 * P:i * 2 * P].rearrange("a (k p) n -> p (a k) n", p=P)


def norm_stage(nc, io, keep):
    xh, xl, tab, ident, g_dram, w_raw, wkv, wq, wg = (keep[k] for k in (
        "xh", "xl", "tab", "ident", "g_dram", "w_raw", "wkv", "wq", "wg"))
    assert B * H == P
    with ExitStack() as ctx:
        def sb(name, shape, dt=F32):
            return ctx.enter_context(nc.sbuf_tensor(name, shape, dt))

        def pb(name, shape):
            return ctx.enter_context(nc.psum_tensor(name, shape, F32))

        def sem(name):
            return ctx.enter_context(nc.semaphore(name))

        xin = sb("n_xin", [P, NT, HID])
        stats = sb("n_stats", [P, NT, 6])
        mv = sb("n_mv", [P, NT, 2])
        var = sb("n_var", [P, NT])
        rstd = sb("n_rstd", [P, NT])
        mhalf = sb("n_mhalf", [P, NT])
        xn = sb("n_xn", [P, 2, HID])
        xt = sb("n_xt", [P, 2, KT, P])
        win = sb("n_win", [P, KT, H])
        hcol = sb("n_hcol", [P, 3])
        ones = sb("n_ones", [P, C])
        pre, ab, ex, u1, ln, df, rc, gg, G, wexp = (sb(f"n_{n}", [P, L]) for n in (
            "pre", "ab", "ex", "u1", "ln", "df", "rc", "gg", "G", "wexp"))
        rows = sb("n_rows", [P, TAB, L])
        pt = [pb(f"n_pt{i}", [P, KT, P]) for i in range(2)]
        pdt = pb("n_pdt", [P, L])
        ptab = [pb(f"n_ptab{k}", [P, NC, P]) for k in range(TAB)]

        x_in = [sem(f"n_x_in{b}") for b in range(B)]
        small_in = sem("n_small_in")
        kv_in, q_in, g_in = sem("n_kv_in"), sem("n_q_in"), sem("n_g_in")
        w_hi, w_lo = sem("n_w_hi"), sem("n_w_lo")
        const_set, acol_set = sem("n_const_set"), sem("n_acol_set")
        stats_set, mv_set, var_set, rstd_set, xn_set = (sem(f"n_{n}_set") for n in ("stats", "mv", "var", "rstd", "xn"))
        xt_done, xt_saved, lo_set, dt_done = sem("n_xt_done"), sem("n_xt_saved"), sem("n_lo_set"), sem("n_dt_done")
        pre_set, ex_set, u1_set, df_set, rc_set, ln_set, log_set = (sem(f"n_{n}_set") for n in (
            "pre", "ex", "u1", "df", "rc", "ln", "log"))
        gg_set, G_set, wexp_set = sem("n_gg_set"), sem("n_G_set"), sem("n_wexp_set")
        row_set = [sem(f"n_row_set{k}") for k in range(TAB)]
        tabs_done, tabs_saved, g_out = sem("n_tabs_done"), sem("n_tabs_saved"), sem("n_g_out")
        block = ctx.enter_context(nc.Block())

        @block.sync
        def _(sp):
            def load_x(b):
                sp.dma_start(xin[:, b * NC:(b + 1) * NC, :],
                             io["x"][b * L:(b + 1) * L, :].rearrange("(c p) n -> p c n", p=P)).then_inc(x_in[b], 16)

            load_x(0)
            sp.dma_start(win[:, :, :], io["win_t"].rearrange("(k p) h -> p k h", p=P)).then_inc(small_in, 16)
            load_x(1)
            for b in range(B):
                at = slice(b * H, (b + 1) * H)
                sp.dma_start(hcol[at, 0:1], io["dt_bias"].rearrange("(h a) -> h a", a=1)).then_inc(small_in, 16)
                sp.dma_start(hcol[at, 1:2], io["A_log_bias"].rearrange("(h a) -> h a", a=1)).then_inc(small_in, 16)
            load_x(2)
            load_x(3)
            sp.dma_start(part(w_raw, 0), kv_piece(io, 0)).then_inc(kv_in, 16)
            for i in (1, 2):
                sp.dma_start(part(w_raw, i), half_piece(io["wq_t"], 0, i)).then_inc(q_in, 16)
            sp.wait_ge(w_lo, 3)
            for i in (1, 2):
                sp.dma_start(part(w_raw, i), half_piece(io["wg_t"], 0, i)).then_inc(g_in, 16)
            sp.wait_ge(G_set, 1)
            for b in range(B):
                for g in range(KVH):
                    h0 = b * H + g * HG
                    sp.dma_start(g_dram[g, b].rearrange("c h t -> h c t"),
                                 G[h0:h0 + HG, :].rearrange("h (c t) -> h c t", t=C)).then_inc(g_out, 16)
            sp.wait_ge(g_out, 16 * B * KVH)

        @block.gpsimd
        def _(pool):
            pool.memset(ident[:, :], 0.0).then_inc(const_set, 1)
            pool.memset(mhalf[:, :], -0.5).then_inc(const_set, 1)
            pool.memset(ones[:, :], 1.0).then_inc(const_set, 1)
            pool.wait_ge(const_set, 3)
            pool.affine_select(out=ident[:, :], in_=ident[:, :], compare_op=ALU.not_equal, fill=1.0,
                               base=0, pattern=[[-1, P]], channel_multiplier=1).then_inc(const_set, 1)
            for b in range(B):
                c0, c1 = b * NC, (b + 1) * NC
                pool.wait_ge(mv_set, c1)
                pool.tensor_scalar(var[:, c0:c1], mv[:, c0:c1, 1], EPS, None, ALU.add).then_inc(var_set, 1)
                pool.wait_ge(var_set, b + 1)
                pool.tensor_tensor(rstd[:, c0:c1], var[:, c0:c1], mhalf[:, c0:c1], ALU.pow).then_inc(rstd_set, 1)
            for j, (w, i) in enumerate(((wkv, 0), (wq, 1), (wq, 2), (wg, 1), (wg, 2))):
                pool.wait_ge(w_hi, j + 1)
                pool.tensor_tensor(dst(w[1], i), part(w_raw, i), dst(w[0], i).bitcast(F32), ALU.subtract).then_inc(w_lo, 1)

        @block.vector
        def _(dve):
            def statistics(b):
                dve.wait_ge(x_in[b], 16)
                for i in range(b * NC, (b + 1) * NC):
                    dve.bn_stats(stats[:, i, :], xin[:, i, :]).then_inc(stats_set, 1)
                for i in range(b * NC, (b + 1) * NC):
                    dve.wait_ge(stats_set, i + 1)
                    dve.bn_aggr(mv[:, i, :], stats[:, i, :]).then_inc(mv_set, 1)

            def normalise(i):
                if i % NC == 0:
                    dve.wait_ge(rstd_set, i // NC + 1)
                if i >= 2:
                    dve.wait_ge(xt_done, i - 1)
                dve.tensor_scalar(xn[:, i % 2, :], xin[:, i, :], mv[:, i, 0:1], rstd[:, i:i + 1],
                                  ALU.subtract, ALU.mult).then_inc(xn_set, 1)

            def low_part(i):
                dve.wait_ge(xt_saved, i + 1)
                dve.tensor_tensor(xl[:, :, i * P:(i + 1) * P], pt[i % 2][:, :, :],
                                  xh[:, :, i * P:(i + 1) * P].bitcast(F32), ALU.subtract).then_inc(lo_set, 1)

            dve.wait_ge(const_set, 3)
            statistics(0)
            for b in range(B):
                if b + 1 < B:
                    statistics(b + 1)
                for i in range(b * NC, (b + 1) * NC):
                    normalise(i)
                    if i:
                        low_part(i - 1)
            low_part(NT - 1)
            dve.wait_ge(ex_set, 1)
            dve.tensor_scalar(u1[:, :], ex[:, :], 1.0, None, ALU.add).then_inc(u1_set, 1)
            dve.wait_ge(u1_set, 1)
            dve.scalar_tensor_tensor(df[:, :], u1[:, :], -1.0, ex[:, :], ALU.add, ALU.subtract).then_inc(df_set, 1)
            dve.reciprocal(rc[:, :], u1[:, :]).then_inc(rc_set, 1)
            dve.wait_ge(df_set, 1)
            dve.wait_ge(rc_set, 1)
            dve.tensor_tensor(df[:, :], df[:, :], rc[:, :], ALU.mult).then_inc(df_set, 1)
            dve.wait_ge(df_set, 2)
            dve.wait_ge(log_set, 1)
            dve.tensor_tensor(ln[:, :], ln[:, :], df[:, :], ALU.subtract).then_inc(ln_set, 1)
            dve.wait_ge(ln_set, 1)
            dve.scalar_tensor_tensor(rows[:, T_DT, :], pre[:, :], 0.0, ln[:, :], ALU.max, ALU.add).then_inc(row_set[T_DT], 1)
            dve.wait_ge(row_set[T_DT], 1)
            dve.wait_ge(acol_set, 1)
            dve.tensor_scalar(gg[:, :], rows[:, T_DT, :], hcol[:, 2:3], -1.0, ALU.mult, ALU.mult).then_inc(gg_set, 1)
            dve.wait_ge(gg_set, 1)
            for c in range(NC):
                at = slice(c * C, (c + 1) * C)
                scan = dve.tensor_tensor_scan(G[:, at], ones[:, :], gg[:, at], 0.0, ALU.mult, ALU.add)
            scan.then_inc(G_set, 1)
            dve.wait_ge(G_set, 1)
            dve.tensor_scalar(rows[:, T_NEGG, :], G[:, :], -1.0, None, ALU.mult).then_inc(row_set[T_NEGG], 1)
            dve.wait_ge(wexp_set, 1)
            dve.tensor_tensor(rows[:, T_W, :], rows[:, T_DT, :], wexp[:, :], ALU.mult).then_inc(row_set[T_W], 1)

        @block.scalar
        def _(act):
            def halves(i):
                act.wait_ge(xt_done, i + 1)
                act.activation(xh[:, :, i * P:(i + 1) * P], pt[i % 2][:, :, :], ACT.Copy)
                if i >= 2:
                    act.wait_ge(dt_done, i - 1)
                act.activation(xt[:, i % 2, :, :], pt[i % 2][:, :, :], ACT.Copy).then_inc(xt_saved, 1)

            def w_high(w, i, loaded, count):
                act.wait_ge(loaded, count)
                act.activation(dst(w[0], i), part(w_raw, i), ACT.Copy).then_inc(w_hi, 1)

            act.wait_ge(small_in, 16 * (1 + 2 * B))
            act.activation(hcol[:, 2:3], hcol[:, 1:2], ACT.Exp).then_inc(acol_set, 1)
            for i in range(NT):
                halves(i)
                if i == NT - NC - 1:
                    w_high(wkv, 0, kv_in, 16)
                if i == NT - NC + 1:
                    w_high(wq, 1, q_in, 32)
                if i == NT - NC + 2:
                    w_high(wq, 2, q_in, 32)
            act.wait_ge(dt_done, NT)
            act.activation(ab[:, :], pdt[:, :], ACT.Abs, bias=hcol[:, 0:1]).then_inc(pre_set, 1)
            act.wait_ge(pre_set, 1)
            act.activation(ex[:, :], ab[:, :], ACT.Exp, scale=-1.0).then_inc(ex_set, 1)
            act.activation(pre[:, :], pdt[:, :], ACT.Identity, bias=hcol[:, 0:1]).then_inc(pre_set, 1)
            act.wait_ge(u1_set, 1)
            act.activation(ln[:, :], u1[:, :], ACT.Ln).then_inc(log_set, 1)
            w_high(wg, 1, g_in, 32)
            w_high(wg, 2, g_in, 32)
            act.wait_ge(G_set, 1)
            for c in range(NC):
                at = slice(c * C, (c + 1) * C)
                w = act.activation(wexp[:, at], G[:, at], ACT.Exp, scale=-1.0, bias=G[:, (c + 1) * C - 1:(c + 1) * C])
            w.then_inc(wexp_set, 1)
            act.activation(rows[:, T_EXPG, :], G[:, :], ACT.Exp).then_inc(row_set[T_EXPG], 1)
            for j, k in enumerate((T_DT, T_NEGG, T_EXPG, T_W)):
                act.wait_ge(tabs_done, j + 1)
                act.activation(tab[:, :, k, :], ptab[k][:, :, :], ACT.Copy).then_inc(tabs_saved, 1)

        @block.tensor
        def _(pe):
            pe.wait_ge(const_set, 4)
            pe.wait_ge(small_in, 16 * (1 + 2 * B))

            def turn(i):
                pe.wait_ge(xn_set, i + 1)
                if i >= 2:
                    pe.wait_ge(lo_set, i - 1)
                for k in range(KT):
                    t = pe.transpose(pt[i % 2][:, k, :], xn[:, i % 2, k * P:(k + 1) * P], ident[:, :])
                t.then_inc(xt_done, 1)

            def dt_rows(i):
                b, c = i // NC, i % NC
                pe.wait_ge(xt_saved, i + 1)
                for k in range(KT):
                    m = pe.matmul(pdt[b * H:(b + 1) * H, c * P:(c + 1) * P], win[:, k, :], xt[:, i % 2, k, :],
                                  start=(k == 0), stop=(k == KT - 1))
                m.then_inc(dt_done, 1)

            for i in range(NT):
                turn(i)
                if i:
                    dt_rows(i - 1)
            dt_rows(NT - 1)
            for k in (T_DT, T_NEGG, T_EXPG, T_W):
                pe.wait_ge(row_set[k], 1)
                for c in range(NC):
                    t = pe.transpose(ptab[k][:, c, :], rows[:, k, c * C:(c + 1) * C], ident[:, :])
                t.then_inc(tabs_done, 1)


def attention_stage(nc, io, keep):
    xh, xl, tab, ident, g_dram, z_dram = (keep[k] for k in ("xh", "xl", "tab", "ident", "g_dram", "z_dram"))
    with ExitStack() as ctx:
        def sb(name, shape, dt=F32):
            return ctx.enter_context(nc.sbuf_tensor(name, shape, dt))

        def pb(name):
            return ctx.enter_context(nc.psum_tensor(name, [P, HG, P], F32))

        def sem(name):
            return ctx.enter_context(nc.semaphore(name))

        w_raw, wkv, wq, wg = (keep[k] for k in ("w_raw", "wkv", "wq", "wg"))
        cos = sb("cos", [P, L])
        sin = sb("sin", [P, L])
        rope_a = sb("rope_a", [P, 2, L])
        rope_b = sb("rope_b", [P, 2, L])
        q = sb("q", [P, 2, HG, L])
        k = sb("k", [P, 2, L])
        v_t = sb("v_t", [P, L])
        k_tok = sb("k_tok", [P, NC, D])
        v_tok = sb("v_tok", [P, NC, D])
        stab = sb("stab", [P, 2, NC, TAB, HG])
        xc = sb("xc", [P, 2, HG, D])
        xw = sb("xw", [P, 2, HG, D])
        g_row = sb("g_row", [P, 2, HG, C])
        decay = sb("decay", [P, 2, HG, C])
        chunk_decay = sb("chunk_decay", [P, NC, HG])
        probs = sb("probs", [P, HG, C])
        state = sb("state", [P, 2, HG, D])
        tanh = sb("tanh", [P, GW])
        gate = sb("gate", [P, 2, GW])
        y_int = sb("y_int", [P, HG, D])
        y = sb("y", [P, HG, D])
        square = sb("square", [P, HG, D])
        ssum = sb("ssum", [P, NC, HG])
        svar = sb("svar", [P, NC, HG])
        srstd = sb("srstd", [P, NC, HG])
        mhalf = sb("mhalf", [P, HG])
        eps4 = sb("eps4", [P, HG])
        before = sb("before", [P, C])
        z = sb("z", [P, HG, D])
        z_t = sb("z_t", [P, 2, HG, C])

        p_proj = [pb(f"p_proj{i}") for i in range(2)]
        p_score, p_inter, p_intra, p_cst, p_zt, p_tok = (pb(n) for n in (
            "p_score", "p_inter", "p_intra", "p_cst", "p_zt", "p_tok"))

        w_in = [sem(f"w_in{i}") for i in range(3)]
        tab_in = sem("tab_in")
        g_in = [sem(f"g_in{i}") for i in range(2)]
        z_out = [sem(f"z_out{i}") for i in range(2)]
        unit_done, unit_free = sem("unit_done"), sem("unit_free")
        score_done, intra_done, inter_done = sem("score_done"), sem("intra_done"), sem("inter_done")
        cst_done, zt_done, tok_done = sem("cst_done"), sem("zt_done"), sem("tok_done")
        probs_set, state_set, y_set, z_set = sem("probs_set"), sem("state_set"), sem("y_set"), sem("z_set")
        gate_set, rope_terms, v_set = sem("gate_set"), sem("rope_terms"), sem("v_set")
        kv_split, q_split, g_split = sem("kv_split"), sem("q_split"), sem("g_split")
        kv_hi, q_hi, g_hi = sem("kv_hi"), sem("q_hi"), sem("g_hi")
        decay_set, tanh_set, yint_set = sem("decay_set"), sem("tanh_set"), sem("yint_set")
        squares_set, zt_saved, tok_saved = sem("squares_set"), sem("zt_saved"), sem("tok_saved")
        masked_set, roped, xc_set, xw_set = sem("masked_set"), sem("roped"), sem("xc_set"), sem("xw_set")
        mask_set = sem("mask_set")
        svar_set, srstd_set, stab_set, const_set = sem("svar_set"), sem("srstd_set"), sem("stab_set"), sem("const_set")
        block = ctx.enter_context(nc.Block())

        GATE_UNIT, K_UNIT, V_UNIT, Q_UNIT = (0, 3, 5, 7), 1, 2, (4, 6, 8, 9)

        def unit(n, at):
            if isinstance(n, int) and n == B * KVH - 1:
                at = GATE_UNIT.index(at)
            return UNITS * n + (FIRST_UNITS + at)

        def bank(n, b, at):
            if isinstance(n, int):
                return p_proj[unit(n, at) % 2]
            return p_proj[(FIRST_UNITS + UNITS * b + at) % 2]

        def steps(engine, first, step):
            def group(g):
                for b in range(B):
                    step(g, b, B * g + b)

            first()
            group(0)
            with engine.Fori(1, KVH - 1) as g:
                group(g)
            group(KVH - 1)

        def ahead(n):
            return not (isinstance(n, int) and n == B * KVH - 1)

        def has_last(n):
            return not (isinstance(n, int) and n == 0)

        def more(n, c, by):
            return not (isinstance(n, int) and NC * n + c + by >= NC * B * KVH)

        def group_ahead(g):
            return not (isinstance(g, int) and g == KVH - 1)

        @block.sync
        def _(sp):
            def load_kv(g):
                sp.dma_start(part(w_raw, 0), kv_piece(io, g)).then_inc(w_in[0], 16)

            def load_half(w, g, i):
                sp.dma_start(part(w_raw, i), half_piece(io[w], g, i)).then_inc(w_in[i], 16)

            def load_g(g, b, c):
                src = g_dram[bass.ds(g, 1), b, c].rearrange("a h t -> a (h t)").to_broadcast([P, HG * C])
                sp.dma_start(g_row[:, c % 2].rearrange("p h t -> p (h t)"), src).then_inc(g_in[c % 2], 16)

            def first():
                sp.dma_start(cos[:, :], io["cos_t"]).then_inc(tab_in, 16)
                sp.dma_start(sin[:, :], io["sin_t"]).then_inc(tab_in, 16)
                load_g(0, 0, 0)
                load_g(0, 0, 1)

            def step(g, b, n):
                for c in range(NC):
                    m = NC * n + c
                    if more(n, c, 2):
                        sp.wait_ge(decay_set, m + 1)
                        nb, ncc = b + (c + 2) // NC, (c + 2) % NC
                        load_g(g + nb // B, nb % B, ncc)
                    if c > 0:
                        store_z(g, b, n, c - 1)
                    elif has_last(n):
                        store_z(g if b else g - 1, (b - 1) % B, n - 1, NC - 1)
                    if group_ahead(g):
                        if b == 0 and c == 1:
                            wait_ge(sp, kv_split, g)
                            load_kv(g + 1)
                        if b == 0 and c == 2:
                            wait_ge(sp, g_split, 2 * g)
                            load_half("wq_t", g + 1, 1)
                            load_half("wq_t", g + 1, 2)
                        if b == B - 1 and c == 2:
                            sp.wait_ge(q_split, g + 1)
                            load_half("wg_t", g + 1, 1)
                            load_half("wg_t", g + 1, 2)

            def store_z(g, b, n, c):
                sp.wait_ge(zt_saved, NC * n + c + 1)
                sp.dma_start(z_dram[b * NC + c, :, bass.ds(g * HG, HG), :], z_t[:, c % 2]).then_inc(z_out[c % 2], 16)

            steps(sp, first, step)
            store_z(KVH - 1, B - 1, B * KVH - 1, NC - 1)
            for s in range(2):
                sp.wait_ge(z_out[s], 16 * B * KVH * NC // 2)

        @block.tensor
        def _(pe):
            def wide(out, pairs):
                for i, (lhs, rhs) in enumerate(pairs):
                    for j, (a, e) in enumerate(((0, 0), (1, 0), (0, 1))):
                        mm = pe.matmul(out, lhs[a], rhs[e], start=(i == 0 and j == 0),
                                       stop=(i == len(pairs) - 1 and j == 2))
                return mm

            def project(w, w0, b, u, into):
                t = slice(b * L, (b + 1) * L)
                wide(into[:, :, :].rearrange("p h t -> p (h t)"),
                     [((w[0][:, kt, w0:w0 + D], w[1][:, kt, w0:w0 + D]), (xh[:, kt, t], xl[:, kt, t]))
                      for kt in range(KT)]).then_inc(unit_done, 1)

            def gates(g, b, n, c):
                u = unit(n, GATE_UNIT[c])
                wait_ge(pe, unit_free, u - 1)
                if b == 0 and c == 0:
                    wait_ge(pe, g_split, 2 * g)
                t = slice(b * L + c * C, b * L + (c + 1) * C)
                wide(bank(n, b, GATE_UNIT[c])[:, :, :].rearrange("p h t -> p (h t)"),
                     [((xh[:, kt, t], xl[:, kt, t]), (wg[0][:, kt, :], wg[1][:, kt, :]))
                      for kt in range(KT)]).then_inc(unit_done, 1)

            def next_unit(g, b, n, at):
                if not ahead(n):
                    return
                u = unit(n, at)
                wait_ge(pe, unit_free, u - 1)
                if b == B - 1 and at == K_UNIT:
                    pe.wait_ge(kv_split, g + 1)
                if b == B - 1 and at == Q_UNIT[0]:
                    pe.wait_ge(q_split, g + 1)
                w, w0 = (wkv, 0) if at == K_UNIT else (wkv, D) if at == V_UNIT else (wq, Q_UNIT.index(at) * D)
                project(w, w0, (b + 1) % B, u, bank(n, b, at))

            def v_turn(n):
                pe.wait_ge(v_set, n + 1)
                wait_ge(pe, tok_saved, 2 * n)
                for c in range(NC):
                    t = pe.transpose(p_tok[:, c, :], v_t[:, c * C:(c + 1) * C], ident[:, :])
                t.then_inc(tok_done, 1)

            def k_turn(n, b):
                pe.wait_ge(roped, ROPED * n + 1)
                pe.wait_ge(tok_saved, 2 * n + 1)
                for c in range(NC - 1):
                    t = pe.transpose(p_tok[:, c, :], k[:, b % 2, c * C:(c + 1) * C], ident[:, :])
                t.then_inc(tok_done, 1)

            def scores(n, b, c):
                if c == 0:
                    pe.wait_ge(roped, ROPED * (n + 1))
                wait_ge(pe, probs_set, NC * n + c)
                pe.matmul(p_score[:, :, :], k[:, b % 2, c * C:(c + 1) * C], q[:, b % 2, :, c * C:(c + 1) * C],
                          start=True, stop=True).then_inc(score_done, 1)

            def chunk_state(n, c):
                pe.wait_ge(xw_set, 3 * n + c + 1)
                if c == 0:
                    pe.wait_ge(tok_saved, 2 * n + 2)
                wait_ge(pe, state_set, 3 * n + c)
                pe.matmul(p_cst[:, :, :], k_tok[:, c, :], xw[:, c % 2, :, :], start=True, stop=True).then_inc(cst_done, 1)

            def inter(n, b, c):
                wait_ge(pe, state_set, 3 * n + c)
                wait_ge(pe, yint_set, 3 * n + c - 1)
                for h in range(HG):
                    mm = pe.matmul(p_inter[:, h, :], q[:, b % 2, h, c * C:(c + 1) * C], state[:, c % 2, h, :],
                                   start=True, stop=True)
                mm.then_inc(inter_done, 1)

            def intra(n, c):
                m = NC * n + c
                pe.wait_ge(probs_set, m + 1)
                pe.wait_ge(xc_set, m + 1)
                wait_ge(pe, y_set, m)
                for h in range(HG):
                    mm = pe.matmul(p_intra[:, h, :], probs[:, h, :], xc[:, c % 2, h, :], start=True, stop=True)
                mm.then_inc(intra_done, 1)

            def z_turn(n, c):
                m = NC * n + c
                pe.wait_ge(z_set, m + 1)
                wait_ge(pe, zt_saved, m)
                for h in range(HG):
                    t = pe.transpose(p_zt[:, h, :], z[:, h, :], ident[:, :])
                t.then_inc(zt_done, 1)

            def first():
                project(wkv, 0, 0, 0, p_proj[0])
                project(wkv, D, 0, 1, p_proj[1])
                for h in range(HG):
                    pe.wait_ge(unit_free, h + 1)
                    project(wq, h * D, 0, 2 + h, p_proj[h % 2])
                v_turn(0)
                k_turn(0, 0)

            def step(g, b, n):
                gates(g, b, n, 0)
                if has_last(n):
                    z_turn(n - 1, 3)
                next_unit(g, b, n, K_UNIT)
                scores(n, b, 0)
                chunk_state(n, 0)
                next_unit(g, b, n, V_UNIT)
                intra(n, 0)
                for c in (1, 2):
                    scores(n, b, c)
                    gates(g, b, n, c)
                    chunk_state(n, c)
                    inter(n, b, c)
                    next_unit(g, b, n, Q_UNIT[c - 1])
                    intra(n, c)
                    z_turn(n, c - 1)
                scores(n, b, 3)
                if ahead(n):
                    v_turn(n + 1)
                gates(g, b, n, 3)
                if ahead(n):
                    k_turn(n + 1, b + 1)
                inter(n, b, 3)
                intra(n, 3)
                z_turn(n, 2)
                next_unit(g, b, n, Q_UNIT[2])
                next_unit(g, b, n, Q_UNIT[3])

            steps(pe, first, step)
            z_turn(B * KVH - 1, 3)

        @block.vector
        def _(dve):
            def split(w, pieces, hi_sem, done, g):
                for j, i in enumerate(pieces):
                    dve.wait_ge(hi_sem, len(pieces) * g + (j + 1 - len(pieces)))
                    lo = dve.tensor_tensor(dst(w[1], i), part(w_raw, i), dst(w[0], i).bitcast(F32), ALU.subtract)
                lo.then_inc(done, 1)

            def g_low(g, i):
                dve.wait_ge(g_hi, 2 * g - 2 + i)
                dve.tensor_tensor(dst(wg[1], i), part(w_raw, i), dst(wg[0], i).bitcast(F32), ALU.subtract).then_inc(g_split, 1)

            def rotate(bank_, r, n, b):
                s, half = (b + r) % 2, D // 2
                x = bank_[:, :, :].rearrange("p h t -> p (h t)")
                wait_ge(dve, roped, ROPED * n + r - 1)
                dve.tensor_tensor(rope_a[:, s, :], x, cos[:, :], ALU.mult)
                dve.tensor_tensor(rope_b[0:half, s, :], x[half:D, :], sin[0:half, :], ALU.mult)
                dve.tensor_tensor(rope_b[half:D, s, :], x[0:half, :], sin[half:D, :], ALU.mult).then_inc(rope_terms, 1)

            def rotate_next(g, b, n, at, r):
                if not ahead(n):
                    return
                u = unit(n, at)
                dve.wait_ge(unit_done, u + 1)
                rotate(bank(n, b, at), r, n + 1, b + 1)
                dve.wait_ge(rope_terms, ROPED * (n + 1) + r + 1)
                dve.sem_inc(unit_free, 1)

            def first():
                dve.memset(mhalf[:, :], -0.5).then_inc(const_set, 1)
                dve.memset(eps4[:, :], 4.0 * EPS).then_inc(const_set, 1)
                dve.wait_ge(tab_in, 32)
                for j in range(FIRST_UNITS):
                    dve.wait_ge(unit_done, j + 1)
                    if j == 1:
                        dve.tensor_copy(v_t[:, :], p_proj[1][:, :, :].rearrange("p h t -> p (h t)")).then_inc(v_set, 1)
                        dve.wait_ge(v_set, 1)
                    else:
                        r = 0 if j == 0 else j - 1
                        rotate(p_proj[j % 2], r, 0, 0)
                        dve.wait_ge(rope_terms, r + 1)
                    dve.sem_inc(unit_free, 1)

            def make_gate(g, b, n, c):
                m, u = NC * n + c, unit(n, GATE_UNIT[c])
                dve.wait_ge(tanh_set, m + 1)
                dve.scalar_tensor_tensor(gate[:, c % 2, :], tanh[:, :], 1.0,
                                         bank(n, b, GATE_UNIT[c])[:, :, :].rearrange("p h t -> p (h t)"),
                                         ALU.add, ALU.mult).then_inc(unit_free, 1)

            def make_probs(n, c):
                m = NC * n + c
                dve.wait_ge(score_done, m + 1)
                dve.wait_ge(decay_set, m + 1)
                dve.tensor_tensor(probs[:, :, :], p_score[:, :, :], decay[:, c % 2, :, :], ALU.mult).then_inc(probs_set, 1)

            def make_state(n, c):
                dve.wait_ge(cst_done, 3 * n + c + 1)
                if c == 0:
                    s = dve.tensor_copy(state[:, 1, :, :], p_cst[:, :, :])
                else:
                    for h in range(HG):
                        s = dve.scalar_tensor_tensor(state[:, (c + 1) % 2, h, :], state[:, c % 2, h, :],
                                                     chunk_decay[:, c, h:h + 1], p_cst[:, h, :], ALU.mult, ALU.add)
                s.then_inc(state_set, 1)

            def make_y(n, c):
                m = NC * n + c
                dve.wait_ge(intra_done, m + 1)
                if c == 0:
                    dve.tensor_copy(y[:, :, :], p_intra[:, :, :]).then_inc(y_set, 1)
                else:
                    wait_ge(dve, yint_set, 3 * n + c)
                    dve.tensor_tensor(y[:, :, :], p_intra[:, :, :], y_int[:, :, :], ALU.add).then_inc(y_set, 1)

            def make_z(n, c):
                m = NC * n + c
                dve.wait_ge(srstd_set, m + 1)
                wait_ge(dve, zt_done, m)
                for h in range(HG):
                    zz = dve.scalar_tensor_tensor(z[:, h, :], y[:, h, :], srstd[:, c, h:h + 1],
                                                  gate[:, c % 2, h * D:(h + 1) * D], ALU.mult, ALU.mult)
                zz.then_inc(z_set, 1)

            def step(g, b, n):
                if group_ahead(g) and b == B - 1:
                    split(wq, (1, 2), q_hi, q_split, g + 1)
                make_gate(g, b, n, 0)
                rotate_next(g, b, n, K_UNIT, 0)
                make_probs(n, 0)
                make_state(n, 0)
                if ahead(n):
                    dve.wait_ge(unit_done, unit(n, V_UNIT) + 1)
                    dve.tensor_copy(v_t[:, :], bank(n, b, V_UNIT)[:, :, :].rearrange("p h t -> p (h t)")).then_inc(v_set, 1)
                    dve.wait_ge(v_set, n + 2)
                    dve.sem_inc(unit_free, 1)
                make_y(n, 0)
                make_z(n, 0)
                for c in (1, 2):
                    make_probs(n, c)
                    make_gate(g, b, n, c)
                    make_state(n, c)
                    make_y(n, c)
                    rotate_next(g, b, n, Q_UNIT[c - 1], c)
                    if c == 1 and group_ahead(g) and b == B - 2:
                        split(wkv, (0,), kv_hi, kv_split, g + 1)
                    make_z(n, c)
                make_probs(n, 3)
                make_gate(g, b, n, 3)
                make_y(n, 3)
                if group_ahead(g) and b == B - 1:
                    g_low(g + 1, 1)
                rotate_next(g, b, n, Q_UNIT[2], 3)
                make_z(n, 3)
                if group_ahead(g) and b == B - 1:
                    g_low(g + 1, 2)
                rotate_next(g, b, n, Q_UNIT[3], 4)

            steps(dve, first, step)

        @block.scalar
        def _(act):
            def split(w, pieces, done, g, loads):
                for i in pieces:
                    act.wait_ge(w_in[i], 16 * loads)
                    act.activation(dst(w[0], i), part(w_raw, i), ACT.Copy).then_inc(done, 1)

            def make_decay(n, b, c):
                act.wait_ge(masked_set, NC * n + c + 1)
                if c == 0:
                    act.wait_ge(stab_set, n + 1)
                wait_ge(act, probs_set, NC * n + c - 1)
                act.activation(chunk_decay[:, c, :], g_row[:, c % 2, :, C - 1], ACT.Exp)
                for h in range(HG):
                    e = act.activation(decay[:, c % 2, h, :], g_row[:, c % 2, h, :], ACT.Exp,
                                       bias=stab[:, b % 2, c, T_NEGG, h:h + 1])
                e.then_inc(decay_set, 1)

            def make_tanh(g, b, n, c):
                act.wait_ge(unit_done, unit(n, GATE_UNIT[c]) + 1)
                act.activation(tanh[:, :], bank(n, b, GATE_UNIT[c])[:, :, :].rearrange("p h t -> p (h t)"),
                               ACT.Tanh, scale=0.5).then_inc(tanh_set, 1)

            def scale_inter(n, b, c):
                act.wait_ge(inter_done, 3 * n + c)
                wait_ge(act, y_set, NC * n + c)
                for h in range(HG):
                    s = act.activation(y_int[:, h, :], p_inter[:, h, :], ACT.Copy, scale=stab[:, b % 2, c, T_EXPG, h:h + 1])
                s.then_inc(yint_set, 1)

            def squares(n, c):
                act.wait_ge(y_set, NC * n + c + 1)
                for h in range(HG):
                    s = act.activation(square[:, h, :], y[:, h, :], ACT.Square, scale=2.0 / float(np.sqrt(D)),
                                       accum_out=ssum[:, c, h:h + 1])
                s.then_inc(squares_set, 1)

            def save_z(n, c):
                m = NC * n + c
                act.wait_ge(zt_done, m + 1)
                wait_ge(act, z_out[c % 2], 16 * (2 * n + c // 2))
                act.activation(z_t[:, c % 2, :, :], p_zt[:, :, :], ACT.Copy).then_inc(zt_saved, 1)

            def save_v(n):
                act.wait_ge(tok_done, 2 * n + 1)
                wait_ge(act, xc_set, NC * n)
                wait_ge(act, xw_set, 3 * n)
                act.activation(v_tok[:, :, :], p_tok[:, :, :], ACT.Copy).then_inc(tok_saved, 1)

            def save_k(n):
                act.wait_ge(tok_done, 2 * n + 2)
                act.activation(k_tok[:, 0:NC - 1, :], p_tok[:, 0:NC - 1, :], ACT.Copy).then_inc(tok_saved, 1)

            def first():
                make_decay(0, 0, 0)
                save_v(0)
                save_k(0)

            def step(g, b, n):
                if group_ahead(g) and b == B - 1:
                    act.wait_ge(unit_done, UNITS * n + FIRST_UNITS)
                    split(wq, (1, 2), q_hi, g + 1, 2 * g + 1)
                make_tanh(g, b, n, 0)
                if has_last(n):
                    save_z(n - 1, 3)
                make_decay(n, b, 1)
                squares(n, 0)
                for c in (1, 2):
                    make_decay(n, b, c + 1)
                    make_tanh(g, b, n, c)
                    scale_inter(n, b, c)
                    if c == 1 and group_ahead(g) and b == B - 2:
                        act.wait_ge(unit_done, unit(n, V_UNIT) + 1)
                        split(wkv, (0,), kv_hi, g + 1, g + 1)
                    squares(n, c)
                    save_z(n, c - 1)
                if ahead(n):
                    save_v(n + 1)
                make_tanh(g, b, n, 3)
                if ahead(n):
                    save_k(n + 1)
                scale_inter(n, b, 3)
                if group_ahead(g) and b == B - 1:
                    split(wg, (1,), g_hi, g + 1, 2 * g + 2)
                squares(n, 3)
                if group_ahead(g) and b == B - 1:
                    split(wg, (2,), g_hi, g + 1, 2 * g + 2)
                save_z(n, 2)
                if ahead(n):
                    make_decay(n + 1, b + 1, 0)

            steps(act, first, step)
            save_z(B * KVH - 1, 3)

        @block.gpsimd
        def _(pool):
            def step_tables(g, b, n):
                pool.tensor_copy(stab[:, b % 2], tab[:, :, :, bass.ds(g * HG + b * H, HG)]).then_inc(stab_set, 1)

            def mask(n, c):
                pool.wait_ge(g_in[c % 2], 16 * (2 * n + c // 2 + 1))
                pool.tensor_tensor(g_row[:, c % 2], g_row[:, c % 2], before[:, :].unsqueeze(1).to_broadcast([P, HG, C]),
                                   ALU.add).then_inc(masked_set, 1)

            def add_rope(n, b, r):
                s = (b + r) % 2
                pool.wait_ge(rope_terms, ROPED * n + r + 1)
                out = k[:, b % 2, :] if r == 0 else q[:, b % 2, r - 1, :]
                pool.tensor_tensor(out, rope_a[:, s, :], rope_b[:, s, :], ALU.add).then_inc(roped, 1)

            def scaled_v(out, b, c, which):
                v = v_tok[:, c, :].unsqueeze(1).to_broadcast([P, HG, D])
                w = stab[:, b % 2, c, which, :].unsqueeze(2).to_broadcast([P, HG, D])
                return pool.tensor_tensor(out[:, c % 2], v, w, ALU.mult)

            def make_xc(n, b, c):
                if c == 0:
                    pool.wait_ge(tok_saved, 2 * n + 1)
                    pool.wait_ge(stab_set, n + 1)
                wait_ge(pool, intra_done, NC * n + c - 1)
                scaled_v(xc, b, c, T_DT).then_inc(xc_set, 1)

            def make_xw(n, b, c):
                wait_ge(pool, cst_done, 3 * n + (c - 1 if c else 0))
                scaled_v(xw, b, c, T_W).then_inc(xw_set, 1)

            def rms(n, c):
                m = NC * n + c
                pool.wait_ge(squares_set, m + 1)
                pool.tensor_tensor(svar[:, c, :], ssum[:, c, :], eps4[:, :], ALU.add).then_inc(svar_set, 1)
                pool.wait_ge(svar_set, m + 1)
                pool.tensor_tensor(srstd[:, c, :], svar[:, c, :], mhalf[:, :], ALU.pow).then_inc(srstd_set, 1)

            def first():
                pool.memset(before[:, :], 0.0).then_inc(mask_set, 1)
                pool.wait_ge(mask_set, 1)
                pool.affine_select(out=before[:, :], in_=before[:, :], compare_op=ALU.is_ge, fill=-1e30,
                                   base=0, pattern=[[1, C]], channel_multiplier=-1).then_inc(mask_set, 1)
                pool.wait_ge(const_set, 2)
                step_tables(0, 0, 0)
                pool.wait_ge(mask_set, 2)
                mask(0, 0)
                for r in range(ROPED):
                    add_rope(0, 0, r)
                make_xc(0, 0, 0)
                make_xw(0, 0, 0)

            def step(g, b, n):
                mask(n, 1)
                make_xc(n, b, 1)
                make_xw(n, b, 1)
                if ahead(n):
                    wait_ge(pool, yint_set, 3 * n)
                    step_tables(g if b < B - 1 else g + 1, (b + 1) % B, n + 1)
                    add_rope(n + 1, b + 1, 0)
                rms(n, 0)
                mask(n, 2)
                make_xc(n, b, 2)
                make_xw(n, b, 2)
                rms(n, 1)
                if ahead(n):
                    add_rope(n + 1, b + 1, 1)
                mask(n, 3)
                make_xc(n, b, 3)
                rms(n, 2)
                if ahead(n):
                    add_rope(n + 1, b + 1, 2)
                    mask(n + 1, 0)
                    make_xc(n + 1, b + 1, 0)
                    make_xw(n + 1, b + 1, 0)
                rms(n, 3)
                if ahead(n):
                    add_rope(n + 1, b + 1, 3)
                    add_rope(n + 1, b + 1, 4)

            steps(pool, first, step)


def output_stage(nc, io, keep):
    ident, z_dram = keep["ident"], keep["z_dram"]
    HP = 8
    NP = H // HP
    WH = 2
    NW = H // WH
    SLOTS = 4
    SCALE = 1.0 / float(np.sqrt(np.float32(DK)))
    with ExitStack() as ctx:
        def sb(name, shape, dt=F32):
            return ctx.enter_context(nc.sbuf_tensor(name, shape, dt))

        def pb(name, shape=(P, HID)):
            return ctx.enter_context(nc.psum_tensor(name, list(shape), F32))

        def sem(name):
            return ctx.enter_context(nc.semaphore(name))

        raw = [sb(f"raw{i}", [P, HP * P]) for i in range(SLOTS)]
        z_hi = [sb(f"z_hi{i}", [P, HP, P], F32R) for i in range(2)]
        z_lo = [sb(f"z_lo{i}", [P, HP, P], F32R) for i in range(2)]
        wo = [sb(f"wo_{n}", [P, H, HID], F32R) for n in ("hi", "lo")]
        gn = sb("gn", [P, 1])
        ws = sb("ws", [P, KT, HID])
        wqk = sb("wqk", [P, KT, 2 * E * DK])
        wa = sb("wa", [P, KT, E * R])
        bm = sb("bm", [P, HID])
        bias = sb("bias", [P, HID])
        x_res = sb("x_res", [P, 2, HID])
        x1 = sb("x1", [P, HID])
        x1b = sb("x1b", [P, HID])
        xn = sb("xn", [P, HID])
        xt = sb("xt", [P, KT, P])
        stats, mv, var, rstd, mhalf = sb("stats", [P, 6]), sb("mv", [P, 2]), sb("var", [P, 1]), sb("rstd", [P, 1]), sb("mh", [P, 1])
        eps = sb("eps", [P, 1])
        keys = sb("keys", [P, E, DK])
        qk = sb("qk", [P, E, DK])
        sc, ew = sb("sc", [P, E]), sb("ew", [P, E])
        mx, nmx, den, rden = (sb(n, [P, 1]) for n in ("mx", "nmx", "den", "rden"))
        hw, hwn = sb("hw", [P, E, R]), sb("hwn", [P, E * R])
        hwt = sb("hwt", [P, P])
        res = sb("res", [P, 2, HID])

        p_out = [pb(f"p_out{i}") for i in range(2)]
        p_xt, p_qk, p_h, p_hwt, p_f = pb("p_xt", (P, KT, P)), pb("p_qk"), pb("p_h", (P, E * R)), pb("p_hwt", (P, P)), pb("p_f")

        raw_in = [sem(f"raw_in{i}") for i in range(SLOTS)]
        small_in, gn_in = sem("small_in"), sem("gn_in")
        x_in = [sem(f"x_in{i}") for i in range(2)]
        out_sent = [sem(f"out_sent{i}") for i in range(2)]
        hi_set, lo_set, out_done, heads_done = sem("hi_set"), sem("lo_set"), sem("out_done"), sem("heads_done")
        x1_set, x1b_set, stats_set, mv_set, var_set, rstd_set, xn_set = (sem(s) for s in (
            "x1_set", "x1b_set", "stats_set", "mv_set", "var_set", "rstd_set", "xn_set"))
        xt_done, xt_saved, qk_done, keys_saved, prod_set, sc_set, mx_set, nmx_set, ew_set = (sem(s) for s in (
            "xt_done", "xt_saved", "qk_done", "keys_saved", "prod_set", "sc_set", "mx_set", "nmx_set", "ew_set"))
        rden_set, hw_set, hwn_set, hwt_done, hwt_saved, f_done, res_set, c_set = (sem(s) for s in (
            "rden_set", "hw_set", "hwn_set", "hwt_done", "hwt_saved", "f_done", "res_set", "c_set"))
        block = ctx.enter_context(nc.Block())

        def tiles(engine, first, step):
            first()
            step(0, 0, True)
            step(1, 1, True)
            with engine.Fori(1, NT // 2 - 1) as pair:
                step(2 * pair, 0, True)
                step(2 * pair + 1, 1, True)
            step(NT - 2, 0, True)
            step(NT - 1, 1, False)

        def ahead(i):
            more = not isinstance(i, int) or i + 2 < NT
            return [(i + 1, j) for j in range(1, NP)] + [(i + 2, 0)] * more

        @block.sync
        def _(sp):
            def load_z(i, j):
                sp.dma_start(raw[j % SLOTS][:, :], z_dram[bass.ds(i, 1), :, j * HP:(j + 1) * HP, :].rearrange(
                    "a p h t -> p (a h t)")).then_inc(raw_in[j % SLOTS], 16)

            def load_x(i, s):
                sp.dma_start(x_res[:, s, :], io["x"][bass.ds(i * P, P), :]).then_inc(x_in[s], 16)

            def first():
                sp.dma_start(gn[:, :], io["gnorm_w"].rearrange("(p a) -> p a", a=1)).then_inc(gn_in, 16)
                for w in range(NW):
                    if w >= SLOTS:
                        sp.wait_ge(lo_set, w - SLOTS + 1)
                    sp.dma_start(raw[w % SLOTS][:, :].rearrange("p (h n) -> p h n", h=WH),
                                 io["wo_t"][w * WH * P:(w + 1) * WH * P, :].rearrange("(h p) n -> p h n", p=P)).then_inc(raw_in[w % SLOTS], 16)
                    if w == SLOTS - 1:
                        load_x(0, 0)
                        sp.dma_start(bias[:, :], io["b"].rearrange("(a n) -> a n", a=1).to_broadcast([P, HID])).then_inc(small_in, 16)
                        sp.dma_start(wqk[:, :, :], io["wqk_t"].rearrange("(k p) n -> p k n", p=P)).then_inc(small_in, 16)
                        sp.dma_start(wa[:, :, :], io["a_t"].rearrange("(k p) n -> p k n", p=P)).then_inc(small_in, 16)
                        sp.dma_start(ws[:, :, :], io["w_t"].rearrange("(k p) n -> p k n", p=P)).then_inc(small_in, 16)
                        sp.dma_start(bm[:, :], io["bm_t"]).then_inc(small_in, 16)
                for j in range(NP):
                    sp.wait_ge(lo_set, NW - SLOTS + j + 1)
                    load_z(0, j)
                sp.wait_ge(lo_set, NW + 1)
                load_z(1, 0)

            def step(i, s, has_next):
                if has_next:
                    for ii, j in ahead(i):
                        wait_ge(sp, lo_set, NW + NP * (ii - 1) + j + 1)
                        load_z(ii, j)
                if not isinstance(i, int) or i > 0:
                    store(i - 1, 1 - s)
                if has_next:
                    wait_ge(sp, x1_set, i)
                    load_x(i + 1, 1 - s)

            def store(i, s):
                sp.wait_ge(res_set, i + 1)
                sp.dma_start(io["out"][bass.ds(i * P, P), :], res[:, s, :]).then_inc(out_sent[s], 16)

            tiles(sp, first, step)
            store(NT - 1, 1)
            for s in range(2):
                sp.wait_ge(out_sent[s], 16 * NT // 2)

        @block.tensor
        def _(pe):
            def wo_piece(i, s, j):
                pe.wait_ge(lo_set, NW + NP * i + j + 1)
                if j == 0:
                    wait_ge(pe, x1_set, i - 1)
                for h in range(HP):
                    hh = j * HP + h
                    for t, (a, e) in enumerate(((z_hi, 0), (z_lo, 0), (z_hi, 1))):
                        mm = pe.matmul(p_out[s][:, :], a[j % 2][:, h, :], wo[e][:, hh, :],
                                       start=(hh == 0 and t == 0), stop=(hh == H - 1 and t == 2))
                mm.then_inc(heads_done, 1)

            def turn_x(i):
                pe.wait_ge(xn_set, i + 1)
                wait_ge(pe, xt_saved, i)
                for kt in range(KT):
                    t = pe.transpose(p_xt[:, kt, :], xn[:, kt * P:(kt + 1) * P], ident[:, :])
                t.then_inc(xt_done, 1)

            def experts(i):
                pe.wait_ge(xt_saved, i + 1)
                wait_ge(pe, prod_set, i)
                for kt in range(KT):
                    mm = pe.matmul(p_qk[:, :], xt[:, kt, :], wqk[:, kt, :], start=(kt == 0), stop=(kt == KT - 1))
                mm.then_inc(qk_done, 1)
                wait_ge(pe, hw_set, i)
                for kt in range(KT):
                    mm = pe.matmul(p_h[:, :], xt[:, kt, :], wa[:, kt, :], start=(kt == 0), stop=(kt == KT - 1))
                mm.then_inc(qk_done, 1)

            def dense(i):
                wait_ge(pe, res_set, i)
                for kt in range(KT):
                    pe.matmul(p_f[:, :], xt[:, kt, :], ws[:, kt, :], start=(kt == 0), stop=False)

            def turn_hw(i):
                pe.wait_ge(hwn_set, i + 1)
                wait_ge(pe, hwt_saved, i)
                pe.transpose(p_hwt[:, :], hwn[:, :], ident[:, :]).then_inc(hwt_done, 1)

            def combine(i):
                pe.wait_ge(hwt_saved, i + 1)
                pe.matmul(p_f[:, :], hwt[:, :], bm[:, :], start=False, stop=True).then_inc(f_done, 1)

            def first():
                for j in range(NP):
                    wo_piece(0, 0, j)
                pe.wait_ge(small_in, 80)

            def step(i, s, has_next):
                if has_next:
                    wo_piece(i + 1, 1 - s, 0)
                turn_x(i)
                if has_next:
                    wo_piece(i + 1, 1 - s, 1)
                experts(i)
                dense(i)
                if has_next:
                    wo_piece(i + 1, 1 - s, 2)
                turn_hw(i)
                if has_next:
                    wo_piece(i + 1, 1 - s, 3)
                combine(i)

            tiles(pe, first, step)

        @block.vector
        def _(dve):
            def wo_low(w):
                at = slice(w * WH, (w + 1) * WH)
                dve.wait_ge(hi_set, w + 1)
                dve.scalar_tensor_tensor(wo[1][:, at, :], raw[w % SLOTS][:, :].rearrange("p (h n) -> p h n", h=WH), gn[:, 0:1],
                                         wo[0][:, at, :].bitcast(F32), ALU.mult, ALU.subtract).then_inc(lo_set, 1)

            def z_low(i, j):
                dve.wait_ge(hi_set, NW + NP * i + j + 1)
                dve.tensor_tensor(z_lo[j % 2][:, :, :], raw[j % SLOTS][:, :].rearrange("p (h t) -> p h t", h=HP),
                                  z_hi[j % 2][:, :, :].bitcast(F32), ALU.subtract).then_inc(lo_set, 1)

            def first():
                dve.memset(mhalf[:, :], -0.5).then_inc(c_set, 1)
                dve.memset(eps[:, :], EPS).then_inc(c_set, 1)
                dve.wait_ge(gn_in, 16)
                for w in range(NW):
                    wo_low(w)
                for j in range(NP):
                    z_low(0, j)
                z_low(1, 0)

            def step(i, s, has_next):
                dve.wait_ge(heads_done, NP * (i + 1))
                dve.wait_ge(x_in[s], 8 * (i - s) + 16)
                wait_ge(dve, x1b_set, i)
                dve.tensor_tensor(x1[:, :], p_out[s][:, :], x_res[:, s, :], ALU.add).then_inc(x1_set, 1)
                dve.wait_ge(x1_set, i + 1)
                dve.bn_stats(stats[:, :], x1[:, :]).then_inc(stats_set, 1)
                dve.wait_ge(c_set, 2)
                dve.wait_ge(stats_set, i + 1)
                dve.bn_aggr(mv[:, :], stats[:, :]).then_inc(mv_set, 1)
                dve.wait_ge(rstd_set, i + 1)
                wait_ge(dve, xt_done, i)
                dve.tensor_scalar(xn[:, :], x1[:, :], mv[:, 0:1], rstd[:, 0:1], ALU.subtract, ALU.mult).then_inc(xn_set, 1)
                if has_next:
                    z_low(*ahead(i)[0])
                    z_low(*ahead(i)[1])
                dve.wait_ge(keys_saved, i + 1)
                dve.tensor_tensor(qk[:, :, :], p_qk[:, 0:E * DK].rearrange("p (e d) -> p e d", e=E), keys[:, :, :],
                                  ALU.mult).then_inc(prod_set, 1)
                dve.wait_ge(prod_set, i + 1)
                dve.tensor_reduce(sc[:, :], qk[:, :, :], AX.X, ALU.add).then_inc(sc_set, 1)
                dve.wait_ge(sc_set, i + 1)
                dve.reduce_max(mx[:, :], sc[:, :], AX.X).then_inc(mx_set, 1)
                dve.wait_ge(mx_set, i + 1)
                dve.tensor_scalar(nmx[:, :], mx[:, :], -SCALE, None, ALU.mult).then_inc(nmx_set, 1)
                dve.wait_ge(ew_set, i + 1)
                dve.reciprocal(rden[:, :], den[:, :]).then_inc(rden_set, 1)
                dve.wait_ge(qk_done, 2 * i + 2)
                dve.tensor_tensor(hw[:, :, :], p_h[:, :].rearrange("p (e r) -> p e r", e=E),
                                  ew[:, :].unsqueeze(2).to_broadcast([P, E, R]), ALU.mult).then_inc(hw_set, 1)
                dve.wait_ge(hw_set, i + 1)
                dve.wait_ge(rden_set, i + 1)
                wait_ge(dve, hwt_done, i)
                dve.tensor_scalar(hwn[:, :], hw[:, :, :].rearrange("p e r -> p (e r)"), rden[:, 0:1], None,
                                  ALU.mult).then_inc(hwn_set, 1)
                if has_next:
                    for ii, j in ahead(i)[2:]:
                        z_low(ii, j)
                dve.wait_ge(f_done, i + 1)
                dve.wait_ge(x1b_set, i + 1)
                wait_ge(dve, out_sent[s], 8 * (i - s))
                dve.tensor_tensor(res[:, s, :], p_f[:, :], x1b[:, :], ALU.add).then_inc(res_set, 1)

            tiles(dve, first, step)

        @block.scalar
        def _(act):
            def wo_high(w):
                at = slice(w * WH, (w + 1) * WH)
                act.wait_ge(raw_in[w % SLOTS], 16 * (w // SLOTS + 1))
                act.activation(wo[0][:, at, :], raw[w % SLOTS][:, :].rearrange("p (h n) -> p h n", h=WH), ACT.Copy,
                               scale=gn[:, 0:1]).then_inc(hi_set, 1)

            def z_high(i, j):
                act.wait_ge(raw_in[j % SLOTS], 16 * (NW // SLOTS) + 16 * (i + 1))
                wait_ge(act, heads_done, NP * i + j - 1)
                act.activation(z_hi[j % 2][:, :, :], raw[j % SLOTS][:, :].rearrange("p (h t) -> p h t", h=HP),
                               ACT.Copy).then_inc(hi_set, 1)

            def first():
                act.wait_ge(gn_in, 16)
                for w in range(NW):
                    wo_high(w)
                for j in range(NP):
                    z_high(0, j)
                z_high(1, 0)

            def step(i, s, has_next):
                if has_next:
                    z_high(*ahead(i)[0])
                act.wait_ge(xt_done, i + 1)
                wait_ge(act, f_done, i)
                act.activation(xt[:, :, :], p_xt[:, :, :], ACT.Copy).then_inc(xt_saved, 1)
                if has_next:
                    z_high(*ahead(i)[1])
                act.wait_ge(qk_done, 2 * i + 1)
                wait_ge(act, prod_set, i)
                act.activation(keys[:, :, :], p_qk[:, E * DK:].rearrange("p (e d) -> p e d", e=E), ACT.Copy).then_inc(keys_saved, 1)
                act.wait_ge(nmx_set, i + 1)
                wait_ge(act, hw_set, i)
                wait_ge(act, rden_set, i)
                act.activation(ew[:, :], sc[:, :], ACT.Exp, scale=SCALE, bias=nmx[:, 0:1], accum_out=den[:, 0:1]).then_inc(ew_set, 1)
                if has_next:
                    z_high(*ahead(i)[2])
                act.wait_ge(hwt_done, i + 1)
                act.activation(hwt[:, :], p_hwt[:, :], ACT.Copy).then_inc(hwt_saved, 1)
                if has_next:
                    for ii, j in ahead(i)[3:]:
                        z_high(ii, j)

            tiles(act, first, step)

        @block.gpsimd
        def _(pool):
            def first():
                pool.wait_ge(c_set, 2)
                pool.wait_ge(small_in, 80)

            def step(i, s, has_next):
                pool.wait_ge(mv_set, i + 1)
                pool.tensor_tensor(var[:, :], mv[:, 1:2], eps[:, :], ALU.add).then_inc(var_set, 1)
                pool.wait_ge(var_set, i + 1)
                pool.tensor_tensor(rstd[:, :], var[:, :], mhalf[:, :], ALU.pow).then_inc(rstd_set, 1)
                wait_ge(pool, res_set, i)
                pool.wait_ge(xn_set, i + 1)
                pool.tensor_tensor(x1b[:, :], x1[:, :], bias[:, :], ALU.add).then_inc(x1b_set, 1)

            tiles(pool, first, step)


def build(nc, io):
    with ExitStack() as ctx:
        keep = {"g_dram": nc.dram_tensor("g_scratch", [KVH, B, NC, HG, C], F32).ap(),
                "z_dram": nc.dram_tensor("z_scratch", [NT, P, H, C], F32).ap(),
                "ident": ctx.enter_context(nc.sbuf_tensor("ident", [P, P], F32))}
        with ExitStack() as inner:
            keep["xh"] = inner.enter_context(nc.sbuf_tensor("xh", [P, KT, B * L], F32R))
            keep["xl"] = inner.enter_context(nc.sbuf_tensor("xl", [P, KT, B * L], F32R))
            keep["tab"] = inner.enter_context(nc.sbuf_tensor("tab", [P, NC, TAB, B * H], F32))
            keep["w_raw"] = [inner.enter_context(nc.sbuf_tensor(f"w_raw{i}", [P, 2 * GW], F32)) for i in range(3)]
            for name, width in (("wkv", 2 * D), ("wq", GW), ("wg", GW)):
                keep[name] = [inner.enter_context(nc.sbuf_tensor(f"{name}_{n}", [P, KT, width], F32R)) for n in ("hi", "lo")]
            norm_stage(nc, io, keep)
            attention_stage(nc, io, keep)
        output_stage(nc, io, keep)


def rope_tables():
    inv = (1.0 / np.float32(10000.0) ** (np.arange(0, D, 2, dtype=np.float32) / np.float32(D))).astype(np.float32)
    ang = np.arange(L, dtype=np.float32)[:, None] * inv
    cos, sin = np.cos(ang).T, np.sin(ang).T
    return (np.ascontiguousarray(np.concatenate([cos, cos]), np.float32),
            np.ascontiguousarray(np.concatenate([-sin, sin]), np.float32))


def kernel(**inputs):
    import numpy as _np
    import concourse.bacc as _bacc
    from concourse import mybir as _mybir
    from concourse.bass_utils import run_bass_kernel_spmd as _run

    a = {k: _np.asarray(v) for k, v in inputs.items()}
    cos, sin = rope_tables()
    t = _np.ascontiguousarray
    by_group = lambda w, n: t(w.reshape(KVH, n, HID).transpose(0, 2, 1))
    arrays = {
        "x": t(a["L0_attn_hidden_states"].reshape(B * L, HID)),
        "win_t": t(a["L0_attn_Win"].T),
        "dt_bias": t(a["L0_attn_dt_bias"]),
        "A_log_bias": t(a["L0_attn_A_log_bias"]),
        "gnorm_w": t(a["L0_attn_gnorm_w"]),
        "wq_t": by_group(a["L0_attn_Wq"], GW),
        "wg_t": by_group(a["L0_attn_Wg"], GW),
        "wkv_t": t(_np.concatenate([by_group(a["L0_attn_Wk"], D), by_group(a["L0_attn_Wv"], D)], axis=2)),
        "wo_t": t(a["L0_attn_Wo"].T),
        "w_t": t(a["L0_ffn_W"].T),
        "b": t(a["L0_ffn_b"]),
        "wqk_t": t(_np.concatenate([a["L0_ffn_Wq"].T, a["L0_ffn_Wk"].T], axis=1)),
        "a_t": t(a["L0_ffn_A"].reshape(E * R, HID).T),
        "bm_t": t(a["L0_ffn_Bm"].transpose(0, 2, 1).reshape(E * R, HID)),
        "cos_t": cos,
        "sin_t": sin,
    }
    nc = _bacc.Bacc("TRN2", target_bir_lowering=False, num_devices=1)
    io = {k: nc.dram_tensor(f"in_{k}", v.shape, _mybir.dt.from_np(v.dtype), kind="ExternalInput").ap()
          for k, v in arrays.items()}
    io["out"] = nc.dram_tensor("out_dram", (B * L, HID), _mybir.dt.float32, kind="ExternalOutput").ap()
    build(nc, io)
    r = _run(nc, [{f"in_{k}": v for k, v in arrays.items()}], core_ids=[0])
    return r.results[0]["out_dram"].reshape(B, L, HID)
```

```python
from contextlib import ExitStack

import numpy as np

import concourse.bass as bass
from concourse import mybir

ALU = mybir.AluOpType
ACT = mybir.ActivationFunctionType
AX = mybir.AxisListType
F32 = mybir.dt.float32
F32R = mybir.dt.float32r

P = 128
B, L, HID = 4, 512, 512
H, KVH, D = 32, 8, 128
C = 128
HG = H // KVH
NC = L // C
KT = HID // P
NT = B * NC
GW = HG * D
EPS = 1e-5
E, DK, R = 8, 32, 16
NORM_SLOTS = 3
UNITS = 10
ROPED = 1 + HG
TAB = 4
T_DT, T_NEGG, T_EXPG, T_W = range(TAB)


def wait_ge(engine, sem, count):
    if not isinstance(count, int) or count > 0:
        engine.wait_ge(sem, count)


def part(w_raw, i):
    return w_raw[i][:, :].rearrange("p (k n) -> p k n", k=KT if i == 0 else KT // 2)


def dst(w, i):
    return w[:, :, :] if i == 0 else w[:, (i - 1) * 2:i * 2, :]


def kv_piece(io, g):
    return io["wkv_t"][bass.ds(g, 1)].rearrange("a (k p) n -> p (a k) n", p=P)


def half_piece(w, g, i):
    return w[bass.ds(g, 1), (i - 1) * 2 * P:i * 2 * P].rearrange("a (k p) n -> p (a k) n", p=P)


def wide(pe, out, pairs, half=None):
    for i, (lhs, rhs) in enumerate(pairs):
        if half and i == len(pairs) // 2:
            wait_ge(pe, *half)
        for j, (a, e) in enumerate(((0, 0), (1, 0), (0, 1))):
            mm = pe.matmul(out, lhs[a], rhs[e], start=(i == 0 and j == 0), stop=(i == len(pairs) - 1 and j == 2))
    return mm


def x_parts(keep, b, kt, t):
    return keep["shared"][:, b * KT + kt, 0, t], keep["shared"][:, b * KT + kt, 1, t]


def project(pe, keep, w, w0, b, into):
    return wide(pe, into[:, :, :].rearrange("p h t -> p (h t)"),
                [((w[0][:, kt, w0:w0 + D], w[1][:, kt, w0:w0 + D]), x_parts(keep, b, kt, slice(0, L))) for kt in range(KT)])


def rotate(dve, keep, bank, s):
    half, x = D // 2, bank[:, :, :].rearrange("p h t -> p (h t)")
    rope_a, rope_b, sin = keep["rope_a"], keep["rope_b"], keep["sin"]
    dve.tensor_tensor(rope_a[:, s, :], x, keep["cos"][:, :], ALU.mult)
    dve.tensor_tensor(rope_b[0:half, s, :], x[half:D, :], sin[0:half, :], ALU.mult)
    dve.tensor_tensor(rope_b[half:D, s, :], x[0:half, :], sin[half:D, :], ALU.mult).then_inc(keep["rope_terms"], 1)


def add_rope(pool, keep, n, b, r):
    s = (b + r) % 2
    pool.wait_ge(keep["rope_terms"], ROPED * n + r + 1)
    out = keep["k"][:, b % 2, :] if r == 0 else keep["q"][b % 2][:, r - 1, :]
    pool.tensor_tensor(out, keep["rope_a"][:, s, :], keep["rope_b"][:, s, :], ALU.add).then_inc(keep["roped"], 1)


def norm_stage(nc, io, keep):
    shared, tab, ident, g_dram, w_raw, wkv, wq, wg = (keep[k] for k in (
        "shared", "tab", "ident", "g_dram", "w_raw", "wkv", "wq", "wg"))
    assert B * H == P
    with ExitStack() as ctx:
        def sb(name, shape, dt=F32):
            return ctx.enter_context(nc.sbuf_tensor(name, shape, dt))

        def pb(name, shape):
            return ctx.enter_context(nc.psum_tensor(name, shape, F32))

        def sem(name):
            return ctx.enter_context(nc.semaphore(name))

        xin = sb("n_xin", [P, NT, HID])
        stats = sb("n_stats", [P, NT, 6])
        mv = sb("n_mv", [P, NT, 2])
        var = sb("n_var", [P, NT])
        rstd = sb("n_rstd", [P, NT])
        mhalf = sb("n_mhalf", [P, NT])
        xn = sb("n_xn", [P, NORM_SLOTS, HID])
        xt = sb("n_xt", [P, NORM_SLOTS, KT, P])
        win = sb("n_win", [P, KT, H])
        hcol = sb("n_hcol", [P, 3])
        ones = sb("n_ones", [P, C])
        pre, ab, ex, u1, ln, df, rc, gg, G, wexp = (xin[:, i, :] for i in range(10))
        rows = sb("n_rows", [P, TAB, L])
        pt = [pb(f"n_pt{i}", [P, KT, P]) for i in range(2)]
        pdt = pb("n_pdt", [P, L])
        ptab = [pb(f"n_ptab{k}", [P, NC, P]) for k in range(2)] + pt
        p_proj = [pb(f"n_p_proj{i}", [P, HG, P]) for i in range(2)]

        x_in = [sem(f"n_x_in{b}") for b in range(B)]
        x_first = sem("n_x_first")
        small_in = sem("n_small_in")
        kv_in, q_in, g_in, trig_in = sem("n_kv_in"), sem("n_q_in"), sem("n_g_in"), sem("n_trig_in")
        unit_done, rope_terms, roped, v_set = sem("n_unit_done"), keep["rope_terms"], keep["roped"], keep["v_set"]
        w_hi, w_lo = sem("n_w_hi"), sem("n_w_lo")
        const_set, acol_set = sem("n_const_set"), sem("n_acol_set")
        stats_set, mv_set, var_set, rstd_set, xn_set = (sem(f"n_{n}_set") for n in ("stats", "mv", "var", "rstd", "xn"))
        xt_done, xt_saved, lo_set, dt_done = sem("n_xt_done"), sem("n_xt_saved"), sem("n_lo_set"), sem("n_dt_done")
        pre_set, ex_set, u1_set, df_set, rc_set, ln_set, log_set = (sem(f"n_{n}_set") for n in (
            "pre", "ex", "u1", "df", "rc", "ln", "log"))
        gg_set, G_set, wexp_set = sem("n_gg_set"), sem("n_G_set"), sem("n_wexp_set")
        row_set = [sem(f"n_row_set{k}") for k in range(TAB)]
        tabs_done, tabs_saved, g_out = sem("n_tabs_done"), sem("n_tabs_saved"), sem("n_g_out")
        block = ctx.enter_context(nc.Block())

        def x_part(e, i):
            b, c = i // NC, i % NC
            return shared[:, b * KT:(b + 1) * KT, e, c * P:(c + 1) * P]

        @block.sync
        def _(sp):
            def load_x(b):
                sp.dma_start(xin[:, b * NC:(b + 1) * NC, :],
                             io["x"][b * L:(b + 1) * L, :].rearrange("(c p) n -> p c n", p=P)).then_inc(x_in[b], 16)

            sp.dma_start(xin[:, 0:2, :], io["x"][0:2 * P, :].rearrange("(c p) n -> p c n", p=P)).then_inc(x_first, 16)
            sp.dma_start(xin[:, 2:NC, :], io["x"][2 * P:L, :].rearrange("(c p) n -> p c n", p=P)).then_inc(x_in[0], 16)
            sp.dma_start(win[:, :, :], io["win_t"].rearrange("(k p) h -> p k h", p=P)).then_inc(small_in, 16)
            load_x(1)
            for b in range(B):
                at = slice(b * H, (b + 1) * H)
                sp.dma_start(hcol[at, 0:1], io["dt_bias"].rearrange("(h a) -> h a", a=1)).then_inc(small_in, 16)
                sp.dma_start(hcol[at, 1:2], io["A_log_bias"].rearrange("(h a) -> h a", a=1)).then_inc(small_in, 16)
            load_x(2)
            sp.dma_start(part(w_raw, 0), kv_piece(io, 0)).then_inc(kv_in, 16)
            load_x(3)
            for i in (1, 2):
                sp.dma_start(part(w_raw, i), half_piece(io["wq_t"], 0, i)).then_inc(q_in, 16)
            sp.dma_start(keep["cos"][:, :], io["cos_t"]).then_inc(trig_in, 16)
            sp.dma_start(keep["sin"][:, :], io["sin_t"]).then_inc(trig_in, 16)
            sp.wait_ge(w_lo, 3)
            for i in (1, 2):
                sp.dma_start(part(w_raw, i), half_piece(io["wg_t"], 0, i)).then_inc(g_in, 16)
            sp.wait_ge(G_set, 1)
            sp.dma_start(g_dram.rearrange("c b g h t -> (b g h) c t"), G[:, :].rearrange("h (c t) -> h c t", t=C)).then_inc(g_out, 16)
            sp.wait_ge(g_out, 16)

        @block.gpsimd
        def _(pool):
            def w_low(j, w, i):
                pool.wait_ge(w_hi, j + 1)
                pool.tensor_tensor(dst(w[1], i), part(w_raw, i), dst(w[0], i).bitcast(F32), ALU.subtract).then_inc(w_lo, 1)

            pool.memset(ident[:, :], 0.0).then_inc(const_set, 1)
            pool.memset(mhalf[:, :], -0.5).then_inc(const_set, 1)
            pool.memset(ones[:, :], 1.0).then_inc(const_set, 1)
            pool.wait_ge(const_set, 3)
            pool.affine_select(out=ident[:, :], in_=ident[:, :], compare_op=ALU.not_equal, fill=1.0,
                               base=0, pattern=[[-1, P]], channel_multiplier=1).then_inc(const_set, 1)
            for b in range(B):
                c0, c1 = b * NC, (b + 1) * NC
                pool.wait_ge(mv_set, c1)
                pool.tensor_scalar(var[:, c0:c1], mv[:, c0:c1, 1], EPS, None, ALU.add).then_inc(var_set, 1)
                pool.wait_ge(var_set, b + 1)
                pool.tensor_tensor(rstd[:, c0:c1], var[:, c0:c1], mhalf[:, c0:c1], ALU.pow).then_inc(rstd_set, 1)
                if b == 1:
                    w_low(0, wkv, 0)
            w_low(1, wq, 1)
            w_low(2, wq, 2)
            add_rope(pool, keep, 0, 0, 0)
            add_rope(pool, keep, 0, 0, 1)
            w_low(3, wg, 1)
            add_rope(pool, keep, 0, 0, 2)
            w_low(4, wg, 2)
            for r in range(3, ROPED):
                add_rope(pool, keep, 0, 0, r)

        @block.vector
        def _(dve):
            def statistics(b):
                dve.wait_ge(x_in[b] if b else x_first, 16)
                for i in range(b * NC, (b + 1) * NC):
                    if i == 2:
                        dve.wait_ge(x_in[0], 16)
                    dve.bn_stats(stats[:, i, :], xin[:, i, :]).then_inc(stats_set, 1)
                for i in range(b * NC, (b + 1) * NC):
                    dve.wait_ge(stats_set, i + 1)
                    dve.bn_aggr(mv[:, i, :], stats[:, i, :]).then_inc(mv_set, 1)

            def normalise(i):
                if i % NC == 0:
                    dve.wait_ge(rstd_set, i // NC + 1)
                if i >= NORM_SLOTS:
                    dve.wait_ge(xt_done, i - NORM_SLOTS + 1)
                dve.tensor_scalar(xn[:, i % NORM_SLOTS, :], xin[:, i, :], mv[:, i, 0:1], rstd[:, i:i + 1],
                                  ALU.subtract, ALU.mult).then_inc(xn_set, 1)

            def low_part(i):
                dve.wait_ge(xt_saved, i + 1)
                dve.tensor_tensor(x_part(1, i), xt[:, i % NORM_SLOTS], x_part(0, i).bitcast(F32), ALU.subtract).then_inc(lo_set, 1)

            def rotate_tile(r):
                unit = r if r == 0 else r + 1
                dve.wait_ge(unit_done, unit + 1)
                if r >= 2:
                    dve.wait_ge(roped, r - 1)
                rotate(dve, keep, p_proj[unit % 2], r % 2)

            dve.wait_ge(const_set, 3)
            statistics(0)
            for b in range(B):
                for i in range(b * NC, (b + 1) * NC):
                    if i % NC == 2 and b + 1 < B:
                        statistics(b + 1)
                    normalise(i)
                    if i >= 2:
                        low_part(i - 2)
                    if i == 11:
                        dve.wait_ge(trig_in, 32)
                        rotate_tile(0)
            low_part(NT - 2)
            low_part(NT - 1)
            dve.wait_ge(ex_set, 1)
            dve.tensor_scalar(u1[:, :], ex[:, :], 1.0, None, ALU.add).then_inc(u1_set, 1)
            dve.wait_ge(u1_set, 1)
            dve.scalar_tensor_tensor(df[:, :], u1[:, :], -1.0, ex[:, :], ALU.add, ALU.subtract).then_inc(df_set, 1)
            rotate_tile(1)
            rotate_tile(2)
            dve.wait_ge(df_set, 1)
            dve.wait_ge(rc_set, 1)
            dve.tensor_tensor(df[:, :], df[:, :], rc[:, :], ALU.mult).then_inc(df_set, 1)
            dve.wait_ge(df_set, 2)
            dve.wait_ge(log_set, 1)
            dve.tensor_tensor(ln[:, :], ln[:, :], df[:, :], ALU.subtract).then_inc(ln_set, 1)
            dve.wait_ge(ln_set, 1)
            dve.scalar_tensor_tensor(rows[:, T_DT, :], pre[:, :], 0.0, ln[:, :], ALU.max, ALU.add).then_inc(row_set[T_DT], 1)
            dve.wait_ge(row_set[T_DT], 1)
            dve.wait_ge(acol_set, 1)
            dve.tensor_scalar(gg[:, :], rows[:, T_DT, :], hcol[:, 2:3], -1.0, ALU.mult, ALU.mult).then_inc(gg_set, 1)
            dve.wait_ge(gg_set, 1)
            for c in range(NC):
                at = slice(c * C, (c + 1) * C)
                scan = dve.tensor_tensor_scan(G[:, at], ones[:, :], gg[:, at], 0.0, ALU.mult, ALU.add)
            scan.then_inc(G_set, 1)
            dve.wait_ge(G_set, 1)
            dve.tensor_scalar(rows[:, T_NEGG, :], G[:, :], -1.0, None, ALU.mult).then_inc(row_set[T_NEGG], 1)
            rotate_tile(3)
            dve.wait_ge(wexp_set, 1)
            dve.tensor_tensor(rows[:, T_W, :], rows[:, T_DT, :], wexp[:, :], ALU.mult).then_inc(row_set[T_W], 1)
            rotate_tile(4)

        @block.scalar
        def _(act):
            def halves(i):
                act.wait_ge(xt_done, i + 1)
                act.activation(x_part(0, i), pt[i % 2][:, :, :], ACT.Copy)
                if i >= NORM_SLOTS:
                    act.wait_ge(dt_done, i - NORM_SLOTS + 1)
                    act.wait_ge(lo_set, i - NORM_SLOTS + 1)
                act.activation(xt[:, i % NORM_SLOTS, :, :], pt[i % 2][:, :, :], ACT.Copy).then_inc(xt_saved, 1)

            def w_high(w, i, loaded, count):
                act.wait_ge(loaded, count)
                act.activation(dst(w[0], i), part(w_raw, i), ACT.Copy).then_inc(w_hi, 1)

            act.wait_ge(small_in, 16 * (1 + 2 * B))
            act.activation(hcol[:, 2:3], hcol[:, 1:2], ACT.Exp).then_inc(acol_set, 1)
            for i in range(NT):
                halves(i)
                if i == 5:
                    w_high(wkv, 0, kv_in, 16)
                if i == 8:
                    w_high(wq, 1, q_in, 32)
                if i == 9:
                    w_high(wq, 2, q_in, 32)
                if i == 13:
                    act.wait_ge(unit_done, 2)
                    act.activation(keep["v_t"][:, :], p_proj[1][:, :, :].rearrange("p h t -> p (h t)"), ACT.Copy).then_inc(v_set, 1)
            act.wait_ge(dt_done, NT)
            act.activation(ab[:, :], pdt[:, :], ACT.Abs, bias=hcol[:, 0:1]).then_inc(pre_set, 1)
            act.wait_ge(pre_set, 1)
            act.activation(ex[:, :], ab[:, :], ACT.Exp, scale=-1.0).then_inc(ex_set, 1)
            act.activation(pre[:, :], pdt[:, :], ACT.Identity, bias=hcol[:, 0:1]).then_inc(pre_set, 1)
            w_high(wg, 1, g_in, 32)
            act.wait_ge(u1_set, 1)
            act.activation(ln[:, :], u1[:, :], ACT.Ln).then_inc(log_set, 1)
            act.wait_ge(log_set, 1)
            act.activation(rc[:, :], ln[:, :], ACT.Exp, scale=-1.0).then_inc(rc_set, 1)
            w_high(wg, 2, g_in, 32)
            act.wait_ge(G_set, 1)
            for c in range(NC):
                at = slice(c * C, (c + 1) * C)
                w = act.activation(wexp[:, at], G[:, at], ACT.Exp, scale=-1.0, bias=G[:, (c + 1) * C - 1:(c + 1) * C])
            w.then_inc(wexp_set, 1)
            act.activation(rows[:, T_EXPG, :], G[:, :], ACT.Exp).then_inc(row_set[T_EXPG], 1)
            for j, k in enumerate((T_DT, T_NEGG, T_EXPG, T_W)):
                act.wait_ge(tabs_done, j + 1)
                act.activation(tab[:, :, k, :], ptab[k][:, :, :], ACT.Copy).then_inc(tabs_saved, 1)

        @block.tensor
        def _(pe):
            pe.wait_ge(const_set, 4)
            pe.wait_ge(small_in, 16 * (1 + 2 * B))

            def turn(i):
                pe.wait_ge(xn_set, i + 1)
                if i >= 2:
                    pe.wait_ge(xt_saved, i - 1)
                for k in range(KT):
                    t = pe.transpose(pt[i % 2][:, k, :], xn[:, i % NORM_SLOTS, k * P:(k + 1) * P], ident[:, :])
                t.then_inc(xt_done, 1)

            def dt_rows(i):
                b, c = i // NC, i % NC
                pe.wait_ge(xt_saved, i + 1)
                for k in range(KT):
                    m = pe.matmul(pdt[b * H:(b + 1) * H, c * P:(c + 1) * P], win[:, k, :], xt[:, i % NORM_SLOTS, k, :],
                                  start=(k == 0), stop=(k == KT - 1))
                m.then_inc(dt_done, 1)

            def turn_table(k):
                pe.wait_ge(row_set[k], 1)
                for c in range(NC):
                    t = pe.transpose(ptab[k][:, c, :], rows[:, k, c * C:(c + 1) * C], ident[:, :])
                t.then_inc(tabs_done, 1)

            def project_q(h):
                if h == 1:
                    pe.wait_ge(v_set, 1)
                else:
                    pe.wait_ge(rope_terms, max(h, 1))
                project(pe, keep, wq, h * D, 0, p_proj[h % 2]).then_inc(unit_done, 1)

            for i in range(NT):
                turn(i)
                if i:
                    dt_rows(i - 1)
                if i == 9:
                    pe.wait_ge(w_lo, 1)
                    pe.wait_ge(lo_set, NC)
                    project(pe, keep, wkv, 0, 0, p_proj[0]).then_inc(unit_done, 1)
                if i == 12:
                    project(pe, keep, wkv, D, 0, p_proj[1]).then_inc(unit_done, 1)
            dt_rows(NT - 1)
            pe.wait_ge(w_lo, 3)
            for h in range(HG):
                project_q(h)
            for k in (T_DT, T_NEGG, T_EXPG, T_W):
                turn_table(k)


def attention_stage(nc, io, keep):
    shared, tab, ident, g_dram, z_dram = (keep[k] for k in ("shared", "tab", "ident", "g_dram", "z_dram"))
    with ExitStack() as ctx:
        def sb(name, shape, dt=F32):
            return ctx.enter_context(nc.sbuf_tensor(name, shape, dt))

        def pb(name):
            return ctx.enter_context(nc.psum_tensor(name, [P, HG, P], F32))

        def sem(name):
            return ctx.enter_context(nc.semaphore(name))

        w_raw, wkv, wq, wg = (keep[k] for k in ("w_raw", "wkv", "wq", "wg"))
        k, q, v_t = keep["k"], keep["q"], keep["v_t"]
        q.append(sb("q1", [P, HG, L]))
        k_tok = sb("k_tok", [P, NC, D])
        v_tok = sb("v_tok", [P, NC, D])
        stab = sb("stab", [P, 2, NC, TAB, HG])
        xc = sb("xc", [P, 2, HG, D])
        xw = sb("xw", [P, 2, HG, D])
        g_row = sb("g_row", [P, 2, HG, C])
        probs = sb("probs", [P, 2, HG, C])
        q_part = [sb(f"q_{e}", [P, HG, C], F32R) for e in ("hi", "lo")]
        k_part = [sb(f"k_{e}", [P, C], F32R) for e in ("hi", "lo")]
        chunk_decay = sb("chunk_decay", [P, NC, HG])
        state = sb("state", [P, 2, HG, D])
        tanh = sb("tanh", [P, GW])
        gate = sb("gate", [P, 2, GW])
        y_int = sb("y_int", [P, HG, D])
        y = sb("y", [P, HG, D])
        ssum = sb("ssum", [P, NC, HG])
        svar = sb("svar", [P, NC, HG])
        srstd = sb("srstd", [P, NC, HG])
        mhalf = sb("mhalf", [P, HG])
        eps4 = sb("eps4", [P, HG])
        before = sb("before", [P, C])
        z = sb("z", [P, HG, D])
        z_t = sb("z_t", [P, 2, HG, C])

        p_proj = [pb(f"p_proj{i}") for i in range(2)]
        p_score, p_inter, p_intra, p_cst, p_zt = (pb(n) for n in (
            "p_score", "p_inter", "p_intra", "p_cst", "p_zt"))
        p_tok = keep["p_tok"]

        w_in = [sem(f"w_in{i}") for i in range(3)]
        g_in = [sem(f"g_in{i}") for i in range(2)]
        z_out = keep["z_out"]
        unit_done, unit_free = sem("unit_done"), sem("unit_free")
        score_done, intra_done, inter_done = sem("score_done"), sem("intra_done"), sem("inter_done")
        cst_done, zt_done, tok_done = sem("cst_done"), sem("zt_done"), sem("tok_done")
        probs_set, state_set, y_set, z_set = sem("probs_set"), sem("state_set"), sem("y_set"), sem("z_set")
        rope_terms, roped, v_set = keep["rope_terms"], keep["roped"], keep["v_set"]
        kv_split, q_split, g_split = sem("kv_split"), sem("q_split"), sem("g_split")
        kv_hi, q_hi, g_hi = sem("kv_hi"), sem("q_hi"), sem("g_hi")
        decay_set, tanh_set, yint_set = sem("decay_set"), sem("tanh_set"), sem("yint_set")
        squares_set, zt_saved, tok_saved = sem("squares_set"), sem("zt_saved"), sem("tok_saved")
        masked_set, xc_set, xw_set = sem("masked_set"), sem("xc_set"), sem("xw_set")
        mask_set, qk_hi_set, qk_lo_set = sem("mask_set"), sem("qk_hi_set"), sem("qk_lo_set")
        svar_set, srstd_set, stab_set, const_set = sem("svar_set"), sem("srstd_set"), sem("stab_set"), sem("const_set")
        block = ctx.enter_context(nc.Block())

        GATE_UNIT, K_UNIT, V_UNIT, Q_UNIT = (0, 3, 5, 7), 1, 2, (4, 6, 8, 9)

        def unit(n, at):
            if isinstance(n, int) and n == B * KVH - 1:
                at = GATE_UNIT.index(at)
            return UNITS * n + at

        def bank(n, b, at):
            if isinstance(n, int):
                return p_proj[unit(n, at) % 2]
            return p_proj[(UNITS * b + at) % 2]

        def steps(engine, first, step):
            def group(g):
                for b in range(B):
                    step(g, b, B * g + b)

            first()
            group(0)
            with engine.Fori(1, KVH - 1) as g:
                group(g)
            group(KVH - 1)

        def ahead(n):
            return not (isinstance(n, int) and n == B * KVH - 1)

        def has_last(n):
            return not (isinstance(n, int) and n == 0)

        def more(n, c, by):
            return not (isinstance(n, int) and NC * n + c + by >= NC * B * KVH)

        def group_ahead(g):
            return not (isinstance(g, int) and g == KVH - 1)

        @block.sync
        def _(sp):
            def load_kv(g):
                sp.dma_start(part(w_raw, 0), kv_piece(io, g)).then_inc(w_in[0], 16)

            def load_half(w, g, i):
                sp.dma_start(part(w_raw, i), half_piece(io[w], g, i)).then_inc(w_in[i], 16)

            def load_g(g, b, c):
                src = g_dram[c, b, bass.ds(g, 1)].rearrange("a h t -> a (h t)").to_broadcast([P, HG * C])
                sp.dma_start(g_row[:, c % 2].rearrange("p h t -> p (h t)"), src).then_inc(g_in[c % 2], 16)

            def first():
                load_g(0, 0, 0)
                load_g(0, 0, 1)
                sp.dma_start(keep["gn"][:, :], io["gnorm_w"].rearrange("(p a) -> p a", a=1)).then_inc(keep["gn_in"], 16)

            def step(g, b, n):
                if not ahead(n):
                    for s in range(2):
                        sp.wait_ge(z_out[s], 16 * 2 * (n - 2))
                    sp.wait_ge(intra_done, NC * n)
                    for k in range(SLOTS):
                        load_opening(sp, io, keep, k)
                for c in range(NC):
                    m = NC * n + c
                    if more(n, c, 2):
                        sp.wait_ge(decay_set, m + 1)
                        nb, ncc = b + (c + 2) // NC, (c + 2) % NC
                        load_g(g + nb // B, nb % B, ncc)
                    if c > 0:
                        store_z(g, b, n, c - 1)
                    elif has_last(n):
                        store_z(g if b else g - 1, (b - 1) % B, n - 1, NC - 1)
                    if not ahead(n):
                        for k in (SLOTS + 2 * c, SLOTS + 2 * c + 1):
                            load_opening(sp, io, keep, k)
                    if group_ahead(g):
                        if b == 0 and c == 1:
                            wait_ge(sp, kv_split, g)
                            load_kv(g + 1)
                        if b == 0 and c == 2:
                            wait_ge(sp, g_split, 2 * g)
                            load_half("wq_t", g + 1, 1)
                            load_half("wq_t", g + 1, 2)
                        if b == B - 1 and c == 2:
                            sp.wait_ge(q_split, g + 1)
                            load_half("wg_t", g + 1, 1)
                            load_half("wg_t", g + 1, 2)

            def store_z(g, b, n, c):
                sp.wait_ge(zt_saved, NC * n + c + 1)
                sp.dma_start(z_dram[b * NC + c, :, bass.ds(g * HG, HG), :], z_t[:, c % 2]).then_inc(z_out[c % 2], 16)

            steps(sp, first, step)
            store_z(KVH - 1, B - 1, B * KVH - 1, NC - 1)

        @block.tensor
        def _(pe):
            def gates(g, b, n, c):
                u = unit(n, GATE_UNIT[c])
                wait_ge(pe, unit_free, u - 1)
                if b == 0 and c == 0:
                    wait_ge(pe, g_split, 2 * g - 1)
                wide(pe, bank(n, b, GATE_UNIT[c])[:, :, :].rearrange("p h t -> p (h t)"),
                     [(x_parts(keep, b, kt, slice(c * C, (c + 1) * C)), (wg[0][:, kt, :], wg[1][:, kt, :])) for kt in range(KT)],
                     (g_split, 2 * g) if b == 0 and c == 0 else None).then_inc(unit_done, 1)

            def next_unit(g, b, n, at):
                if not ahead(n):
                    return
                u = unit(n, at)
                wait_ge(pe, unit_free, u - 1)
                if b == B - 1 and at == K_UNIT:
                    pe.wait_ge(kv_split, g + 1)
                if b == B - 1 and at == Q_UNIT[0]:
                    pe.wait_ge(q_split, g + 1)
                w, w0 = (wkv, 0) if at == K_UNIT else (wkv, D) if at == V_UNIT else (wq, Q_UNIT.index(at) * D)
                project(pe, keep, w, w0, (b + 1) % B, bank(n, b, at)).then_inc(unit_done, 1)

            def v_turn(n):
                pe.wait_ge(v_set, n + 1)
                wait_ge(pe, tok_saved, 2 * n)
                for c in range(NC):
                    t = pe.transpose(p_tok[:, c, :], v_t[:, c * C:(c + 1) * C], ident[:, :])
                t.then_inc(tok_done, 1)

            def k_turn(n, b):
                pe.wait_ge(roped, ROPED * n + 1)
                pe.wait_ge(tok_saved, 2 * n + 1)
                for c in range(NC - 1):
                    t = pe.transpose(p_tok[:, c, :], k[:, b % 2, c * C:(c + 1) * C], ident[:, :])
                t.then_inc(tok_done, 1)

            def scores(n, b, c):
                if c == 0:
                    pe.wait_ge(roped, ROPED * (n + 1))
                wait_ge(pe, probs_set, NC * n + c)
                pe.wait_ge(qk_lo_set, NC * n + c + 1)
                wide(pe, p_score[:, :, :], [([w[:, :] for w in k_part], [w[:, :, :] for w in q_part])]).then_inc(score_done, 1)

            def chunk_state(n, c):
                pe.wait_ge(xw_set, 3 * n + c + 1)
                if c == 0:
                    pe.wait_ge(tok_saved, 2 * n + 2)
                wait_ge(pe, state_set, 3 * n + c)
                pe.matmul(p_cst[:, :, :], k_tok[:, c, :], xw[:, c % 2, :, :], start=True, stop=True).then_inc(cst_done, 1)

            def inter(n, b, c):
                wait_ge(pe, state_set, 3 * n + c)
                wait_ge(pe, yint_set, 3 * n + c - 1)
                for h in range(HG):
                    mm = pe.matmul(p_inter[:, h, :], q[b % 2][:, h, c * C:(c + 1) * C], state[:, c % 2, h, :],
                                   start=True, stop=True)
                mm.then_inc(inter_done, 1)

            def intra(n, c):
                m = NC * n + c
                pe.wait_ge(probs_set, m + 1)
                pe.wait_ge(xc_set, m + 1)
                wait_ge(pe, y_set, m)
                for h in range(HG):
                    mm = pe.matmul(p_intra[:, h, :], probs[:, c % 2, h, :], xc[:, c % 2, h, :], start=True, stop=True)
                mm.then_inc(intra_done, 1)

            def z_turn(n, c):
                m = NC * n + c
                pe.wait_ge(z_set, m + 1)
                wait_ge(pe, zt_saved, m)
                for h in range(HG):
                    t = pe.transpose(p_zt[:, h, :], z[:, h, :], ident[:, :])
                t.then_inc(zt_done, 1)

            def first():
                v_turn(0)
                k_turn(0, 0)

            def first_heads(n, some):
                if not ahead(n):
                    pe.wait_ge(tok_saved, 2 * n + 2)
                    heads(pe, keep, p_tok[:, :, :].rearrange("p h t -> p (h t)"), 0, 0, 0, opening=True, some=some)

            def step(g, b, n):
                gates(g, b, n, 0)
                if has_last(n):
                    z_turn(n - 1, 3)
                next_unit(g, b, n, K_UNIT)
                chunk_state(n, 0)
                scores(n, b, 0)
                next_unit(g, b, n, V_UNIT)
                intra(n, 0)
                for c in (1, 2):
                    scores(n, b, c)
                    gates(g, b, n, c)
                    chunk_state(n, c)
                    inter(n, b, c)
                    next_unit(g, b, n, Q_UNIT[c - 1])
                    if c == 2:
                        first_heads(n, range(0, 2))
                    intra(n, c)
                    z_turn(n, c - 1)
                scores(n, b, 3)
                if ahead(n):
                    v_turn(n + 1)
                gates(g, b, n, 3)
                if ahead(n):
                    k_turn(n + 1, b + 1)
                inter(n, b, 3)
                first_heads(n, range(2, 4))
                intra(n, 3)
                z_turn(n, 2)
                first_heads(n, range(4, HP))
                next_unit(g, b, n, Q_UNIT[2])
                next_unit(g, b, n, Q_UNIT[3])

            steps(pe, first, step)
            z_turn(B * KVH - 1, 3)

        @block.vector
        def _(dve):
            def split(w, pieces, hi_sem, done, g):
                for j, i in enumerate(pieces):
                    dve.wait_ge(hi_sem, len(pieces) * g + (j + 1 - len(pieces)))
                    lo = dve.tensor_tensor(dst(w[1], i), part(w_raw, i), dst(w[0], i).bitcast(F32), ALU.subtract)
                lo.then_inc(done, 1)

            def g_low(g, i):
                dve.wait_ge(g_hi, 2 * g - 2 + i)
                dve.tensor_tensor(dst(wg[1], i), part(w_raw, i), dst(wg[0], i).bitcast(F32), ALU.subtract).then_inc(g_split, 1)

            def rotate_next(g, b, n, at, r):
                if not ahead(n):
                    return
                u = unit(n, at)
                dve.wait_ge(unit_done, u + 1)
                wait_ge(dve, roped, ROPED * (n + 1) + r - 1)
                rotate(dve, keep, bank(n, b, at), (b + 1 + r) % 2)
                dve.wait_ge(rope_terms, ROPED * (n + 1) + r + 1)
                dve.sem_inc(unit_free, 1)

            def first():
                dve.memset(mhalf[:, :], -0.5).then_inc(const_set, 1)
                dve.memset(eps4[:, :], 4.0 * EPS).then_inc(const_set, 1)

            def make_gate(g, b, n, c):
                m, u = NC * n + c, unit(n, GATE_UNIT[c])
                dve.wait_ge(tanh_set, m + 1)
                dve.scalar_tensor_tensor(gate[:, c % 2, :], tanh[:, :], 1.0,
                                         bank(n, b, GATE_UNIT[c])[:, :, :].rearrange("p h t -> p (h t)"),
                                         ALU.add, ALU.mult).then_inc(unit_free, 1)

            def make_probs(n, c):
                m = NC * n + c
                dve.wait_ge(score_done, m + 1)
                dve.wait_ge(decay_set, m + 1)
                dve.tensor_tensor(probs[:, c % 2], p_score[:, :, :], probs[:, c % 2], ALU.mult).then_inc(probs_set, 1)

            def qk_low(n, b, c):
                dve.wait_ge(qk_hi_set, NC * n + c + 1)
                at = slice(c * C, (c + 1) * C)
                dve.tensor_tensor(q_part[1][:, :, :], q[b % 2][:, :, at], q_part[0][:, :, :].bitcast(F32), ALU.subtract)
                dve.tensor_tensor(k_part[1][:, :], k[:, b % 2, at], k_part[0][:, :].bitcast(F32), ALU.subtract).then_inc(qk_lo_set, 1)

            def make_state(n, c):
                dve.wait_ge(cst_done, 3 * n + c + 1)
                if c == 0:
                    s = dve.tensor_copy(state[:, 1, :, :], p_cst[:, :, :])
                else:
                    for h in range(HG):
                        s = dve.scalar_tensor_tensor(state[:, (c + 1) % 2, h, :], state[:, c % 2, h, :],
                                                     chunk_decay[:, c, h:h + 1], p_cst[:, h, :], ALU.mult, ALU.add)
                s.then_inc(state_set, 1)

            def make_y(n, c):
                m = NC * n + c
                wait_ge(dve, z_set, m)
                dve.wait_ge(intra_done, m + 1)
                if c == 0:
                    dve.tensor_copy(y[:, :, :], p_intra[:, :, :]).then_inc(y_set, 1)
                else:
                    wait_ge(dve, yint_set, 3 * n + c)
                    dve.tensor_tensor(y[:, :, :], p_intra[:, :, :], y_int[:, :, :], ALU.add).then_inc(y_set, 1)

            def make_z(n, c):
                m = NC * n + c
                dve.wait_ge(srstd_set, m + 1)
                wait_ge(dve, zt_done, m)
                for h in range(HG):
                    zz = dve.scalar_tensor_tensor(z[:, h, :], y[:, h, :], srstd[:, c, h:h + 1],
                                                  gate[:, c % 2, h * D:(h + 1) * D], ALU.mult, ALU.mult)
                zz.then_inc(z_set, 1)

            def opening_lows(n, pieces):
                if not ahead(n):
                    for k in pieces:
                        opening_low(dve, keep, k)

            def step(g, b, n):
                if group_ahead(g) and b == B - 1:
                    split(wq, (1, 2), q_hi, q_split, g + 1)
                make_gate(g, b, n, 0)
                qk_low(n, b, 0)
                rotate_next(g, b, n, K_UNIT, 0)
                make_probs(n, 0)
                make_state(n, 0)
                qk_low(n, b, 1)
                if ahead(n):
                    dve.wait_ge(unit_done, unit(n, V_UNIT) + 1)
                    dve.tensor_copy(v_t[:, :], bank(n, b, V_UNIT)[:, :, :].rearrange("p h t -> p (h t)")).then_inc(v_set, 1)
                    dve.wait_ge(v_set, n + 2)
                    dve.sem_inc(unit_free, 1)
                opening_lows(n, (0,))
                make_y(n, 0)
                opening_lows(n, (1,))
                make_probs(n, 1)
                make_z(n, 0)
                for c in (1, 2):
                    qk_low(n, b, c + 1)
                    make_gate(g, b, n, c)
                    make_state(n, c)
                    opening_lows(n, (2 * c,))
                    make_y(n, c)
                    opening_lows(n, (2 * c + 1,))
                    rotate_next(g, b, n, Q_UNIT[c - 1], c)
                    if c == 1 and group_ahead(g) and b == B - 2:
                        split(wkv, (0,), kv_hi, kv_split, g + 1)
                    make_probs(n, c + 1)
                    make_z(n, c)
                make_gate(g, b, n, 3)
                opening_lows(n, (6,))
                make_y(n, 3)
                opening_lows(n, (7,))
                if group_ahead(g) and b == B - 1:
                    g_low(g + 1, 1)
                rotate_next(g, b, n, Q_UNIT[2], 3)
                make_z(n, 3)
                if group_ahead(g) and b == B - 1:
                    g_low(g + 1, 2)
                rotate_next(g, b, n, Q_UNIT[3], 4)

            steps(dve, first, step)

        @block.scalar
        def _(act):
            def split(w, pieces, done, g, loads):
                for i in pieces:
                    act.wait_ge(w_in[i], 16 * loads)
                    act.activation(dst(w[0], i), part(w_raw, i), ACT.Copy).then_inc(done, 1)

            def make_decay(n, b, c):
                act.wait_ge(masked_set, NC * n + c + 1)
                if c == 0:
                    act.wait_ge(stab_set, n + 1)
                wait_ge(act, intra_done, NC * n + c - 1)
                act.activation(chunk_decay[:, c, :], g_row[:, c % 2, :, C - 1], ACT.Exp)
                for h in range(HG):
                    e = act.activation(probs[:, c % 2, h, :], g_row[:, c % 2, h, :], ACT.Exp,
                                       bias=stab[:, b % 2, c, T_NEGG, h:h + 1])
                e.then_inc(decay_set, 1)

            def make_tanh(g, b, n, c):
                wait_ge(act, squares_set, NC * n + c)
                act.wait_ge(unit_done, unit(n, GATE_UNIT[c]) + 1)
                act.activation(tanh[:, :], bank(n, b, GATE_UNIT[c])[:, :, :].rearrange("p h t -> p (h t)"),
                               ACT.Tanh, scale=0.5).then_inc(tanh_set, 1)

            def qk_high(n, b, c):
                act.wait_ge(roped, ROPED * (n + 1))
                wait_ge(act, score_done, NC * n + c)
                at = slice(c * C, (c + 1) * C)
                act.activation(q_part[0][:, :, :], q[b % 2][:, :, at], ACT.Copy)
                act.activation(k_part[0][:, :], k[:, b % 2, at], ACT.Copy).then_inc(qk_hi_set, 1)

            def scale_inter(n, b, c):
                act.wait_ge(inter_done, 3 * n + c)
                wait_ge(act, y_set, NC * n + c)
                for h in range(HG):
                    s = act.activation(y_int[:, h, :], p_inter[:, h, :], ACT.Copy, scale=stab[:, b % 2, c, T_EXPG, h:h + 1])
                s.then_inc(yint_set, 1)

            def squares(n, c):
                act.wait_ge(y_set, NC * n + c + 1)
                for h in range(HG):
                    s = act.activation(tanh[:, h * D:(h + 1) * D], y[:, h, :], ACT.Square, scale=2.0 / float(np.sqrt(D)),
                                       accum_out=ssum[:, c, h:h + 1])
                s.then_inc(squares_set, 1)

            def save_z(n, c):
                m = NC * n + c
                act.wait_ge(zt_done, m + 1)
                wait_ge(act, z_out[c % 2], 16 * (2 * n + c // 2))
                act.activation(z_t[:, c % 2, :, :], p_zt[:, :, :], ACT.Copy).then_inc(zt_saved, 1)

            def save_v(n):
                act.wait_ge(tok_done, 2 * n + 1)
                wait_ge(act, xc_set, NC * n)
                wait_ge(act, xw_set, 3 * n)
                act.activation(v_tok[:, :, :], p_tok[:, :, :], ACT.Copy).then_inc(tok_saved, 1)

            def save_k(n):
                act.wait_ge(tok_done, 2 * n + 2)
                act.activation(k_tok[:, 0:NC - 1, :], p_tok[:, 0:NC - 1, :], ACT.Copy).then_inc(tok_saved, 1)

            def first():
                save_v(0)
                save_k(0)
                make_decay(0, 0, 0)

            def opening_highs(n, pieces):
                if not ahead(n):
                    for k in pieces:
                        opening_high(act, keep, k)

            def step(g, b, n):
                if group_ahead(g) and b == B - 1:
                    act.wait_ge(unit_done, UNITS * n)
                    split(wq, (1, 2), q_hi, g + 1, 2 * g + 1)
                make_tanh(g, b, n, 0)
                if has_last(n):
                    save_z(n - 1, 3)
                qk_high(n, b, 0)
                make_decay(n, b, 1)
                qk_high(n, b, 1)
                if not ahead(n):
                    act.wait_ge(keep["gn_in"], 16)
                opening_highs(n, (0, 1))
                squares(n, 0)
                for c in (1, 2):
                    qk_high(n, b, c + 1)
                    make_decay(n, b, c + 1)
                    make_tanh(g, b, n, c)
                    scale_inter(n, b, c)
                    if c == 1 and group_ahead(g) and b == B - 2:
                        act.wait_ge(unit_done, unit(n, V_UNIT) + 1)
                        split(wkv, (0,), kv_hi, g + 1, g + 1)
                    opening_highs(n, (2 * c, 2 * c + 1))
                    squares(n, c)
                    save_z(n, c - 1)
                if ahead(n):
                    save_v(n + 1)
                make_tanh(g, b, n, 3)
                if ahead(n):
                    save_k(n + 1)
                scale_inter(n, b, 3)
                if group_ahead(g) and b == B - 1:
                    split(wg, (1,), g_hi, g + 1, 2 * g + 2)
                opening_highs(n, (6, 7))
                squares(n, 3)
                if group_ahead(g) and b == B - 1:
                    split(wg, (2,), g_hi, g + 1, 2 * g + 2)
                save_z(n, 2)
                if ahead(n):
                    make_decay(n + 1, b + 1, 0)

            steps(act, first, step)
            save_z(B * KVH - 1, 3)

        @block.gpsimd
        def _(pool):
            def step_tables(g, b, n):
                pool.tensor_copy(stab[:, b % 2], tab[:, :, :, bass.ds(g * HG + b * H, HG)]).then_inc(stab_set, 1)

            def mask(n, c):
                pool.wait_ge(g_in[c % 2], 16 * (2 * n + c // 2 + 1))
                pool.tensor_tensor(g_row[:, c % 2], g_row[:, c % 2], before[:, :].unsqueeze(1).to_broadcast([P, HG, C]),
                                   ALU.add).then_inc(masked_set, 1)

            def scaled_v(out, b, c, which):
                v = v_tok[:, c, :].unsqueeze(1).to_broadcast([P, HG, D])
                w = stab[:, b % 2, c, which, :].unsqueeze(2).to_broadcast([P, HG, D])
                return pool.tensor_tensor(out[:, c % 2], v, w, ALU.mult)

            def make_xc(n, b, c):
                if c == 0:
                    pool.wait_ge(tok_saved, 2 * n + 1)
                    pool.wait_ge(stab_set, n + 1)
                wait_ge(pool, intra_done, NC * n + c - 1)
                scaled_v(xc, b, c, T_DT).then_inc(xc_set, 1)

            def make_xw(n, b, c):
                if c == 0:
                    pool.wait_ge(tok_saved, 2 * n + 1)
                    pool.wait_ge(stab_set, n + 1)
                wait_ge(pool, cst_done, 3 * n + (c - 1 if c else 0))
                scaled_v(xw, b, c, T_W).then_inc(xw_set, 1)

            def rms(n, c):
                m = NC * n + c
                pool.wait_ge(squares_set, m + 1)
                pool.tensor_tensor(svar[:, c, :], ssum[:, c, :], eps4[:, :], ALU.add).then_inc(svar_set, 1)
                pool.wait_ge(svar_set, m + 1)
                pool.tensor_tensor(srstd[:, c, :], svar[:, c, :], mhalf[:, :], ALU.pow).then_inc(srstd_set, 1)

            def first():
                pool.memset(before[:, :], 0.0).then_inc(mask_set, 1)
                pool.wait_ge(mask_set, 1)
                pool.affine_select(out=before[:, :], in_=before[:, :], compare_op=ALU.is_ge, fill=-1e30,
                                   base=0, pattern=[[1, C]], channel_multiplier=-1).then_inc(mask_set, 1)
                pool.wait_ge(const_set, 2)
                step_tables(0, 0, 0)
                make_xw(0, 0, 0)
                pool.wait_ge(mask_set, 2)
                mask(0, 0)
                make_xc(0, 0, 0)

            def step(g, b, n):
                mask(n, 1)
                make_xc(n, b, 1)
                make_xw(n, b, 1)
                if ahead(n):
                    wait_ge(pool, yint_set, 3 * n)
                    step_tables(g if b < B - 1 else g + 1, (b + 1) % B, n + 1)
                    add_rope(pool, keep, n + 1, b + 1, 0)
                rms(n, 0)
                mask(n, 2)
                make_xc(n, b, 2)
                make_xw(n, b, 2)
                rms(n, 1)
                if ahead(n):
                    add_rope(pool, keep, n + 1, b + 1, 1)
                mask(n, 3)
                make_xc(n, b, 3)
                rms(n, 2)
                if ahead(n):
                    add_rope(pool, keep, n + 1, b + 1, 2)
                    mask(n + 1, 0)
                    make_xc(n + 1, b + 1, 0)
                    make_xw(n + 1, b + 1, 0)
                rms(n, 3)
                if ahead(n):
                    add_rope(pool, keep, n + 1, b + 1, 3)
                    add_rope(pool, keep, n + 1, b + 1, 4)

            steps(pool, first, step)


HP = 8
NP = H // HP
WH = 2
NW = H // WH
WPZ = HP // WH
SLOTS = 4
Z, WO, WS = "z", "wo", "ws"
OPENING = [(Z, 0, 0), (WO, 0), (Z, 1, 0), (WO, 1), (WO, 2), (WO, 3), (WO, 4), (WO, 5),
           (WO, 6), (WO, 7), (Z, 0, 1), (WO, 8), (Z, 1, 1), (WO, 9),
           (WO, 10), (WO, 11), (Z, 0, 2), (WO, 12), (Z, 1, 2), (WO, 13),
           (WO, 14), (WO, 15), (Z, 0, 3), (Z, 1, 3)] + [(WS, kt) for kt in range(KT)]
SPLIT_EARLY = 8
LOADED_EARLY = SPLIT_EARLY + SLOTS
assert len(OPENING) % SLOTS == 0 and WH * (SPLIT_EARLY - 2) <= (B - 1) * KT


def number(i, j):
    return len(OPENING) + NP * (i - 2) + j


def load_z_piece(sp, keep, i, j, slot):
    sp.dma_start(keep["raw"][slot], keep["z_dram"][bass.ds(i, 1), :, j * HP:(j + 1) * HP, :].rearrange(
        "a p h t -> p (a h t)")).then_inc(keep["raw_in"][slot], 16)


def load_opening(sp, io, keep, k):
    if k >= SLOTS:
        sp.wait_ge(keep["lo_set"], k - SLOTS + 1)
    kind, a = OPENING[k][:2]
    if kind == Z:
        load_z_piece(sp, keep, a, OPENING[k][2], k % SLOTS)
    elif kind == WS:
        sp.dma_start(keep["raw"][k % SLOTS][:, 0:HID], io["w_t"][a * P:(a + 1) * P, :]).then_inc(keep["raw_in"][k % SLOTS], 16)
    else:
        sp.dma_start(keep["raw"][k % SLOTS].rearrange("p (h n) -> p h n", h=WH),
                     io["wo_t"][a * WH * P:(a + 1) * WH * P, :].rearrange("(h p) n -> p h n", p=P)).then_inc(
                         keep["raw_in"][k % SLOTS], 16)


def wo_part(keep, e, h, n):
    return keep["shared"][:, h:h + n, e, :] if h < H // 2 else keep["wo_rest"][:, h - H // 2:h - H // 2 + n, e, :]


def split_high(act, keep, slot, raw_slot):
    act.activation(keep["z_hi"][slot], keep["raw"][raw_slot].rearrange("p (h t) -> p h t", h=HP),
                   ACT.Copy).then_inc(keep["hi_set"], 1)


def split_low(dve, keep, slot, raw_slot):
    dve.tensor_tensor(keep["z_lo"][slot], keep["raw"][raw_slot].rearrange("p (h t) -> p h t", h=HP),
                      keep["z_hi"][slot].bitcast(F32), ALU.subtract).then_inc(keep["lo_set"], 1)


def opening_high(act, keep, k):
    act.wait_ge(keep["raw_in"][k % SLOTS], 16 * (k // SLOTS + 1))
    kind, a = OPENING[k][:2]
    if kind == Z:
        wait_ge(act, keep["heads_done"], 2 * OPENING[k][2] + a - 1)
        split_high(act, keep, a, k % SLOTS)
    elif kind == WS:
        act.activation(keep["ws"][:, a, 0, :], keep["raw"][k % SLOTS][:, 0:HID], ACT.Copy).then_inc(keep["hi_set"], 1)
    else:
        act.activation(wo_part(keep, 0, a * WH, WH), keep["raw"][k % SLOTS].rearrange("p (h n) -> p h n", h=WH), ACT.Copy,
                       scale=keep["gn"][:, 0:1]).then_inc(keep["hi_set"], 1)


def opening_low(dve, keep, k):
    dve.wait_ge(keep["hi_set"], k + 1)
    kind, a = OPENING[k][:2]
    if kind == Z:
        split_low(dve, keep, a, k % SLOTS)
    elif kind == WS:
        dve.tensor_tensor(keep["ws"][:, a, 1, :], keep["raw"][k % SLOTS][:, 0:HID], keep["ws"][:, a, 0, :].bitcast(F32),
                          ALU.subtract).then_inc(keep["lo_set"], 1)
    else:
        dve.scalar_tensor_tensor(wo_part(keep, 1, a * WH, WH), keep["raw"][k % SLOTS].rearrange("p (h n) -> p h n", h=WH),
                                 keep["gn"][:, 0:1], wo_part(keep, 0, a * WH, WH).bitcast(F32),
                                 ALU.mult, ALU.subtract).then_inc(keep["lo_set"], 1)


def heads(pe, keep, out, s, j, slot, opening=False, some=range(HP)):
    z_hi, z_lo = keep["z_hi"], keep["z_lo"]
    for h in some:
        hh = j * HP + h
        if opening and h % WH == 0:
            pe.wait_ge(keep["lo_set"], 1 + max(OPENING.index((Z, s, j)), OPENING.index((WO, hh // WH))))
        for t, (a, e) in enumerate(((z_hi, 0), (z_lo, 0), (z_hi, 1))):
            mm = pe.matmul(out, a[slot][:, h, :], wo_part(keep, e, hh, 1).rearrange("p a n -> p (a n)"),
                           start=(hh == 0 and t == 0), stop=(hh == H - 1 and t == 2))
    if some[-1] == HP - 1:
        mm.then_inc(keep["heads_done"], 1)


def output_stage(nc, io, keep):
    ident, raw_in, z_out, hi_set, lo_set, heads_done, z_hi, z_lo = (keep[k] for k in (
        "ident", "raw_in", "z_out", "hi_set", "lo_set", "heads_done", "z_hi", "z_lo"))
    tokens = keep["tokens"]
    SCALE = 1.0 / float(np.sqrt(np.float32(DK)))
    with ExitStack() as ctx:
        def sb(name, shape, dt=F32):
            return ctx.enter_context(nc.sbuf_tensor(name, shape, dt))

        def pb(name, shape=(P, HID)):
            return ctx.enter_context(nc.psum_tensor(name, list(shape), F32))

        def sem(name):
            return ctx.enter_context(nc.semaphore(name))

        keep["wo_rest"] = sb("wo_rest", [P, H // 2, 2, HID], F32R)
        ws = keep["ws"] = sb("ws", [P, KT, 2, HID], F32R)
        xn = sb("xn", [P, HID])
        xt = sb("xt", [P, KT, P])
        xt_part = [sb(f"xt_{n}", [P, KT, P], F32R) for n in ("hi", "lo")]
        stats, mv, var, rstd, mhalf = sb("stats", [P, 6]), sb("mv", [P, 2]), sb("var", [P, 1]), sb("rstd", [P, 1]), sb("mh", [P, 1])
        eps = sb("eps", [P, 1])
        keys = sb("keys", [P, E, DK])
        qk = sb("qk", [P, E, DK])
        sc, ew = sb("sc", [P, E]), sb("ew", [P, E])
        mx, nmx, den, rden = (sb(n, [P, 1]) for n in ("mx", "nmx", "den", "rden"))
        hw, hwn = sb("hw", [P, E, R]), sb("hwn", [P, E * R])
        hwt = sb("hwt", [P, P])
        wqk = sb("wqk", [P, KT, 2 * E * DK])
        wa = sb("wa", [P, KT, E * R])
        bm = sb("bm", [P, HID])
        bias = sb("bias", [P, HID])

        p_out = [keep["p_tok"][:, :, :].rearrange("p h t -> p (h t)"), pb("p_out1")[:, :]]
        p_xt, p_qk, p_h, p_hwt, p_f = pb("p_xt", (P, KT, P)), pb("p_qk"), pb("p_h", (P, E * R)), pb("p_hwt", (P, P)), pb("p_f")

        small_in = sem("small_in")
        x_in = [sem(f"x_in{i}") for i in range(2)]
        out_sent = [sem(f"out_sent{i}") for i in range(2)]
        x1_set, x1b_set, stats_set, mv_set, var_set, rstd_set, xn_set = (sem(s) for s in (
            "x1_set", "x1b_set", "stats_set", "mv_set", "var_set", "rstd_set", "xn_set"))
        xt_done, xt_saved, qk_done, keys_saved, prod_set, sc_set, mx_set, nmx_set, ew_set = (sem(s) for s in (
            "xt_done", "xt_saved", "qk_done", "keys_saved", "prod_set", "sc_set", "mx_set", "nmx_set", "ew_set"))
        rden_set, hw_set, hwn_set, hwt_done, hwt_saved, f_done, res_set, c_set = (sem(s) for s in (
            "rden_set", "hw_set", "hwn_set", "hwt_done", "hwt_saved", "f_done", "res_set", "c_set"))
        xt_hi_set, xt_lo_set = sem("xt_hi_set"), sem("xt_lo_set")
        block = ctx.enter_context(nc.Block())

        def tiles(engine, first, step):
            first()
            step(0, 0, True)
            step(1, 1, True)
            with engine.Fori(1, NT // 2 - 1) as pair:
                step(2 * pair, 0, True)
                step(2 * pair + 1, 1, True)
            step(NT - 2, 0, True)
            step(NT - 1, 1, False)

        def has_before(i):
            return not (isinstance(i, int) and i == 0)

        def has_ahead(i, by):
            return not (isinstance(i, int) and i + by >= NT)

        def ahead(i):
            same = [(i + 1, j) for j in range(1, NP)] if has_before(i) and has_ahead(i, 1) else []
            return same + ([(i + 2, 0)] if has_ahead(i, 2) else [])

        @block.sync
        def _(sp):
            def load_x(i, s):
                sp.dma_start(tokens[:, s, :], io["x"][bass.ds(i * P, P), :]).then_inc(x_in[s], 16)

            def first():
                for k in range(LOADED_EARLY, len(OPENING)):
                    load_opening(sp, io, keep, k)
                load_x(0, 0)
                for s in range(2):
                    sp.wait_ge(z_out[s], 16 * B * KVH * NC // 2)
                sp.dma_start(bias[:, :], io["b"].rearrange("(a n) -> a n", a=1).to_broadcast([P, HID])).then_inc(small_in, 16)
                sp.dma_start(wqk[:, :, :], io["wqk_t"].rearrange("(k p) n -> p k n", p=P)).then_inc(small_in, 16)
                sp.dma_start(wa[:, :, :], io["a_t"].rearrange("(k p) n -> p k n", p=P)).then_inc(small_in, 16)
                sp.dma_start(bm[:, :], io["bm_t"]).then_inc(small_in, 16)

            def step(i, s, has_next):
                load_z(ahead(i)[0:1])
                if has_before(i):
                    store(i - 1, 1 - s)
                load_z(ahead(i)[1:2])
                if has_next:
                    wait_ge(sp, out_sent[1 - s], 8 * (i - s) + 16 * s)
                    load_x(i + 1, 1 - s)
                load_z(ahead(i)[2:])

            def load_z(pieces):
                for i, j in pieces:
                    sp.wait_ge(lo_set, number(i, j) - SLOTS + 1)
                    load_z_piece(sp, keep, i, j, j % SLOTS)

            def store(i, s):
                sp.wait_ge(res_set, i + 1)
                sp.dma_start(io["out"][bass.ds(i * P, P), :], tokens[:, s, :]).then_inc(out_sent[s], 16)

            tiles(sp, first, step)
            store(NT - 1, 1)
            for s in range(2):
                sp.wait_ge(out_sent[s], 16 * NT // 2)

        @block.tensor
        def _(pe):
            def wo_piece(i, s, j):
                pe.wait_ge(lo_set, number(i, j) + 1)
                if j == 0:
                    pe.wait_ge(x1_set, i - 1)
                heads(pe, keep, p_out[s], s, j, j % 2)

            def turn_x(i):
                pe.wait_ge(xn_set, i + 1)
                wait_ge(pe, xt_hi_set, i)
                for kt in range(KT):
                    t = pe.transpose(p_xt[:, kt, :], xn[:, kt * P:(kt + 1) * P], ident[:, :])
                t.then_inc(xt_done, 1)

            def experts(i):
                pe.wait_ge(xt_saved, i + 1)
                wait_ge(pe, prod_set, i)
                for kt in range(KT):
                    mm = pe.matmul(p_qk[:, :], xt[:, kt, :], wqk[:, kt, :], start=(kt == 0), stop=(kt == KT - 1))
                mm.then_inc(qk_done, 1)
                wait_ge(pe, hw_set, i)
                for kt in range(KT):
                    mm = pe.matmul(p_h[:, :], xt[:, kt, :], wa[:, kt, :], start=(kt == 0), stop=(kt == KT - 1))
                mm.then_inc(qk_done, 1)

            def dense(i):
                pe.wait_ge(xt_lo_set, i + 1)
                wait_ge(pe, res_set, i)
                for kt in range(KT):
                    for a, e in ((0, 0), (1, 0), (0, 1)):
                        pe.matmul(p_f[:, :], xt_part[a][:, kt, :], ws[:, kt, e, :], start=(kt == 0 and a == e == 0), stop=False)

            def turn_hw(i):
                pe.wait_ge(hwn_set, i + 1)
                wait_ge(pe, hwt_saved, i)
                pe.transpose(p_hwt[:, :], hwn[:, :], ident[:, :]).then_inc(hwt_done, 1)

            def combine(i):
                pe.wait_ge(hwt_saved, i + 1)
                pe.matmul(p_f[:, :], hwt[:, :], bm[:, :], start=False, stop=True).then_inc(f_done, 1)

            def first():
                for j in range(NP):
                    for s in range(2):
                        if (s, j) != (0, 0):
                            heads(pe, keep, p_out[s], s, j, s, opening=True)
                pe.wait_ge(small_in, 64)
                pe.wait_ge(lo_set, len(OPENING))

            def step(i, s, has_next):
                has_next = has_next and not (isinstance(i, int) and i == 0)
                if has_next:
                    wo_piece(i + 1, 1 - s, 0)
                turn_x(i)
                if has_next:
                    wo_piece(i + 1, 1 - s, 1)
                experts(i)
                dense(i)
                if has_next:
                    wo_piece(i + 1, 1 - s, 2)
                turn_hw(i)
                if has_next:
                    wo_piece(i + 1, 1 - s, 3)
                combine(i)

            tiles(pe, first, step)

        @block.vector
        def _(dve):
            def z_low(i, j):
                dve.wait_ge(hi_set, number(i, j) + 1)
                split_low(dve, keep, j % 2, j % SLOTS)

            def first():
                dve.memset(mhalf[:, :], -0.5).then_inc(c_set, 1)
                dve.memset(eps[:, :], EPS).then_inc(c_set, 1)
                for k in range(SPLIT_EARLY, len(OPENING)):
                    opening_low(dve, keep, k)

            def step(i, s, has_next):
                x1 = tokens[:, s, :]
                dve.wait_ge(heads_done, NP * (i + 1) if has_before(i) else 2 * NP - 1)
                dve.wait_ge(x_in[s], 8 * (i - s) + 16)
                dve.tensor_tensor(x1, p_out[s], x1, ALU.add).then_inc(x1_set, 1)
                dve.wait_ge(x1_set, i + 1)
                dve.bn_stats(stats[:, :], x1).then_inc(stats_set, 1)
                dve.wait_ge(c_set, 2)
                dve.wait_ge(stats_set, i + 1)
                dve.bn_aggr(mv[:, :], stats[:, :]).then_inc(mv_set, 1)
                dve.wait_ge(rstd_set, i + 1)
                wait_ge(dve, xt_done, i)
                dve.tensor_scalar(xn[:, :], x1, mv[:, 0:1], rstd[:, 0:1], ALU.subtract, ALU.mult).then_inc(xn_set, 1)
                for ii, j in ahead(i)[:1]:
                    z_low(ii, j)
                dve.wait_ge(xt_hi_set, i + 1)
                wait_ge(dve, f_done, i)
                dve.tensor_tensor(xt_part[1][:, :, :], xt[:, :, :], xt_part[0][:, :, :].bitcast(F32),
                                  ALU.subtract).then_inc(xt_lo_set, 1)
                for ii, j in ahead(i)[1:2]:
                    z_low(ii, j)
                dve.wait_ge(keys_saved, i + 1)
                dve.tensor_tensor(qk[:, :, :], p_qk[:, 0:E * DK].rearrange("p (e d) -> p e d", e=E), keys[:, :, :],
                                  ALU.mult).then_inc(prod_set, 1)
                dve.wait_ge(prod_set, i + 1)
                dve.tensor_reduce(sc[:, :], qk[:, :, :], AX.X, ALU.add).then_inc(sc_set, 1)
                dve.wait_ge(sc_set, i + 1)
                dve.reduce_max(mx[:, :], sc[:, :], AX.X).then_inc(mx_set, 1)
                dve.wait_ge(mx_set, i + 1)
                dve.tensor_scalar(nmx[:, :], mx[:, :], -SCALE, None, ALU.mult).then_inc(nmx_set, 1)
                dve.wait_ge(ew_set, i + 1)
                dve.reciprocal(rden[:, :], den[:, :]).then_inc(rden_set, 1)
                dve.wait_ge(qk_done, 2 * i + 2)
                dve.tensor_tensor(hw[:, :, :], p_h[:, :].rearrange("p (e r) -> p e r", e=E),
                                  ew[:, :].unsqueeze(2).to_broadcast([P, E, R]), ALU.mult).then_inc(hw_set, 1)
                dve.wait_ge(hw_set, i + 1)
                dve.wait_ge(rden_set, i + 1)
                wait_ge(dve, hwt_done, i)
                dve.tensor_scalar(hwn[:, :], hw[:, :, :].rearrange("p e r -> p (e r)"), rden[:, 0:1], None,
                                  ALU.mult).then_inc(hwn_set, 1)
                for ii, j in ahead(i)[2:]:
                    z_low(ii, j)
                dve.wait_ge(f_done, i + 1)
                dve.wait_ge(x1b_set, i + 1)
                dve.tensor_tensor(x1, p_f[:, :], x1, ALU.add).then_inc(res_set, 1)

            tiles(dve, first, step)

        @block.scalar
        def _(act):
            def z_high(i, j):
                act.wait_ge(raw_in[j % SLOTS], 16 * (len(OPENING) // SLOTS - 1 + i))
                act.wait_ge(heads_done, NP * i + j - 1)
                split_high(act, keep, j % 2, j % SLOTS)

            def first():
                for k in range(SPLIT_EARLY, len(OPENING)):
                    opening_high(act, keep, k)

            def step(i, s, has_next):
                for ii, j in ahead(i)[0:1]:
                    z_high(ii, j)
                act.wait_ge(xt_done, i + 1)
                wait_ge(act, f_done, i)
                act.activation(xt[:, :, :], p_xt[:, :, :], ACT.Copy).then_inc(xt_saved, 1)
                act.activation(xt_part[0][:, :, :], p_xt[:, :, :], ACT.Copy).then_inc(xt_hi_set, 1)
                for ii, j in ahead(i)[1:2]:
                    z_high(ii, j)
                act.wait_ge(qk_done, 2 * i + 1)
                wait_ge(act, prod_set, i)
                act.activation(keys[:, :, :], p_qk[:, E * DK:].rearrange("p (e d) -> p e d", e=E), ACT.Copy).then_inc(keys_saved, 1)
                act.wait_ge(nmx_set, i + 1)
                wait_ge(act, hw_set, i)
                wait_ge(act, rden_set, i)
                act.activation(ew[:, :], sc[:, :], ACT.Exp, scale=SCALE, bias=nmx[:, 0:1], accum_out=den[:, 0:1]).then_inc(ew_set, 1)
                for ii, j in ahead(i)[2:3]:
                    z_high(ii, j)
                act.wait_ge(hwt_done, i + 1)
                act.activation(hwt[:, :], p_hwt[:, :], ACT.Copy).then_inc(hwt_saved, 1)
                for ii, j in ahead(i)[3:]:
                    z_high(ii, j)

            tiles(act, first, step)

        @block.gpsimd
        def _(pool):
            def first():
                pool.wait_ge(c_set, 2)
                pool.wait_ge(small_in, 64)

            def step(i, s, has_next):
                pool.wait_ge(mv_set, i + 1)
                pool.tensor_tensor(var[:, :], mv[:, 1:2], eps[:, :], ALU.add).then_inc(var_set, 1)
                pool.wait_ge(var_set, i + 1)
                pool.tensor_tensor(rstd[:, :], var[:, :], mhalf[:, :], ALU.pow).then_inc(rstd_set, 1)
                pool.wait_ge(xn_set, i + 1)
                pool.tensor_tensor(tokens[:, s, :], tokens[:, s, :], bias[:, :], ALU.add).then_inc(x1b_set, 1)

            tiles(pool, first, step)


def build(nc, io):
    with ExitStack() as ctx:
        def sb(stack, name, shape, dt=F32):
            return stack.enter_context(nc.sbuf_tensor(name, shape, dt))

        keep = {"g_dram": nc.dram_tensor("g_scratch", [NC, B, KVH, HG, C], F32).ap(),
                "z_dram": nc.dram_tensor("z_scratch", [NT, P, H, C], F32).ap(),
                "ident": sb(ctx, "ident", [P, P]),
                "w_raw": [sb(ctx, f"w_raw{i}", [P, 2 * GW]) for i in range(3)],
                "shared": sb(ctx, "shared", [P, H // 2, 2, HID], F32R),
                "gn": sb(ctx, "gn", [P, 1]),
                "p_tok": ctx.enter_context(nc.psum_tensor("p_tok", [P, HG, P], F32))}
        assert B * KT == H // 2 and L == HID
        keep["wq"] = [sb(ctx, f"wq_{part_}", [P, KT, GW], F32R) for part_ in ("hi", "lo")]
        keep["q0"] = sb(ctx, "q0", [P, HG, L])
        keep["z_out"] = [ctx.enter_context(nc.semaphore(f"z_out{i}")) for i in range(2)]
        keep["raw_in"] = [ctx.enter_context(nc.semaphore(f"raw_in{i}")) for i in range(SLOTS)]
        for name in ("gn_in", "hi_set", "lo_set", "heads_done", "rope_terms", "roped", "v_set"):
            keep[name] = ctx.enter_context(nc.semaphore(name))
        keep["raw"] = [r[:, :] for r in keep["w_raw"]] + [keep["q0"][:, 0:2, :].rearrange("p h t -> p (h t)")]
        keep["tokens"] = keep["q0"][:, 2:4, :]
        keep["z_hi"], keep["z_lo"] = (
            [w[:, :, :].rearrange("p k n -> p (k n)")[:, s * HP * P:(s + 1) * HP * P].rearrange("p (h t) -> p h t", h=HP)
             for s in range(2)] for w in keep["wq"])
        with ExitStack() as inner:
            keep["tab"] = sb(inner, "tab", [P, NC, TAB, B * H])
            keep["cos"] = sb(inner, "cos", [P, L])
            keep["sin"] = sb(inner, "sin", [P, L])
            keep["rope_a"] = sb(inner, "rope_a", [P, 2, L])
            keep["rope_b"] = sb(inner, "rope_b", [P, 2, L])
            keep["k"] = sb(inner, "k", [P, 2, L])
            keep["v_t"] = sb(inner, "v_t", [P, L])
            keep["q"] = [keep["q0"]]
            for name, width in (("wkv", 2 * D), ("wg", GW)):
                keep[name] = [sb(inner, f"{name}_{part_}", [P, KT, width], F32R) for part_ in ("hi", "lo")]
            norm_stage(nc, io, keep)
            attention_stage(nc, io, keep)
        output_stage(nc, io, keep)


def rope_tables():
    inv = (1.0 / np.float32(10000.0) ** (np.arange(0, D, 2, dtype=np.float32) / np.float32(D))).astype(np.float32)
    ang = np.arange(L, dtype=np.float32)[:, None] * inv
    cos, sin = np.cos(ang).T, np.sin(ang).T
    return (np.ascontiguousarray(np.concatenate([cos, cos]), np.float32),
            np.ascontiguousarray(np.concatenate([-sin, sin]), np.float32))


def kernel(**inputs):
    import numpy as _np
    import concourse.bacc as _bacc
    from concourse import mybir as _mybir
    from concourse.bass_utils import run_bass_kernel_spmd as _run

    a = {k: _np.asarray(v) for k, v in inputs.items()}
    cos, sin = rope_tables()
    t = _np.ascontiguousarray
    by_group = lambda w, n: t(w.reshape(KVH, n, HID).transpose(0, 2, 1))
    arrays = {
        "x": t(a["L0_attn_hidden_states"].reshape(B * L, HID)),
        "win_t": t(a["L0_attn_Win"].T),
        "dt_bias": t(a["L0_attn_dt_bias"]),
        "A_log_bias": t(a["L0_attn_A_log_bias"]),
        "gnorm_w": t(a["L0_attn_gnorm_w"]),
        "wq_t": by_group(a["L0_attn_Wq"], GW),
        "wg_t": by_group(a["L0_attn_Wg"], GW),
        "wkv_t": t(_np.concatenate([by_group(a["L0_attn_Wk"], D), by_group(a["L0_attn_Wv"], D)], axis=2)),
        "wo_t": t(a["L0_attn_Wo"].T),
        "w_t": t(a["L0_ffn_W"].T),
        "b": t(a["L0_ffn_b"]),
        "wqk_t": t(_np.concatenate([a["L0_ffn_Wq"].T, a["L0_ffn_Wk"].T], axis=1)),
        "a_t": t(a["L0_ffn_A"].reshape(E * R, HID).T),
        "bm_t": t(a["L0_ffn_Bm"].transpose(0, 2, 1).reshape(E * R, HID)),
        "cos_t": cos,
        "sin_t": sin,
    }
    nc = _bacc.Bacc("TRN2", target_bir_lowering=False, num_devices=1)
    io = {k: nc.dram_tensor(f"in_{k}", v.shape, _mybir.dt.from_np(v.dtype), kind="ExternalInput").ap()
          for k, v in arrays.items()}
    io["out"] = nc.dram_tensor("out_dram", (B * L, HID), _mybir.dt.float32, kind="ExternalOutput").ap()
    build(nc, io)
    r = _run(nc, [{f"in_{k}": v for k, v in arrays.items()}], core_ids=[0])
    return r.results[0]["out_dram"].reshape(B, L, HID)
```
